# Optimizing a Trainium2 kernel written in Bass

```python
import numpy as np
import jax
import jax.numpy as jnp

def _softmax(x, axis=-1):
    return jax.nn.softmax(x, axis=axis)

def _gelu(x):
    return jax.nn.gelu(x, approximate=True)

def _silu(x):
    return jax.nn.silu(x)

def _sigmoid(x):
    return jax.nn.sigmoid(x)

def _layernorm(x, axis=-1, eps=1e-05):
    m = jnp.mean(x, axis=axis, keepdims=True)
    v = jnp.var(x, axis=axis, keepdims=True)
    return (x - m) / jnp.sqrt(v + eps)

def _scatter_add(tgt, idx, src, axis=0):
    return tgt.at[idx].add(src)

def _segment_sum(src, seg, n):
    return jax.ops.segment_sum(src, seg, n)
kernel_name = 'mk_flamingo_gated_d4_seqx_r8_e4f72b'

def setup_inputs(seed: int=0):
    np.random.seed(seed)
    _w = jnp.asarray

    def _rec_inputs():
        import jax
        import jax.numpy as jnp
        _rk = jax.random.key(seed)
        x = 7.22e-05 + 1 * jax.random.normal(jax.random.fold_in(_rk, 1), (64, 128, 128), jnp.float32)
        _lenS = 128 - jax.random.randint(jax.random.fold_in(_rk, 7), (64,), 0, max(1, 128 // 4) + 1, jnp.int32)
        _lenS2 = 120 - jax.random.randint(jax.random.fold_in(_rk, 8), (64,), 0, max(1, 120 // 4) + 1, jnp.int32)
        _ctx_768P = jax.random.normal(jax.random.fold_in(_rk, 11), (64, 16, 96), jnp.float32)
        _ctx_768c = jax.random.dirichlet(jax.random.fold_in(_rk, 511), 0.3 * jnp.ones((16,), jnp.float32), (64, 120))
        _ctx_768t = jnp.einsum('bsk,bkd->bsd', _ctx_768c, _ctx_768P)
        _ctx_768t = _ctx_768t * jax.lax.rsqrt(jnp.mean(jnp.square(_ctx_768t)) + 1e-12) * 0.953939
        ctx_768 = -0.000191848 + 0.999787 * (_ctx_768t + 0.3 * jax.random.normal(jax.random.fold_in(_rk, 611), (64, 120, 96), jnp.float32))
        _validS = jnp.arange(128)[None, :] < _lenS[:, None]
        _validS2 = jnp.arange(120)[None, :] < _lenS2[:, None]
        _causal = jnp.tril(jnp.ones((128, 128), dtype=bool))
        mask_BxS_bf1 = jnp.ones((64, 128), dtype=bool)
        mask_BxS2_bf1 = jnp.ones((64, 120), dtype=bool)
        _g = jax.random.normal(jax.random.fold_in(_rk, 9001), (2, 4), jnp.float32)
        _g = jnp.sign(_g) * jnp.maximum(jnp.abs(_g), 1.0) + (_g == 0) * 1.0
        g_xattn = _g[0]
        g_ffn = _g[1]
        return (x, ctx_768, mask_BxS_bf1, mask_BxS2_bf1, g_xattn, g_ffn)
    x, ctx_768, mask_BxS_bf1, mask_BxS2_bf1, g_xattn, g_ffn = _rec_inputs()

    def _L0_xattn_setup():
        import jax, jax.numpy as jnp
        import numpy as np
        NUM_HEADS = 16
        CLAMP = 10000.0
        key = jax.random.key(seed)
        ks = jax.random.split(key, 8)
        B, Nq, Nkv, Cq, Ckv = (4, 256, 256, 128, 96)
        s_q = 1.0 / np.sqrt(Cq)
        s_kv = 1.0 / np.sqrt(Ckv)
        return {'query': jax.random.normal(ks[0], (B, Nq, Cq), jnp.float32), 'key_value': jax.random.normal(ks[1], (B, Nkv, Ckv), jnp.float32), 'Wq': jax.random.normal(ks[2], (Cq, Cq), jnp.float32) * s_q, 'bq': jnp.zeros((Cq,), jnp.float32), 'Wk': jax.random.normal(ks[3], (Ckv, Cq), jnp.float32) * s_kv, 'bk': jnp.zeros((Cq,), jnp.float32), 'Wv': jax.random.normal(ks[4], (Ckv, Cq), jnp.float32) * s_kv, 'bv': jnp.zeros((Cq,), jnp.float32), 'Wo': jax.random.normal(ks[5], (Cq, Cq), jnp.float32) * s_q, 'bo': jnp.zeros((Cq,), jnp.float32)}
    _L0_xattn_all = _L0_xattn_setup()
    _L0_xattn_in = {k: v for k, v in _L0_xattn_all.items() if k in ('Wq', 'bq', 'Wk', 'bk', 'Wv', 'bv', 'Wo', 'bo')}
    del _L0_xattn_all

    def _L0_ffn_setup():
        import jax, jax.numpy as jnp
        import numpy as np
        H = 16
        TOP_K = 2
        LN_EPS = 1e-05
        key = jax.random.key(seed)
        ks = jax.random.split(key, 8)
        B, S, E, NE = (2, 128, 128, 8)
        w = lambda k, shp: jax.random.normal(k, shp, dtype=jnp.float32) * 0.02
        return {'x': jax.random.normal(ks[0], (B, S, E), dtype=jnp.float32), 'rW1': w(ks[1], (E // 2, E)), 'rb1': jnp.zeros((E // 2,), jnp.float32), 'ln_g': jnp.ones((E // 2,), jnp.float32), 'ln_b': jnp.zeros((E // 2,), jnp.float32), 'rW2': w(ks[2], (NE, E // 2)), 'rb2': jnp.zeros((NE,), jnp.float32), 'qW': w(ks[3], (NE, E, E)), 'qb': jnp.zeros((NE, E), jnp.float32), 'kW': w(ks[4], (NE, E, E)), 'kb': jnp.zeros((NE, E), jnp.float32), 'vW': w(ks[5], (NE, E, E)), 'vb': jnp.zeros((NE, E), jnp.float32), 'oW': w(ks[6], (NE, E, E)), 'ob': jnp.zeros((NE, E), jnp.float32)}
    _L0_ffn_all = _L0_ffn_setup()
    _L0_ffn_in = {k: v for k, v in _L0_ffn_all.items() if k in ('rW1', 'rb1', 'ln_g', 'ln_b', 'rW2', 'rb2', 'qW', 'qb', 'kW', 'kb', 'vW', 'vb', 'oW', 'ob')}
    del _L0_ffn_all

    def _L1_xattn_setup():
        import jax, jax.numpy as jnp
        import numpy as np
        B, T, DT, G, DV = (16, 64, 128, 72, 96)
        H, DH = (4, 32)
        INNER = H * DH
        HID = 4 * DT
        N_STATE = 64
        K_TOP = 32

        def layernorm(x, g, b, eps=1e-05):
            m = x.mean(-1, keepdims=True)
            v = x.var(-1, keepdims=True)
            return (x - m) * jax.lax.rsqrt(v + eps) * g + b

        def s4d(x, log_dt, A_re, A_im, C_re, C_im, D_skip):
            Bb, L, D = x.shape
            dt = jnp.exp(log_dt)
            A = A_re + 1j * A_im
            C = C_re + 1j * C_im
            dtA = dt[:, None] * A
            dC = C * (jnp.exp(dtA) - 1.0) / A
            powers = jnp.exp(dtA[:, :, None] * jnp.arange(L))
            K = 2.0 * jnp.einsum('dn,dnl->dl', dC, powers).real
            n = 2 * L
            Kf = jnp.fft.rfft(K, n=n, axis=-1)
            xf = jnp.fft.rfft(x, n=n, axis=1)
            y = jnp.fft.irfft(xf * Kf.T[None], n=n, axis=1)[:, :L]
            return y + x * D_skip
        key = jax.random.key(seed)
        ks = jax.random.split(key, 16)
        s = 0.02
        inp = {'x_text': jax.random.normal(ks[0], (B, T, DT), jnp.float32), 'x_vision': jax.random.normal(ks[1], (B, G, DV), jnp.float32), 'text_mask': jnp.ones((B, T), bool), 'vision_mask': jnp.ones((B, G), bool), 'Wq': jax.random.normal(ks[2], (DT, INNER), jnp.float32) * s, 'Wk': jax.random.normal(ks[3], (DV, INNER), jnp.float32) * s, 'Wv': jax.random.normal(ks[4], (DV, DT), jnp.float32) * s, 'W_film_in': jax.random.normal(ks[5], (DT, 2 * DT), jnp.float32) * s, 'b_film_in': jnp.zeros((2 * DT,), jnp.float32), 'W_film_out': jax.random.normal(ks[6], (DT, 2 * DT), jnp.float32) * s, 'b_film_out': jnp.zeros((2 * DT,), jnp.float32), 'g_norm_in': jnp.ones((DT,), jnp.float32), 'b_norm_in': jnp.zeros((DT,), jnp.float32), 'g_norm_out': jnp.ones((DT,), jnp.float32), 'b_norm_out': jnp.zeros((DT,), jnp.float32), 'g_ffn': jnp.ones((DT,), jnp.float32), 'b_ffn': jnp.zeros((DT,), jnp.float32), 'W1': jax.random.normal(ks[7], (DT, HID), jnp.float32) * s, 'b1': jnp.zeros((HID,), jnp.float32), 'W2': jax.random.normal(ks[8], (HID, DT), jnp.float32) * s, 'b2': jnp.zeros((DT,), jnp.float32), 'log_dt': jnp.log(0.001) + jax.random.uniform(ks[9], (DT,), jnp.float32) * (jnp.log(0.1) - jnp.log(0.001)), 'A_re': -0.5 * jnp.ones((DT, N_STATE), jnp.float32), 'A_im': jnp.tile(jnp.pi * jnp.arange(N_STATE, dtype=jnp.float32), (DT, 1)), 'C_re': jax.random.normal(ks[10], (DT, N_STATE), jnp.float32) * 0.5 ** 0.5, 'C_im': jax.random.normal(ks[11], (DT, N_STATE), jnp.float32) * 0.5 ** 0.5, 'D_skip': jax.random.normal(ks[12], (DT,), jnp.float32), 'mod_gate': jnp.array(0.5, jnp.float32)}
        return inp
    _L1_xattn_all = _L1_xattn_setup()
    _L1_xattn_in = {k: v for k, v in _L1_xattn_all.items() if k in ('Wq', 'Wk', 'Wv', 'W_film_in', 'b_film_in', 'W_film_out', 'b_film_out', 'g_norm_in', 'b_norm_in', 'g_norm_out', 'b_norm_out', 'g_ffn', 'b_ffn', 'W1', 'b1', 'W2', 'b2', 'log_dt', 'A_re', 'A_im', 'C_re', 'C_im', 'D_skip', 'mod_gate')}
    del _L1_xattn_all

    def _L1_ffn_setup():
        import jax, jax.numpy as jnp
        import numpy as np
        BEST_K = 2

        def _expert(xf, w1, w3, w2):
            return jax.nn.silu(xf @ w1) * (xf @ w3) @ w2
        key = jax.random.key(seed)
        ks = jax.random.split(key, 9)
        E, S_sh, D, H = (8, 2, 128, 64)
        B, S = (2, 256)
        w = lambda k, shape: jax.random.normal(k, shape, dtype=jnp.float32) * 0.02
        return {'x': jax.random.normal(ks[0], (B, S, D), dtype=jnp.float32), 'router_w': w(ks[1], (D, E)), 'router_b': jnp.zeros((E,), dtype=jnp.float32), 'routed_w1': w(ks[2], (E, D, H)), 'routed_w3': w(ks[3], (E, D, H)), 'routed_w2': w(ks[4], (E, H, D)), 'shared_w1': w(ks[5], (S_sh, D, H)), 'shared_w3': w(ks[6], (S_sh, D, H)), 'shared_w2': w(ks[7], (S_sh, H, D))}
    _L1_ffn_all = _L1_ffn_setup()
    _L1_ffn_in = {k: v for k, v in _L1_ffn_all.items() if k in ('router_w', 'router_b', 'routed_w1', 'routed_w3', 'routed_w2', 'shared_w1', 'shared_w3', 'shared_w2')}
    del _L1_ffn_all

    def _L2_xattn_setup():
        import jax, jax.numpy as jnp
        import numpy as np
        HEADS = 16
        DIM_HEAD = 64
        key = jax.random.key(seed)
        ks = jax.random.split(key, 7)
        B, Nq, Dq = (4, 256, 128)
        Nk, Dc = (128, 96)
        inner = HEADS * DIM_HEAD
        sq = 1.0 / np.sqrt(Dq)
        sc = 1.0 / np.sqrt(Dc)
        si = 1.0 / np.sqrt(inner)
        return {'x': jax.random.normal(ks[0], (B, Nq, Dq), dtype=jnp.float32), 'context': jax.random.normal(ks[1], (B, Nk, Dc), dtype=jnp.float32), 'Wq': jax.random.normal(ks[2], (Dq, inner), dtype=jnp.float32) * sq, 'Wk': jax.random.normal(ks[3], (Dc, inner), dtype=jnp.float32) * sc, 'Wv': jax.random.normal(ks[4], (Dc, inner), dtype=jnp.float32) * sc, 'Wo': jax.random.normal(ks[5], (inner, Dq), dtype=jnp.float32) * si, 'bo': jax.random.normal(ks[6], (Dq,), dtype=jnp.float32) * 0.01}
    _L2_xattn_all = _L2_xattn_setup()
    _L2_xattn_in = {k: v for k, v in _L2_xattn_all.items() if k in ('Wq', 'Wk', 'Wv', 'Wo', 'bo')}
    del _L2_xattn_all

    def _L2_ffn_setup():
        import jax, jax.numpy as jnp
        import numpy as np
        B, S, D = (2, 256, 128)
        M = 256
        E = 8
        TOP_K = 2
        key = jax.random.key(seed)
        ks = jax.random.split(key, 5)
        std = 0.02
        return {'residual': jax.random.normal(ks[0], (B, S, D), jnp.float32), 'W_router': jax.random.normal(ks[1], (D, E), jnp.float32) * std, 'W_gate': jax.random.normal(ks[2], (E, D, M), jnp.float32) * std, 'b_gate': jnp.zeros((E, M), jnp.float32), 'W_up': jax.random.normal(ks[3], (E, D, M), jnp.float32) * std, 'b_up': jnp.zeros((E, M), jnp.float32), 'W_out': jax.random.normal(ks[4], (E, M, D), jnp.float32) * std, 'b_out': jnp.zeros((E, D), jnp.float32)}
    _L2_ffn_all = _L2_ffn_setup()
    _L2_ffn_in = {k: v for k, v in _L2_ffn_all.items() if k in ('W_router', 'W_gate', 'b_gate', 'W_up', 'b_up', 'W_out', 'b_out')}
    del _L2_ffn_all

    def _L3_xattn_setup():
        import jax, jax.numpy as jnp
        import numpy as np
        NUM_HEADS = 16
        HEAD_DIM = 64
        INNER = NUM_HEADS * HEAD_DIM
        QUERY_DIM = 128
        CONTEXT_DIM = 96
        SCALE = HEAD_DIM ** (-0.5)
        key = jax.random.key(seed)
        ks = jax.random.split(key, 6)
        B, NQ, NKV = (8, 128, 256)
        query = jax.random.normal(ks[0], (B, NQ, QUERY_DIM), dtype=jnp.float32)
        context = jax.random.normal(ks[1], (B, NKV, CONTEXT_DIM), dtype=jnp.float32)
        w_q = jax.random.normal(ks[2], (QUERY_DIM, INNER), dtype=jnp.float32) * QUERY_DIM ** (-0.5)
        w_kv = jax.random.normal(ks[3], (CONTEXT_DIM, 2 * INNER), dtype=jnp.float32) * CONTEXT_DIM ** (-0.5)
        w_out = jax.random.normal(ks[4], (INNER, QUERY_DIM), dtype=jnp.float32) * INNER ** (-0.5)
        b_out = jax.random.normal(ks[5], (QUERY_DIM,), dtype=jnp.float32) * 0.01
        return {'query': query, 'context': context, 'w_q': w_q, 'w_kv': w_kv, 'w_out': w_out, 'b_out': b_out}
    _L3_xattn_all = _L3_xattn_setup()
    _L3_xattn_in = {k: v for k, v in _L3_xattn_all.items() if k in ('w_q', 'w_kv', 'w_out', 'b_out')}
    del _L3_xattn_all

    def _L3_ffn_setup():
        import jax, jax.numpy as jnp
        import numpy as np
        B, S, D, E, F = (4, 256, 128, 8, 512)
        key = jax.random.key(seed)
        k0, k1, k2, k3 = jax.random.split(key, 4)
        x = jax.random.normal(k0, (B, S, D), dtype=jnp.float32)
        wg = jax.random.normal(k1, (D, E), dtype=jnp.float32) * 0.02
        w_gate = jax.random.normal(k2, (E, D, F), dtype=jnp.float32) * 0.02
        w_down = jax.random.normal(k3, (E, F, D), dtype=jnp.float32) * 0.02
        return {'x': x, 'wg': wg, 'w_gate': w_gate, 'w_down': w_down}
    _L3_ffn_all = _L3_ffn_setup()
    _L3_ffn_in = {k: v for k, v in _L3_ffn_all.items() if k in ('wg', 'w_gate', 'w_down')}
    del _L3_ffn_all
    return {'x': x, 'ctx_768': ctx_768, 'mask_BxS_bf1': mask_BxS_bf1, 'mask_BxS2_bf1': mask_BxS2_bf1, 'g_xattn': g_xattn, 'g_ffn': g_ffn, 'L0_xattn_Wq': _L0_xattn_in['Wq'], 'L0_xattn_bq': _L0_xattn_in['bq'], 'L0_xattn_Wk': _L0_xattn_in['Wk'], 'L0_xattn_bk': _L0_xattn_in['bk'], 'L0_xattn_Wv': _L0_xattn_in['Wv'], 'L0_xattn_bv': _L0_xattn_in['bv'], 'L0_xattn_Wo': _L0_xattn_in['Wo'], 'L0_xattn_bo': _L0_xattn_in['bo'], 'L0_ffn_rW1': _L0_ffn_in['rW1'], 'L0_ffn_rb1': _L0_ffn_in['rb1'], 'L0_ffn_ln_g': _L0_ffn_in['ln_g'], 'L0_ffn_ln_b': _L0_ffn_in['ln_b'], 'L0_ffn_rW2': _L0_ffn_in['rW2'], 'L0_ffn_rb2': _L0_ffn_in['rb2'], 'L0_ffn_qW': _L0_ffn_in['qW'], 'L0_ffn_qb': _L0_ffn_in['qb'], 'L0_ffn_kW': _L0_ffn_in['kW'], 'L0_ffn_kb': _L0_ffn_in['kb'], 'L0_ffn_vW': _L0_ffn_in['vW'], 'L0_ffn_vb': _L0_ffn_in['vb'], 'L0_ffn_oW': _L0_ffn_in['oW'], 'L0_ffn_ob': _L0_ffn_in['ob'], 'L1_xattn_Wq': _L1_xattn_in['Wq'], 'L1_xattn_Wk': _L1_xattn_in['Wk'], 'L1_xattn_Wv': _L1_xattn_in['Wv'], 'L1_xattn_W_film_in': _L1_xattn_in['W_film_in'], 'L1_xattn_b_film_in': _L1_xattn_in['b_film_in'], 'L1_xattn_W_film_out': _L1_xattn_in['W_film_out'], 'L1_xattn_b_film_out': _L1_xattn_in['b_film_out'], 'L1_xattn_g_norm_in': _L1_xattn_in['g_norm_in'], 'L1_xattn_b_norm_in': _L1_xattn_in['b_norm_in'], 'L1_xattn_g_norm_out': _L1_xattn_in['g_norm_out'], 'L1_xattn_b_norm_out': _L1_xattn_in['b_norm_out'], 'L1_xattn_g_ffn': _L1_xattn_in['g_ffn'], 'L1_xattn_b_ffn': _L1_xattn_in['b_ffn'], 'L1_xattn_W1': _L1_xattn_in['W1'], 'L1_xattn_b1': _L1_xattn_in['b1'], 'L1_xattn_W2': _L1_xattn_in['W2'], 'L1_xattn_b2': _L1_xattn_in['b2'], 'L1_xattn_log_dt': _L1_xattn_in['log_dt'], 'L1_xattn_A_re': _L1_xattn_in['A_re'], 'L1_xattn_A_im': _L1_xattn_in['A_im'], 'L1_xattn_C_re': _L1_xattn_in['C_re'], 'L1_xattn_C_im': _L1_xattn_in['C_im'], 'L1_xattn_D_skip': _L1_xattn_in['D_skip'], 'L1_xattn_mod_gate': _L1_xattn_in['mod_gate'], 'L1_ffn_router_w': _L1_ffn_in['router_w'], 'L1_ffn_router_b': _L1_ffn_in['router_b'], 'L1_ffn_routed_w1': _L1_ffn_in['routed_w1'], 'L1_ffn_routed_w3': _L1_ffn_in['routed_w3'], 'L1_ffn_routed_w2': _L1_ffn_in['routed_w2'], 'L1_ffn_shared_w1': _L1_ffn_in['shared_w1'], 'L1_ffn_shared_w3': _L1_ffn_in['shared_w3'], 'L1_ffn_shared_w2': _L1_ffn_in['shared_w2'], 'L2_xattn_Wq': _L2_xattn_in['Wq'], 'L2_xattn_Wk': _L2_xattn_in['Wk'], 'L2_xattn_Wv': _L2_xattn_in['Wv'], 'L2_xattn_Wo': _L2_xattn_in['Wo'], 'L2_xattn_bo': _L2_xattn_in['bo'], 'L2_ffn_W_router': _L2_ffn_in['W_router'], 'L2_ffn_W_gate': _L2_ffn_in['W_gate'], 'L2_ffn_b_gate': _L2_ffn_in['b_gate'], 'L2_ffn_W_up': _L2_ffn_in['W_up'], 'L2_ffn_b_up': _L2_ffn_in['b_up'], 'L2_ffn_W_out': _L2_ffn_in['W_out'], 'L2_ffn_b_out': _L2_ffn_in['b_out'], 'L3_xattn_w_q': _L3_xattn_in['w_q'], 'L3_xattn_w_kv': _L3_xattn_in['w_kv'], 'L3_xattn_w_out': _L3_xattn_in['w_out'], 'L3_xattn_b_out': _L3_xattn_in['b_out'], 'L3_ffn_wg': _L3_ffn_in['wg'], 'L3_ffn_w_gate': _L3_ffn_in['w_gate'], 'L3_ffn_w_down': _L3_ffn_in['w_down']}

def reference(x, ctx_768, mask_BxS_bf1, mask_BxS2_bf1, g_xattn, g_ffn, L0_xattn_Wq, L0_xattn_bq, L0_xattn_Wk, L0_xattn_bk, L0_xattn_Wv, L0_xattn_bv, L0_xattn_Wo, L0_xattn_bo, L0_ffn_rW1, L0_ffn_rb1, L0_ffn_ln_g, L0_ffn_ln_b, L0_ffn_rW2, L0_ffn_rb2, L0_ffn_qW, L0_ffn_qb, L0_ffn_kW, L0_ffn_kb, L0_ffn_vW, L0_ffn_vb, L0_ffn_oW, L0_ffn_ob, L1_xattn_Wq, L1_xattn_Wk, L1_xattn_Wv, L1_xattn_W_film_in, L1_xattn_b_film_in, L1_xattn_W_film_out, L1_xattn_b_film_out, L1_xattn_g_norm_in, L1_xattn_b_norm_in, L1_xattn_g_norm_out, L1_xattn_b_norm_out, L1_xattn_g_ffn, L1_xattn_b_ffn, L1_xattn_W1, L1_xattn_b1, L1_xattn_W2, L1_xattn_b2, L1_xattn_log_dt, L1_xattn_A_re, L1_xattn_A_im, L1_xattn_C_re, L1_xattn_C_im, L1_xattn_D_skip, L1_xattn_mod_gate, L1_ffn_router_w, L1_ffn_router_b, L1_ffn_routed_w1, L1_ffn_routed_w3, L1_ffn_routed_w2, L1_ffn_shared_w1, L1_ffn_shared_w3, L1_ffn_shared_w2, L2_xattn_Wq, L2_xattn_Wk, L2_xattn_Wv, L2_xattn_Wo, L2_xattn_bo, L2_ffn_W_router, L2_ffn_W_gate, L2_ffn_b_gate, L2_ffn_W_up, L2_ffn_b_up, L2_ffn_W_out, L2_ffn_b_out, L3_xattn_w_q, L3_xattn_w_kv, L3_xattn_w_out, L3_xattn_b_out, L3_ffn_wg, L3_ffn_w_gate, L3_ffn_w_down):
    import jax
    import jax.numpy as jnp

    def _L0_xattn_ref(query, key_value, Wq, bq, Wk, bk, Wv, bv, Wo, bo):
        import jax, jax.numpy as jnp
        import numpy as np
        NUM_HEADS = 16
        CLAMP = 10000.0
        B, Nq, Cq = query.shape
        Nkv = key_value.shape[1]
        H = NUM_HEADS
        D = Cq // H
        scale = D ** (-0.5)
        q = (query @ Wq + bq).reshape(B, Nq, H, D).transpose(0, 2, 1, 3)
        k = (key_value @ Wk + bk).reshape(B, Nkv, H, D).transpose(0, 2, 1, 3)
        v = (key_value @ Wv + bv).reshape(B, Nkv, H, D).transpose(0, 2, 1, 3)
        attn = jnp.einsum('bhqd,bhkd->bhqk', q, k) * scale
        attn = jnp.clip(attn, -CLAMP, CLAMP)
        attn = jax.nn.softmax(attn, axis=-1)
        attn = jnp.where(jnp.any(jnp.isnan(attn)), jnp.asarray(1.0 / Nkv, attn.dtype), attn)
        x = jnp.einsum('bhqk,bhkd->bqhd', attn, v).reshape(B, Nq, Cq)
        return x @ Wo + bo

    def _L0_ffn_ref(x, rW1, rb1, ln_g, ln_b, rW2, rb2, qW, qb, kW, kb, vW, vb, oW, ob):
        import jax, jax.numpy as jnp
        import numpy as np
        H = 16
        TOP_K = 2
        LN_EPS = 1e-05
        B, S, E = x.shape
        NE = qW.shape[0]
        Dh = E // H
        scale = 1.0 / jnp.sqrt(jnp.asarray(Dh, x.dtype))
        h = x @ rW1.T + rb1
        mu = h.mean(-1, keepdims=True)
        var = ((h - mu) ** 2).mean(-1, keepdims=True)
        h = (h - mu) * jax.lax.rsqrt(var + LN_EPS) * ln_g + ln_b
        h = jax.nn.relu(h)
        logits = h @ rW2.T + rb2
        probs = jax.nn.softmax(logits, axis=-1)
        tp, ti = jax.lax.top_k(probs, TOP_K)
        tp = tp / tp.sum(-1, keepdims=True)
        expert_mask = (jax.nn.one_hot(ti, NE, dtype=probs.dtype) * tp[..., None]).sum(-2)
        gates = jnp.moveaxis(expert_mask, -1, 0)

        def expert_step(acc, params):
            qw, qb_, kw, kb_, vw, vb_, ow, ob_, g = params
            q = (x @ qw.T + qb_).reshape(B, S, H, Dh).transpose(0, 2, 1, 3)
            k = (x @ kw.T + kb_).reshape(B, S, H, Dh).transpose(0, 2, 1, 3)
            v = (x @ vw.T + vb_).reshape(B, S, H, Dh).transpose(0, 2, 1, 3)
            scores = jnp.einsum('bhqd,bhkd->bhqk', q, k) * scale
            p = jax.nn.softmax(scores, axis=-1)
            o = jnp.einsum('bhqk,bhkd->bhqd', p, v)
            o = o.transpose(0, 2, 1, 3).reshape(B, S, E) @ ow.T + ob_
            return (acc + o * g[..., None], None)
        out, _ = jax.lax.scan(expert_step, jnp.zeros_like(x), (qW, qb, kW, kb, vW, vb, oW, ob, gates))
        return out

    def _L1_xattn_ref(x_text, x_vision, text_mask, vision_mask, Wq, Wk, Wv, W_film_in, b_film_in, W_film_out, b_film_out, g_norm_in, b_norm_in, g_norm_out, b_norm_out, g_ffn, b_ffn, W1, b1, W2, b2, log_dt, A_re, A_im, C_re, C_im, D_skip, mod_gate):
        import jax, jax.numpy as jnp
        import numpy as np
        B, T, DT, G, DV = (16, 64, 128, 72, 96)
        H, DH = (4, 32)
        INNER = H * DH
        HID = 4 * DT
        N_STATE = 64
        K_TOP = 32

        def layernorm(x, g, b, eps=1e-05):
            m = x.mean(-1, keepdims=True)
            v = x.var(-1, keepdims=True)
            return (x - m) * jax.lax.rsqrt(v + eps) * g + b

        def s4d(x, log_dt, A_re, A_im, C_re, C_im, D_skip):
            Bb, L, D = x.shape
            dt = jnp.exp(log_dt)
            A = A_re + 1j * A_im
            C = C_re + 1j * C_im
            dtA = dt[:, None] * A
            dC = C * (jnp.exp(dtA) - 1.0) / A
            powers = jnp.exp(dtA[:, :, None] * jnp.arange(L))
            K = 2.0 * jnp.einsum('dn,dnl->dl', dC, powers).real
            n = 2 * L
            Kf = jnp.fft.rfft(K, n=n, axis=-1)
            xf = jnp.fft.rfft(x, n=n, axis=1)
            y = jnp.fft.irfft(xf * Kf.T[None], n=n, axis=1)[:, :L]
            return y + x * D_skip
        Bb, Tt, D = x_text.shape
        Gg = x_vision.shape[1]
        Q = (x_text @ Wq).reshape(Bb, Tt, H, DH)
        K = (x_vision @ Wk).reshape(Bb, Gg, H, DH)
        scores = jnp.einsum('bthd,bghd->bhtg', Q, K) / np.sqrt(DH).astype(np.float32)
        scores = jnp.where(vision_mask[:, None, None, :], scores, -jnp.inf)
        topv, topi = jax.lax.top_k(scores, K_TOP)
        probs = jax.nn.softmax(topv, axis=-1)
        bi = jnp.arange(Bb)[:, None, None, None]
        hi = jnp.arange(H)[None, :, None, None]
        ti = jnp.arange(Tt)[None, None, :, None]
        attn = jnp.zeros_like(scores).at[bi, hi, ti, topi].set(probs)
        attn_mean = attn.mean(axis=1)
        V = x_vision @ Wv
        c_t = jnp.einsum('btg,bgd->btd', attn_mean, V)
        c_t = c_t * text_mask[..., None]
        x = layernorm(x_text, g_norm_in, b_norm_in)
        scale_in, shift_in = jnp.split(c_t @ W_film_in + b_film_in, 2, axis=-1)
        x = x * (1.0 + mod_gate * scale_in) + mod_gate * shift_in
        y = s4d(x, log_dt, A_re, A_im, C_re, C_im, D_skip)
        scale_out, shift_out = jnp.split(c_t @ W_film_out + b_film_out, 2, axis=-1)
        y = y * (1.0 + mod_gate * scale_out) + mod_gate * shift_out
        xt = x_text + y
        h = layernorm(xt, g_ffn, b_ffn)
        h = jax.nn.gelu(h @ W1 + b1, approximate=False) @ W2 + b2
        xt = xt + h
        return layernorm(xt, g_norm_out, b_norm_out)

    def _L1_ffn_ref(x, router_w, router_b, routed_w1, routed_w3, routed_w2, shared_w1, shared_w3, shared_w2):
        import jax, jax.numpy as jnp
        import numpy as np
        BEST_K = 2

        def _expert(xf, w1, w3, w2):
            return jax.nn.silu(xf @ w1) * (xf @ w3) @ w2
        B, S, D = x.shape
        T = B * S
        xf = x.reshape(T, D)
        logits = xf @ router_w + router_b
        topk_vals, topk_idx = jax.lax.top_k(logits, BEST_K)
        sparse = jnp.full_like(logits, -jnp.inf)
        sparse = sparse.at[jnp.arange(T)[:, None], topk_idx].set(topk_vals)
        gates = jax.nn.softmax(sparse, axis=-1)
        routed = jax.vmap(_expert, in_axes=(None, 0, 0, 0))(xf, routed_w1, routed_w3, routed_w2)
        routed_out = jnp.einsum('etd,te->td', routed, gates)
        shared_out = jax.vmap(_expert, in_axes=(None, 0, 0, 0))(xf, shared_w1, shared_w3, shared_w2).sum(axis=0)
        return (routed_out + shared_out).reshape(B, S, D)

    def _L2_xattn_ref(x, context, Wq, Wk, Wv, Wo, bo):
        import jax, jax.numpy as jnp
        import numpy as np
        HEADS = 16
        DIM_HEAD = 64
        B, Nq, _ = x.shape
        Nk = context.shape[1]
        h, dh = (HEADS, DIM_HEAD)
        q = (x @ Wq).reshape(B, Nq, h, dh)
        k = (context @ Wk).reshape(B, Nk, h, dh)
        v = (context @ Wv).reshape(B, Nk, h, dh)
        scale = 1.0 / jnp.sqrt(jnp.asarray(dh, dtype=x.dtype))
        scores = jnp.einsum('bqhd,bkhd->bhqk', q, k) * scale
        attn = jax.nn.softmax(scores, axis=-1)
        out = jnp.einsum('bhqk,bkhd->bqhd', attn, v).reshape(B, Nq, h * dh)
        return out @ Wo + bo

    def _L2_ffn_ref(residual, W_router, W_gate, b_gate, W_up, b_up, W_out, b_out):
        import jax, jax.numpy as jnp
        import numpy as np
        B, S, D = (2, 256, 128)
        M = 256
        E = 8
        TOP_K = 2
        router_logits = jnp.einsum('bsd,de->bse', residual, W_router)
        router_probs = jax.nn.softmax(router_logits, axis=-1)
        top_k_probs, top_k_idx = jax.lax.top_k(router_probs, TOP_K)
        top_k_probs = top_k_probs / (jnp.sum(top_k_probs, -1, keepdims=True) + 1e-08)
        one_hot = jax.nn.one_hot(top_k_idx, E, dtype=residual.dtype)
        expert_weights = jnp.einsum('bsk,bske->bse', top_k_probs, one_hot)
        gate = jax.nn.silu(jnp.einsum('bsd,edm->ebsm', residual, W_gate) + b_gate[:, None, None, :])
        up = jnp.einsum('bsd,edm->ebsm', residual, W_up) + b_up[:, None, None, :]
        hidden = gate * up
        expert_out = jnp.einsum('ebsm,emd->ebsd', hidden, W_out) + b_out[:, None, None, :]
        output = jnp.einsum('bse,ebsd->bsd', expert_weights, expert_out)
        return output

    def _L3_xattn_ref(query, context, w_q, w_kv, w_out, b_out):
        import jax, jax.numpy as jnp
        import numpy as np
        NUM_HEADS = 16
        HEAD_DIM = 64
        INNER = NUM_HEADS * HEAD_DIM
        QUERY_DIM = 128
        CONTEXT_DIM = 96
        SCALE = HEAD_DIM ** (-0.5)
        B, NQ, _ = query.shape
        NKV = context.shape[1]
        q = query @ w_q
        kv = context @ w_kv
        k, v = jnp.split(kv, 2, axis=-1)
        q = q.reshape(B, NQ, NUM_HEADS, HEAD_DIM).transpose(0, 2, 1, 3)
        k = k.reshape(B, NKV, NUM_HEADS, HEAD_DIM).transpose(0, 2, 1, 3)
        v = v.reshape(B, NKV, NUM_HEADS, HEAD_DIM).transpose(0, 2, 1, 3)
        scores = jnp.einsum('bhqd,bhkd->bhqk', q, k) * SCALE
        attn = jax.nn.softmax(scores, axis=-1)
        out = jnp.einsum('bhqk,bhkd->bhqd', attn, v)
        out = out.transpose(0, 2, 1, 3).reshape(B, NQ, INNER)
        return out @ w_out + b_out

    def _L3_ffn_ref(x, wg, w_gate, w_down):
        import jax, jax.numpy as jnp
        import numpy as np
        B, S, D, E, F = (4, 256, 128, 8, 512)
        Bb, Ss, Dd = x.shape
        Ee = wg.shape[1]
        T = Bb * Ss
        C = 2 * T // Ee
        tokens = x.reshape(T, Dd)
        logits = tokens.astype(jnp.float32) @ wg.astype(jnp.float32)
        gates = jax.nn.softmax(logits, axis=-1)
        idx1 = jnp.argmax(gates, axis=-1)
        mask1 = jax.nn.one_hot(idx1, Ee, dtype=jnp.int32)
        logits_no1 = jnp.where(mask1 > 0, -jnp.inf, logits)
        idx2 = jnp.argmax(logits_no1, axis=-1)
        mask2 = jax.nn.one_hot(idx2, Ee, dtype=jnp.int32)
        g1 = jnp.take_along_axis(gates, idx1[:, None], axis=-1)[:, 0]
        g2 = jnp.take_along_axis(gates, idx2[:, None], axis=-1)[:, 0]
        denom = jnp.clip(g1 + g2, 1e-09, None)
        g1, g2 = (g1 / denom, g2 / denom)
        loc1 = jnp.cumsum(mask1, axis=0) - mask1
        loc2 = jnp.cumsum(mask2, axis=0) - mask2 + jnp.sum(mask1, axis=0, keepdims=True)
        loc1_s = jnp.sum(loc1 * mask1, axis=-1)
        loc2_s = jnp.sum(loc2 * mask2, axis=-1)
        keep1 = (loc1_s < C).astype(x.dtype)
        keep2 = (loc2_s < C).astype(x.dtype)
        f1 = idx1 * C + jnp.minimum(loc1_s, C - 1)
        f2 = idx2 * C + jnp.minimum(loc2_s, C - 1)
        disp = jnp.zeros((Ee * C, Dd), dtype=x.dtype)
        disp = disp.at[f1].add(tokens * keep1[:, None])
        disp = disp.at[f2].add(tokens * keep2[:, None])
        disp = disp.reshape(Ee, C, Dd)
        h = jax.nn.gelu(jnp.einsum('ecd,edf->ecf', disp, w_gate), approximate=False)
        eo = jnp.einsum('ecf,efd->ecd', h, w_down).reshape(Ee * C, Dd)
        out = (g1 * keep1)[:, None].astype(x.dtype) * eo[f1] + (g2 * keep2)[:, None].astype(x.dtype) * eo[f2]
        return out.reshape(Bb, Ss, Dd)
    x = x + jnp.tanh(g_xattn[0]) * _L0_xattn_ref(_layernorm(x, axis=-1), ctx_768, L0_xattn_Wq, L0_xattn_bq, L0_xattn_Wk, L0_xattn_bk, L0_xattn_Wv, L0_xattn_bv, L0_xattn_Wo, L0_xattn_bo)
    x = x + jnp.tanh(g_ffn[0]) * _L0_ffn_ref(_layernorm(x, axis=-1), L0_ffn_rW1, L0_ffn_rb1, L0_ffn_ln_g, L0_ffn_ln_b, L0_ffn_rW2, L0_ffn_rb2, L0_ffn_qW, L0_ffn_qb, L0_ffn_kW, L0_ffn_kb, L0_ffn_vW, L0_ffn_vb, L0_ffn_oW, L0_ffn_ob)
    x = x + jnp.tanh(g_xattn[1]) * _L1_xattn_ref(_layernorm(x, axis=-1), ctx_768, mask_BxS_bf1, mask_BxS2_bf1, L1_xattn_Wq, L1_xattn_Wk, L1_xattn_Wv, L1_xattn_W_film_in, L1_xattn_b_film_in, L1_xattn_W_film_out, L1_xattn_b_film_out, L1_xattn_g_norm_in, L1_xattn_b_norm_in, L1_xattn_g_norm_out, L1_xattn_b_norm_out, L1_xattn_g_ffn, L1_xattn_b_ffn, L1_xattn_W1, L1_xattn_b1, L1_xattn_W2, L1_xattn_b2, L1_xattn_log_dt, L1_xattn_A_re, L1_xattn_A_im, L1_xattn_C_re, L1_xattn_C_im, L1_xattn_D_skip, L1_xattn_mod_gate)
    x = x + jnp.tanh(g_ffn[1]) * _L1_ffn_ref(_layernorm(x, axis=-1), L1_ffn_router_w, L1_ffn_router_b, L1_ffn_routed_w1, L1_ffn_routed_w3, L1_ffn_routed_w2, L1_ffn_shared_w1, L1_ffn_shared_w3, L1_ffn_shared_w2)
    x = x + jnp.tanh(g_xattn[2]) * _L2_xattn_ref(_layernorm(x, axis=-1), ctx_768, L2_xattn_Wq, L2_xattn_Wk, L2_xattn_Wv, L2_xattn_Wo, L2_xattn_bo)
    x = x + jnp.tanh(g_ffn[2]) * _L2_ffn_ref(_layernorm(x, axis=-1), L2_ffn_W_router, L2_ffn_W_gate, L2_ffn_b_gate, L2_ffn_W_up, L2_ffn_b_up, L2_ffn_W_out, L2_ffn_b_out)
    x = x + jnp.tanh(g_xattn[3]) * _L3_xattn_ref(_layernorm(x, axis=-1), ctx_768, L3_xattn_w_q, L3_xattn_w_kv, L3_xattn_w_out, L3_xattn_b_out)
    x = x + jnp.tanh(g_ffn[3]) * _L3_ffn_ref(_layernorm(x, axis=-1), L3_ffn_wg, L3_ffn_w_gate, L3_ffn_w_down)
    return x

_drawn_inputs = setup_inputs


def setup_inputs(seed=0):
    import zlib

    import numpy as np

    out = dict(_drawn_inputs(seed))
    spreads = {'L0_xattn_bq': (0.0, 0.373),
     'L0_xattn_bk': (0.0, 2.0),
     'L0_xattn_bv': (0.0, 0.1),
     'L0_xattn_bo': (0.0, 0.1),
     'L0_ffn_rb1': (0.0, 0.27),
     'L0_ffn_ln_g': (1.0, 0.6),
     'L0_ffn_ln_b': (0.0, 0.454),
     'L0_ffn_rb2': (0.0, 0.1),
     'L0_ffn_qb': (0.0, 0.8),
     'L0_ffn_kb': (0.0, 2.0),
     'L0_ffn_vb': (0.0, 0.566),
     'L0_ffn_ob': (0.0, 0.1),
     'L1_xattn_b_film_in': (0.0, 0.1),
     'L1_xattn_b_film_out': (0.0, 0.1),
     'L1_xattn_g_norm_in': (1.0, 0.2),
     'L1_xattn_b_norm_in': (0.0, 0.1),
     'L1_xattn_g_norm_out': (1.0, 0.2),
     'L1_xattn_b_norm_out': (0.0, 0.1),
     'L1_xattn_g_ffn': (1.0, 0.6),
     'L1_xattn_b_ffn': (0.0, 0.8),
     'L1_xattn_b1': (0.0, 0.546),
     'L1_xattn_b2': (0.0, 0.1),
     'L1_xattn_A_re': (-0.5, 0.2),
     'L1_ffn_router_b': (0.0, 0.8),
     'L2_ffn_b_gate': (0.0, 0.8),
     'L2_ffn_b_up': (0.0, 0.8),
     'L2_ffn_b_out': (0.0, 0.737)}
    factors = {'g_ffn': 8.0,
     'L0_ffn_qW': 8.0,
     'L0_ffn_kW': 8.0,
     'L0_ffn_vW': 5.317,
     'L0_ffn_oW': 3.323,
     'L1_xattn_Wq': 8.0,
     'L1_xattn_Wk': 8.0,
     'L1_xattn_Wv': 3.212,
     'L1_xattn_W_film_in': 3.893,
     'L1_xattn_W_film_out': 4.966,
     'L1_ffn_router_w': 8.0,
     'L1_ffn_routed_w1': 8.0,
     'L1_ffn_routed_w3': 8.0,
     'L1_ffn_routed_w2': 8.0,
     'L1_ffn_shared_w1': 8.0,
     'L1_ffn_shared_w3': 8.0,
     'L1_ffn_shared_w2': 8.0,
     'L2_xattn_bo': 5.944,
     'L2_ffn_W_gate': 8.0,
     'L2_ffn_W_up': 8.0,
     'L2_ffn_W_out': 8.0,
     'L3_xattn_b_out': 41.574,
     'L3_ffn_wg': 8.0,
     'L3_ffn_w_gate': 8.0,
     'L3_ffn_w_down': 8.0}
    for name, (base, spread) in spreads.items():
        noise = np.random.default_rng([zlib.crc32(name.encode()), seed]).standard_normal(out[name].shape)
        drawn = base * np.exp(spread * noise) if base else spread * noise
        out[name] = jnp.asarray(drawn.astype(out[name].dtype))
    for name, factor in factors.items():
        out[name] = (out[name] * factor).astype(out[name].dtype)
    return out
```

```python
from contextlib import ExitStack

import concourse.bass as bass
from concourse import mybir

ALU = mybir.AluOpType
ACT = mybir.ActivationFunctionType
F32 = mybir.dt.float32
I32 = mybir.dt.int32
U8 = mybir.dt.uint8
X = mybir.AxisListType.X
ds = bass.ds

P = 128
B = 64
NK = 120
CK = 96
TG = 4
G = B // TG
EPS = 1e-5
NEG = -3e38
TAKEN = -3.3e38
MAGIC = 12582912.0


SIGNALS = """
    dma_landed act_step dve_step centred squared squares_summed
    rooted staged turned copied stored routed
    routes_taken x_ready scores_made max_found exp_done probs_turned
    outputs_made sums_inverted outputs_scaled outputs_turned y_made y_added
    gates_copied scores_clipped ones_column_set h1_made h3_made h1_activated
    hidden_in_sbuf chosen shifted counted dma_stored angles_ready
    sines_done kernel_ready setup_step scores_masked probs_averaged c_made
    c_in_sbuf film_made film_read outs_taken_act outs_taken_dve pool_step
    probsT_in_sbuf outputsT_in_sbuf q_made k_made v_made q_in_sbuf k_in_sbuf v_in_sbuf taps_landed_0 taps_landed_1
""".split()
FROM_DMA = ("dma_landed", "dma_stored", "taps_landed_0", "taps_landed_1")


class Signal:

    def __init__(self, sem, step=1):
        self.sem, self.step, self.base, self.per = sem, step, 1, 0

    def stage(self, per, rounds=1):
        self.base += self.per
        self.each, self.per = per, per * rounds
        return self

    def upto(self, n, r=0):
        return (self.base + n) * self.step + r * (self.each * self.step)


class Chain:

    def __init__(self, eng, steps):
        self.eng, self.steps, self.n = eng, steps, 0

    def __call__(self, instruction, r=0):
        self.n += 1
        instruction.then_inc(self.steps.sem, 1)
        self.eng.wait_ge(self.steps.sem, self.steps.upto(self.n, r))

    def end_round(self):
        assert self.n == self.steps.each, (self.n, self.steps.each)
        self.n = 0


class Kernel:
    def __init__(self, nc, dram, ctx):
        self.nc, self.d, self.ctx = nc, dram, ctx
        self.events = {n: Signal(ctx.enter_context(nc.semaphore(n)), 16 if n in FROM_DMA else 1) for n in SIGNALS}
        self.names = {}
        sb = self.sb
        self.x_all = sb("x_all", [P, B, P])
        self.nx_all = sb("nx_all", [P, B, P])
        self.nxT_all = sb("nxT_all", [P, B * P])
        self.ident = sb("ident", [P, P])
        self.ones = sb("ones", [P, P])
        self.cols = sb("cols", [P, 16])
        self.rank = sb("rank", [P, 8])
        self.tg = sb("tg", [P, 8])
        self.ps = ctx.enter_context(nc.psum_tensor("ps", [P, 8, 512], F32))

    def sb(self, name, shape, dt=F32, ctx=None):
        self.names[name] = self.names.get(name, 0) + 1
        name = f"{name}_{self.names[name]}" if self.names[name] > 1 else name
        return (ctx or self.ctx).enter_context(self.nc.sbuf_tensor(name, shape, dt))

    def sig(self, name, per, rounds=1, step=1):
        return self.events[name].stage(per, rounds)


def bc(ap, shape):
    return ap.to_broadcast(shape)


def rounds(eng, outer=1):
    if outer == 1:
        with eng.Fori(0, G // 2) as i:
            for u in range(2):
                yield 0, 2 * i + u, u, 2 * i + u
    else:
        with eng.Fori(0, outer) as e:
            with eng.Fori(0, G // 2) as i:
                for u in range(2):
                    yield e, e * G + 2 * i + u, u, 2 * i + u


def gate_arrays(k, ctx):
    k.logits = k.sb("logits", [P, B, 8], ctx=ctx)
    k.gates = k.sb("gates", [P, 10, B], ctx=ctx)


def prime_signals(k):
    with k.nc.Block() as block:
        @block.sync
        def _(sp):
            for s in k.events.values():
                sp.sem_inc(s.sem, s.step)


def load_inputs(k):
    nc, d = k.nc, k.d
    n = 8
    landed = k.sig("dma_landed", n)
    step = k.sig("act_step", 1)
    made = k.sig("pool_step", 1)
    with nc.Block() as block:
        @block.sync
        def _(sp):
            for q in range(4):
                s = slice(16 * q, 16 * q + 16)
                sp.dma_start(k.x_all[:, s, :], d["x"][s].rearrange("b s c -> s b c")).then_inc(landed.sem, 16)
            sp.dma_start(k.ident[:, :], d["ident"]).then_inc(landed.sem, 16)
            sp.dma_start(k.ones[:, :], d["ones"]).then_inc(landed.sem, 16)
            sp.dma_start(k.cols[:, :], d["cols"]).then_inc(landed.sem, 16)
            sp.dma_start(k.tg[:, :], d["g_rows"].partition_broadcast(P)).then_inc(landed.sem, 16)

        @block.gpsimd
        def _(pool):
            pool.iota(k.rank_i[:, :], [[-1, 8]], base=8, channel_multiplier=0).then_inc(made.sem, 1)
            pool.wait_ge(made.sem, made.upto(1))
            pool.tensor_copy(k.rank[:, :], k.rank_i[:, :])

        @block.scalar
        def _(act):
            act.wait_ge(landed.sem, landed.upto(n))
            act.activation(k.tg[:, :], k.tg[:, :], ACT.Tanh).then_inc(step.sem, 1)
            act.wait_ge(step.sem, step.upto(1))


def layer_norm(k, src, dst, n):
    nc = k.nc
    Q = 4
    BQ = B // Q
    with ExitStack() as ctx:
        st = [k.sb(f"ln_{i}", [P, B], ctx=ctx) for i in range(3)]
        sq = k.sb("ln_sq", [P, 2, BQ, n], ctx=ctx)
        total, mean, rstd = st
        chain = k.sig("dve_step", 4 + Q)
        centred = k.sig("centred", Q)
        squared = k.sig("squared", Q)
        summed = k.sig("squares_summed", Q)
        rooted = k.sig("rooted", 1)
        with nc.Block() as block:
            @block.vector
            def _(dve):
                link = Chain(dve, chain)
                link(dve.tensor_reduce(total[:, :], src[:, :, :n], X, ALU.add))
                link(dve.tensor_scalar(mean[:, :], total[:, :], 1.0 / n, None, ALU.mult))
                for q in range(Q):
                    s = slice(BQ * q, BQ * (q + 1))
                    dve.tensor_tensor(dst[:, s, :n], src[:, s, :n], bc(mean[:, s].unsqueeze(2), [P, BQ, n]),
                                      ALU.subtract).then_inc(centred.sem, 1)
                for q in range(Q):
                    dve.wait_ge(squared.sem, squared.upto(q + 1))
                    dve.tensor_reduce(total[:, BQ * q:BQ * (q + 1)], sq[:, q % 2], X, ALU.add).then_inc(summed.sem, 1)
                dve.wait_ge(rooted.sem, rooted.upto(1))
                link(dve.reciprocal(rstd[:, :], mean[:, :]))
                for q in range(Q):
                    s = slice(BQ * q, BQ * (q + 1))
                    link(dve.tensor_tensor(dst[:, s, :n], dst[:, s, :n], bc(rstd[:, s].unsqueeze(2), [P, BQ, n]),
                                           ALU.mult))
                link(dve.tensor_copy(total[:, 0:1], rstd[:, 0:1]))

            @block.scalar
            def _(act):
                for q in range(Q):
                    act.wait_ge(centred.sem, centred.upto(q + 1))
                    if q >= 2:
                        act.wait_ge(summed.sem, summed.upto(q - 1))
                    act.activation(sq[:, q % 2], dst[:, BQ * q:BQ * (q + 1), :n], ACT.Square).then_inc(squared.sem, 1)
                act.wait_ge(summed.sem, summed.upto(Q))
                act.activation(mean[:, :], total[:, :], ACT.Sqrt, bias=k.cols[:, 0:1],
                               scale=1.0 / n).then_inc(rooted.sem, 1)


def transpose_rows(k, router=None):
    nc = k.nc
    with ExitStack() as ctx:
        rows = k.sb("tr_rows", [P, 2, TG, P], ctx=ctx)
        cols = k.sb("tr_cols", [P, 2, TG * P], ctx=ctx)
        staged = k.sig("staged", 1, G)
        turned = k.sig("turned", 1, G)
        copied = k.sig("copied", 1, G)
        stored = k.sig("stored", 1, G)
        if router:
            routed = k.sig("routed", 1, G)
            taken = k.sig("routes_taken", 1, G)
            loaded = k.sig("dma_landed", 2)
            w_dram, b_dram, W, target = router
            w = k.sb("tr_w", [P, W], ctx=ctx)
            b = k.sb("tr_b", [P, W], ctx=ctx)
        with nc.Block() as block:
            if router:
                @block.sync
                def _(sp):
                    sp.dma_start(w[:, :], w_dram).then_inc(loaded.sem, 16)
                    sp.dma_start(b[:, :], b_dram.partition_broadcast(P)).then_inc(loaded.sem, 16)

            @block.gpsimd
            def _(pool):
                for _, r, u, g in rounds(pool):
                    if u == 0:
                        pool.wait_ge(turned.sem, turned.upto(0, r))
                    pool.tensor_copy(rows[:, u], k.nx_all[:, ds(g * TG, TG), :]).then_inc(staged.sem, 1)

            @block.tensor
            def _(pe):
                if router:
                    pe.wait_ge(loaded.sem, loaded.upto(2))
                for _, r, u, g in rounds(pe):
                    pe.wait_ge(staged.sem, staged.upto(1, r))
                    if u == 0:
                        pe.wait_ge(copied.sem, copied.upto(0, r))
                    for t in range(TG):
                        mm = pe.transpose(k.ps[:, u, t * P:(t + 1) * P], rows[:, u, t, :], k.ident[:, :])
                    mm.then_inc(turned.sem, 1)
                    if router:
                        pe.wait_ge(copied.sem, copied.upto(1, r))
                        if u == 0:
                            pe.wait_ge(taken.sem, taken.upto(0, r))
                        for t in range(TG):
                            mm = pe.matmul(k.ps[:, 2 + u, t * W:(t + 1) * W], cols[:, u, t * P:(t + 1) * P], w[:, :],
                                           start=True, stop=True)
                        mm.then_inc(routed.sem, 1)

            @block.scalar
            def _(act):
                for _, r, u, g in rounds(act):
                    act.wait_ge(turned.sem, turned.upto(1, r))
                    if u == 0:
                        act.wait_ge(stored.sem, stored.upto(0, r))
                        if router:
                            act.wait_ge(routed.sem, routed.upto(0, r))
                    act.copy(cols[:, u], k.ps[:, u, :]).then_inc(copied.sem, 1)

            @block.vector
            def _(dve):
                if router:
                    dve.wait_ge(loaded.sem, loaded.upto(2))
                for _, r, u, g in rounds(dve):
                    dve.wait_ge(copied.sem, copied.upto(1, r))
                    dve.tensor_copy(k.nxT_all[:, ds(g * (TG * P), TG * P)], cols[:, u]).then_inc(stored.sem, 1)
                    if router:
                        dve.wait_ge(routed.sem, routed.upto(1, r))
                        dve.tensor_tensor(target[:, ds(g * TG, TG), :],
                                          k.ps[:, 2 + u, 0:TG * W].rearrange("p (t w) -> p t w", w=W),
                                          bc(b[:, :].unsqueeze(1), [P, TG, W]), ALU.add).then_inc(taken.sem, 1)


def attention(k, heads, E, nk, scale, weights, gate_col, clip=None, gated=False):
    nc = k.nc
    dh = P // heads
    narrow = dh < 32
    NS = TG * heads // 4
    per_norm = 4 if narrow else 1
    NN = NS // per_norm
    nh = 16 if narrow else TG
    self_attn = nk == P
    R = E * G
    with ExitStack() as ctx:
        xT = k.sb("at_xT", [P, 2, TG * P], ctx=ctx)
        kv = xT if self_attn else k.sb("at_kv", [P, 2, TG * nk], ctx=ctx)
        w = k.sb("at_w", [P, 4, P], ctx=ctx)
        bcol = k.sb("at_bcol", [P, 2], ctx=ctx)
        vrow = k.sb("at_vrow", [P, P], ctx=ctx)
        orow = k.sb("at_orow", [1, P], ctx=ctx)
        q_sb = k.sb("at_q", [P, TG * P], ctx=ctx)
        NM = 4 if narrow else 1
        k_sb = k.sb("at_k", [P, NM, TG, nk], ctx=ctx)
        v_sb = k.sb("at_v", [P, TG, heads, dh + 1], ctx=ctx)
        clipped = k.sb("at_clip", [P, 2, 4 * nk], ctx=ctx) if clip else None
        negmax = k.sb("at_max", [P, 2, 4], ctx=ctx)
        probs = k.sb("at_p", [P, 2, 4, nk], ctx=ctx)
        pT = k.sb("at_pT", [P, 2, 4 * P], ctx=ctx)
        rec = k.sb("at_rec", [P, nh], ctx=ctx)
        o_sb = k.sb("at_o", [P, TG, P], ctx=ctx)
        oT = k.sb("at_oT", [P, TG * P], ctx=ctx)
        gcur = k.sb("at_g", [P, TG], ctx=ctx)

        loaded = k.sig("dma_landed", 4, E)
        ready = k.sig("x_ready", 1, R)
        q_ps, k_ps, v_ps = (k.sig(f"{n}_made", 1, R) for n in "qkv")
        q_in, k_in, v_in = (k.sig(f"{n}_in_sbuf", 1, R) for n in "qkv")
        s_ps = k.sig("scores_made", NS, R)
        mx = k.sig("max_found", NS, R)
        ex = k.sig("exp_done", NS, R)
        t_ps = k.sig("probs_turned", NS, R)
        t_in = k.sig("probsT_in_sbuf", NS, R)
        pv = k.sig("outputs_made", NS, R)
        rc = k.sig("sums_inverted", NN, R)
        nrm = k.sig("outputs_scaled", NN, R)
        ot_ps = k.sig("outputs_turned", 1, R)
        ot_in = k.sig("outputsT_in_sbuf", 1, R)
        y_ps = k.sig("y_made", 1, R)
        added = k.sig("y_added", 1, R)
        gsel = k.sig("gates_copied", 1, R) if gated else None
        clp = k.sig("scores_clipped", NS, R) if clip else None
        onesc = k.sig("ones_column_set", 1)
        A0, T0, PQ, PK, PO, PY = 0, 2, 4, 5, 6, 7

        with nc.Block() as block:
            @block.sync
            def _(sp):
                with sp.Fori(0, E) as e:
                    sp.wait_ge(added.sem, added.upto(0, e * G))
                    sp.dma_start(w[:, :, :], weights["w"][ds(e, 1)].rearrange("a p n c -> p (a n) c")
                                 ).then_inc(loaded.sem, 16)
                    sp.dma_start(bcol[:, :], weights["bcol"][ds(e, 1)].rearrange("a p n -> p (a n)")
                                 ).then_inc(loaded.sem, 16)
                    sp.dma_start(vrow[:, :], weights["rows"][ds(e, 1), 0, :].rearrange("a c -> (a c)")
                                 .partition_broadcast(P)).then_inc(loaded.sem, 16)
                    sp.dma_start(orow[:, :], weights["rows"][ds(e, 1), 1, :]).then_inc(loaded.sem, 16)

            @block.gpsimd
            def _(pool):
                for e, r, u, g in rounds(pool, E):
                    if u == 0:
                        pool.wait_ge(v_ps.sem, v_ps.upto(0, r))
                    last = pool.tensor_copy(xT[:, u], k.nxT_all[:, ds(g * (TG * P), TG * P)])
                    if not self_attn:
                        last = pool.tensor_copy(kv[0:CK, u], k.ctxT[:, ds(g * (TG * nk), TG * nk)])
                    last.then_inc(ready.sem, 1)

            @block.tensor
            def _(pe):
                ck = P if self_attn else CK

                def scores(r, s):
                    if s >= 2:
                        free = clp or ex
                        pe.wait_ge(free.sem, free.upto(s - 1, r))
                    elif s == 0:
                        free = clp or ex
                        pe.wait_ge(free.sem, free.upto(0, r))
                    bank = k.ps[:, A0 + s % 2, 0:4 * nk]
                    if narrow:
                        t, rg = divmod(s, 4)
                        rows = slice(32 * rg, 32 * rg + 32)
                        mm = pe.matmul(bank.rearrange("p (h n) -> p h n", n=nk), q_sb[rows, t * P:(t + 1) * P],
                                       k_sb[rows, :, t, :], start=True, stop=True)
                    else:
                        rows = slice(dh * s, dh * s + dh)
                        for t in range(TG):
                            mm = pe.matmul(k.ps[:, A0 + s % 2, t * nk:(t + 1) * nk], q_sb[rows, t * P:(t + 1) * P],
                                           k_sb[rows, 0, t, :], start=True, stop=True)
                    mm.then_inc(s_ps.sem, 1)

                def turn(r, s):
                    pe.wait_ge(ex.sem, ex.upto(s + 1, r))
                    pe.wait_ge(t_in.sem, t_in.upto(max(s - 1, 0), r))
                    for j in range(4):
                        mm = pe.transpose(k.ps[0:nk, T0 + s % 2, j * P:(j + 1) * P], probs[:, s % 2, j, :],
                                          k.ident[:, :])
                    mm.then_inc(t_ps.sem, 1)

                def outputs(r, s):
                    pe.wait_ge(t_in.sem, t_in.upto(s + 1, r))
                    if s == 0:
                        pe.wait_ge(v_in.sem, v_in.upto(1, r))
                    if s % per_norm == 0:
                        pe.wait_ge(nrm.sem, nrm.upto(s // per_norm, r))
                    for j in range(4):
                        if narrow:
                            t, h = s // 4, 4 * (s % 4) + j
                            slot = h
                        else:
                            t, h = j, s
                            slot = t
                        mm = pe.matmul(k.ps[:, PO, slot * (dh + 1):(slot + 1) * (dh + 1)],
                                       pT[0:nk, s % 2, j * P:(j + 1) * P], v_sb[0:nk, t, h, :], start=True, stop=True)
                    mm.then_inc(pv.sem, 1)

                for e, r, u, g in rounds(pe, E):
                    if u == 0:
                        pe.wait_ge(loaded.sem, loaded.upto(4, e))
                    pe.wait_ge(ready.sem, ready.upto(1, r))
                    pe.wait_ge(ot_in.sem, ot_in.upto(0, r))
                    pe.matmul(k.ps[:, PQ, :], w[:, 0, :], xT[:, u], start=True, stop=True).then_inc(q_ps.sem, 1)
                    pe.wait_ge(k_in.sem, k_in.upto(0, r))
                    pe.matmul(k.ps[:, PK, 0:TG * nk], w[0:ck, 1, :], kv[0:ck, u], start=True,
                              stop=True).then_inc(k_ps.sem, 1)
                    pe.wait_ge(added.sem, added.upto(0, r))
                    for t in range(TG):
                        mm = pe.matmul(k.ps[0:nk, PY, t * P:(t + 1) * P], kv[0:ck, u, t * nk:(t + 1) * nk],
                                       w[0:ck, 2, :], start=True, stop=True)
                    mm.then_inc(v_ps.sem, 1)
                    pe.wait_ge(q_in.sem, q_in.upto(1, r))
                    pe.wait_ge(k_in.sem, k_in.upto(1, r))
                    for s in range(NS + 2):
                        if s < NS:
                            scores(r, s)
                        if 1 <= s <= NS:
                            turn(r, s - 1)
                        if s >= 2:
                            outputs(r, s - 2)
                    pe.wait_ge(nrm.sem, nrm.upto(NN, r))
                    for t in range(TG):
                        mm = pe.transpose(k.ps[:, PQ, t * P:(t + 1) * P], o_sb[:, t, :], k.ident[:, :])
                    mm.then_inc(ot_ps.sem, 1)
                    pe.wait_ge(ot_in.sem, ot_in.upto(1, r))
                    for t in range(TG):
                        y = k.ps[:, PY, t * P:(t + 1) * P]
                        pe.matmul(y, k.ones[0:1, :], orow[0:1, :], start=True, stop=False)
                        mm = pe.matmul(y, oT[:, t * P:(t + 1) * P], w[:, 3, :], start=False, stop=True)
                    mm.then_inc(y_ps.sem, 1)

            @block.scalar
            def _(act):
                for e, r, u, g in rounds(act, E):
                    for s in range(NS):
                        act.wait_ge(mx.sem, mx.upto(s + 1, r))
                        act.wait_ge(t_ps.sem, t_ps.upto(max(s - 1, 0), r))
                        for j in range(4):
                            src = clipped[:, s % 2, j * nk:(j + 1) * nk] if clip else \
                                k.ps[:, A0 + s % 2, j * nk:(j + 1) * nk]
                            last = act.activation(probs[:, s % 2, j, :], src, ACT.Exp, bias=negmax[:, s % 2, j:j + 1])
                        last.then_inc(ex.sem, 1)
                    act.wait_ge(ot_ps.sem, ot_ps.upto(1, r))
                    act.copy(oT[:, :], k.ps[:, PQ, :]).then_inc(ot_in.sem, 1)

            @block.vector
            def _(dve):
                dve.memset(v_sb[:, :, :, dh:dh + 1], 1.0).then_inc(onesc.sem, 1)
                dve.wait_ge(onesc.sem, onesc.upto(1))

                def top(r, s):
                    dve.wait_ge(s_ps.sem, s_ps.upto(s + 1, r))
                    dve.wait_ge(ex.sem, ex.upto(max(s - 1, 0), r))
                    src = k.ps[:, A0 + s % 2, 0:4 * nk]
                    if clip:
                        dve.tensor_scalar(clipped[:, s % 2], src, clip, -clip, ALU.min, ALU.max).then_inc(clp.sem, 1)
                        dve.wait_ge(clp.sem, clp.upto(s + 1, r))
                        src = clipped[:, s % 2]
                    dve.tensor_reduce(negmax[:, s % 2], src.rearrange("p (h n) -> p h n", n=nk), X, ALU.max,
                                      negate=True).then_inc(mx.sem, 1)

                def fetch(r, s):
                    dve.wait_ge(t_ps.sem, t_ps.upto(s + 1, r))
                    dve.wait_ge(pv.sem, pv.upto(max(s - 1, 0), r))
                    dve.tensor_copy(pT[0:nk, s % 2, :], k.ps[0:nk, T0 + s % 2, :]).then_inc(t_in.sem, 1)

                def scale_outputs(r, s):
                    n = s // per_norm
                    dve.wait_ge(pv.sem, pv.upto(s + 1, r))
                    o = k.ps[:, PO, 0:nh * (dh + 1)].rearrange("p (h c) -> p h c", c=dh + 1)
                    dve.reciprocal(rec[:, :], o[:, :, dh]).then_inc(rc.sem, 1)
                    dve.wait_ge(rc.sem, rc.upto(n + 1, r))
                    out = o_sb[:, n, :].rearrange("p (h c) -> p h c", c=dh) if narrow \
                        else o_sb[:, :, n * dh:(n + 1) * dh]
                    dve.tensor_tensor(out, o[:, :, 0:dh], bc(rec[:, :].unsqueeze(2), [P, nh, dh]),
                                      ALU.mult).then_inc(nrm.sem, 1)

                for e, r, u, g in rounds(dve, E):
                    if u == 0:
                        dve.wait_ge(loaded.sem, loaded.upto(4, e))
                    dve.wait_ge(q_ps.sem, q_ps.upto(1, r))
                    dve.tensor_scalar(q_sb[:, :], k.ps[:, PQ, :], bcol[:, 0:1], scale, ALU.add,
                                      ALU.mult).then_inc(q_in.sem, 1)
                    dve.wait_ge(k_ps.sem, k_ps.upto(1, r))
                    for m in range(NM):
                        mask = k.cols[:, 2 + m:3 + m] if narrow else k.cols[:, 1:2]
                        last = dve.tensor_scalar(k_sb[:, m].rearrange("p t n -> p (t n)"), k.ps[:, PK, 0:TG * nk],
                                                 bcol[:, 1:2], mask, ALU.add, ALU.mult)
                    last.then_inc(k_in.sem, 1)
                    dve.wait_ge(v_ps.sem, v_ps.upto(1, r))
                    for t in range(TG):
                        last = dve.tensor_tensor(v_sb[0:nk, t, :, 0:dh],
                                                 k.ps[0:nk, PY, t * P:(t + 1) * P].rearrange("p (h c) -> p h c", c=dh),
                                                 vrow[0:nk, :].rearrange("p (h c) -> p h c", c=dh), ALU.add)
                    last.then_inc(v_in.sem, 1)
                    if gated:
                        dve.wait_ge(added.sem, added.upto(0, r))
                        dve.tensor_copy(gcur[:, :], k.gates[:, ds(e, 1), ds(g * TG, TG)].rearrange("p a t -> p (a t)")
                                        ).then_inc(gsel.sem, 1)
                    for s in range(NS + 2):
                        if s < NS:
                            top(r, s)
                        if 1 <= s <= NS:
                            fetch(r, s - 1)
                        if s >= 2 and (s - 2) % per_norm == per_norm - 1:
                            scale_outputs(r, s - 2)
                    dve.wait_ge(y_ps.sem, y_ps.upto(1, r))
                    if gated:
                        dve.wait_ge(gsel.sem, gsel.upto(1, r))
                    add_gated(k, dve, k.x_all, g, k.ps[:, PY, :], gcur if gated else None, gate_col, added)


def add_gated(k, dve, target, g, y, gcur, gate_col, done):
    if gcur is None:
        last = dve.scalar_tensor_tensor(target[:, ds(g * TG, TG), :].rearrange("p t c -> p (t c)"), y, gate_col,
                                        target[:, ds(g * TG, TG), :].rearrange("p t c -> p (t c)"), ALU.mult, ALU.add)
    else:
        for t in range(TG):
            x = target[:, ds(g * TG + t, 1), :].rearrange("p a c -> p (a c)")
            last = dve.scalar_tensor_tensor(x, y[:, t * P:(t + 1) * P], gcur[:, t:t + 1], x, ALU.mult, ALU.add)
    last.then_inc(done.sem, 1)


def experts(k, E, MC, func, weights, target, up, pair=False, gate_col=None, gated=True):
    nc = k.nc
    R = E * G
    NY = 2 if pair else 1
    with ExitStack() as ctx:
        w1 = k.sb("ex_w1", [P, MC * P], ctx=ctx)
        w3 = k.sb("ex_w3", [P, MC * P], ctx=ctx) if up else None
        w2 = k.sb("ex_w2", [P, MC, P], ctx=ctx)
        bcol = k.sb("ex_bcol", [P, 2 * MC], ctx=ctx)
        orow = k.sb("ex_orow", [1, P], ctx=ctx)
        act_sb = k.sb("ex_act", [P, 2, TG * P], ctx=ctx)
        hid = k.sb("ex_hid", [P, 2, MC, TG * P], ctx=ctx)
        gcur = k.sb("ex_g", [P, 2, NY * TG], ctx=ctx)
        ND = 4 + bool(up)
        loaded = k.sig("dma_landed", ND, E)
        g_ps = k.sig("h1_made", MC, R)
        u_ps = k.sig("h3_made", MC, R) if up else None
        a_in = k.sig("h1_activated", MC, R)
        h_in = k.sig("hidden_in_sbuf", MC, R) if up else None
        y_ps = k.sig("y_made", 1, R)
        added = k.sig("y_added", NY, R)
        gsel = k.sig("gates_copied", 1, R) if gated else None
        hdone = h_in if up else a_in
        with nc.Block() as block:
            @block.sync
            def _(sp):
                with sp.Fori(0, E) as e:
                    sp.wait_ge(added.sem, added.upto(0, e * G))
                    sp.dma_start(w1[:, :], weights["w1"][ds(e, 1)].rearrange("a p m -> p (a m)")).then_inc(loaded.sem, 16)
                    if up:
                        sp.dma_start(w3[:, :], weights["w3"][ds(e, 1)].rearrange("a p m -> p (a m)")
                                     ).then_inc(loaded.sem, 16)
                    sp.dma_start(w2[:, :, :], weights["w2"][ds(e, 1)].rearrange("a p m c -> p (a m) c")
                                 ).then_inc(loaded.sem, 16)
                    sp.dma_start(bcol[:, :], weights["bcol"][ds(e, 1)].rearrange("a p m -> p (a m)")
                                 ).then_inc(loaded.sem, 16)
                    sp.dma_start(orow[:, :], weights["brow"][ds(e, 1), :]).then_inc(loaded.sem, 16)

            @block.tensor
            def _(pe):
                def hidden(r, u, g):
                    x = k.nxT_all[:, ds(g * (TG * P), TG * P)]
                    for m in range(MC):
                        n = u * MC + m
                        back = m - 1 if m >= 1 else 0
                        pe.wait_ge(hdone.sem, hdone.upto(back, r) if m >= 1 or MC > 1 else hdone.upto(0, r))
                        pe.matmul(k.ps[:, n % 2, :], w1[:, m * P:(m + 1) * P], x, start=True,
                                  stop=True).then_inc(g_ps.sem, 1)
                        if up:
                            pe.matmul(k.ps[:, 2 + n % 2, :], w3[:, m * P:(m + 1) * P], x, start=True,
                                      stop=True).then_inc(u_ps.sem, 1)

                def down(r, u):
                    pe.wait_ge(hdone.sem, hdone.upto(MC, r))
                    pe.wait_ge(added.sem, added.upto(0, r))
                    for t in range(TG):
                        tok = slice(t * P, (t + 1) * P)
                        if pair:
                            for a in range(2):
                                f = slice(64 * a, 64 * a + 64)
                                mm = pe.matmul(k.ps[:, 4 + 2 * u + a, tok], hid[f, u, 0, tok], w2[f, 0, :], start=True,
                                               stop=True)
                        else:
                            pe.matmul(k.ps[:, 4 + u, tok], k.ones[0:1, :], orow[0:1, :], start=True, stop=False)
                            for m in range(MC):
                                mm = pe.matmul(k.ps[:, 4 + u, tok], hid[:, u, m, tok], w2[:, m, :], start=False,
                                               stop=m == MC - 1)
                    mm.then_inc(y_ps.sem, 1)

                todo = []
                for e, r, u, g in rounds(pe, E):
                    if u == 0:
                        pe.wait_ge(loaded.sem, loaded.upto(ND, e))
                    hidden(r, u, g)
                    todo.append((r, u))
                    if u == 1:
                        for a in todo:
                            down(*a)
                        todo = []

            @block.scalar
            def _(act):
                for e, r, u, g in rounds(act, E):
                    if u == 0:
                        act.wait_ge(loaded.sem, loaded.upto(ND, e))
                    for m in range(MC):
                        n = u * MC + m
                        act.wait_ge(g_ps.sem, g_ps.upto(m + 1, r))
                        if up:
                            act.wait_ge(h_in.sem, h_in.upto(max(m - 1, 0), r))
                            out = act_sb[:, n % 2]
                        else:
                            if m == 0:
                                act.wait_ge(y_ps.sem, y_ps.upto(0, r) if u == 0 else y_ps.upto(0, r - 1))
                            out = hid[:, u, m, :]
                        act.activation(out, k.ps[:, n % 2, :], func, bias=bcol[:, m:m + 1]).then_inc(a_in.sem, 1)

            @block.vector
            def _(dve):
                held = []
                for e, r, u, g in rounds(dve, E):
                    if u == 0:
                        dve.wait_ge(loaded.sem, loaded.upto(ND, e))
                    if up:
                        for m in range(MC):
                            n = u * MC + m
                            dve.wait_ge(u_ps.sem, u_ps.upto(m + 1, r))
                            dve.wait_ge(a_in.sem, a_in.upto(m + 1, r))
                            dve.scalar_tensor_tensor(hid[:, u, m, :], k.ps[:, 2 + n % 2, :], bcol[:, MC + m:MC + m + 1],
                                                     act_sb[:, n % 2], ALU.add, ALU.mult).then_inc(h_in.sem, 1)
                    if gated:
                        if u == 0:
                            dve.wait_ge(added.sem, added.upto(0, r))
                        for a in range(NY):
                            last = dve.tensor_copy(gcur[:, u, a * TG:(a + 1) * TG],
                                                   k.gates[:, ds(e * NY + a, 1), ds(g * TG, TG)]
                                                   .rearrange("p a t -> p (a t)"))
                        last.then_inc(gsel.sem, 1)
                    held.append((r, u, g))
                    if u == 1:
                        for r, u, g in held:
                            dve.wait_ge(y_ps.sem, y_ps.upto(1, r))
                            if gated:
                                dve.wait_ge(gsel.sem, gsel.upto(1, r))
                            for a in range(NY):
                                if a:
                                    dve.wait_ge(added.sem, added.upto(a, r))
                                bank = 4 + 2 * u + a if pair else 4 + u
                                add_gated(k, dve, target, g, k.ps[:, bank, :],
                                          gcur[:, u, a * TG:(a + 1) * TG] if gated else None, gate_col, added)
                        held = []


def router_logits(k, h_all, H, rw):
    nc = k.nc
    with ExitStack() as ctx:
        w2 = k.sb("ro_w2", [P, 8], ctx=ctx)
        b2 = k.sb("ro_b2", [P, 8], ctx=ctx)
        lg = k.sb("ro_g", [P, H], ctx=ctx)
        lb = k.sb("ro_b", [P, H], ctx=ctx)
        rows = k.sb("ro_rows", [P, 2, TG, H], ctx=ctx)
        hT = k.sb("ro_hT", [P, 2, TG * P // 2], ctx=ctx)
        loaded = k.sig("dma_landed", 5)
        chain = k.sig("dve_step", 3)
        staged = k.sig("staged", 1, G)
        turned = k.sig("turned", 1, G)
        copied = k.sig("copied", 1, G)
        routed = k.sig("routed", 1, G)
        taken = k.sig("routes_taken", 1, G)
        with nc.Block() as block:
            @block.sync
            def _(sp):
                for to, of in ((w2[0:H, :], rw["w2"]), (w2[H:2 * H, :], rw["w2"]), (b2[:, :], rw["b2"].partition_broadcast(P)),
                               (lg[:, :], rw["g"].partition_broadcast(P)), (lb[:, :], rw["b"].partition_broadcast(P))):
                    sp.dma_start(to, of).then_inc(loaded.sem, 16)

            @block.tensor
            def _(pe):
                pe.wait_ge(loaded.sem, loaded.upto(5))
                for _, r, u, g in rounds(pe):
                    pe.wait_ge(staged.sem, staged.upto(1, r))
                    if u == 0:
                        pe.wait_ge(copied.sem, copied.upto(0, r))
                    for t in range(0, TG, 2):
                        mm = pe.transpose(k.ps[:, u, t * H:(t + 2) * H],
                                          rows[:, u, t:t + 2, :].rearrange("p t h -> p (t h)"), k.ident[:, :])
                    mm.then_inc(turned.sem, 1)
                    pe.wait_ge(copied.sem, copied.upto(1, r))
                    if u == 0:
                        pe.wait_ge(taken.sem, taken.upto(0, r))
                    for t in range(TG):
                        a, f = t % 2, slice(H * (t % 2), H * (t % 2) + H)
                        mm = pe.matmul(k.ps[:, 2 + 2 * a + u, (t // 2) * 8:(t // 2 + 1) * 8],
                                       hT[f, u, (t // 2) * P:(t // 2 + 1) * P], w2[f, :], start=True, stop=True)
                    mm.then_inc(routed.sem, 1)

            @block.scalar
            def _(act):
                for _, r, u, g in rounds(act):
                    act.wait_ge(turned.sem, turned.upto(1, r))
                    if u == 0:
                        act.wait_ge(routed.sem, routed.upto(0, r))
                    act.copy(hT[:, u], k.ps[:, u, 0:TG * H]).then_inc(copied.sem, 1)

            @block.vector
            def _(dve):
                link = Chain(dve, chain)
                dve.wait_ge(loaded.sem, loaded.upto(5))
                link(dve.tensor_tensor(h_all[:, :, :], h_all[:, :, :], bc(lg[:, :].unsqueeze(1), [P, B, H]), ALU.mult))
                link(dve.tensor_tensor(h_all[:, :, :], h_all[:, :, :], bc(lb[:, :].unsqueeze(1), [P, B, H]), ALU.add))
                link(dve.tensor_scalar(h_all[:, :, :], h_all[:, :, :], 0.0, None, ALU.max))
                for _, r, u, g in rounds(dve):
                    if u == 0:
                        dve.wait_ge(turned.sem, turned.upto(0, r))
                    dve.tensor_copy(rows[:, u], h_all[:, ds(g * TG, TG), :]).then_inc(staged.sem, 1)
                    dve.wait_ge(routed.sem, routed.upto(1, r))
                    for a in range(2):
                        last = dve.tensor_tensor(k.logits[:, ds(g * TG + a, TG // 2, 2), :],
                                                 k.ps[:, 2 + 2 * a + u, 0:TG * 4].rearrange("p (t w) -> p t w", w=8),
                                                 bc(b2[:, :].unsqueeze(1), [P, TG // 2, 8]), ALU.add)
                    last.then_inc(taken.sem, 1)


def top_two_gates(k, gate_col, plus=None, least=None, shared=0, capacity=None):
    nc = k.nc
    NE = 8
    S3 = [P, B, NE]
    with ExitStack() as ctx:
        t3 = [k.sb(f"tg_{i}", S3, ctx=ctx) for i in range(6)]
        c2 = [k.sb(f"tg_c{i}", [P, B], ctx=ctx) for i in range(3)]
        first, second, prob, a, b, c = t3
        m, s, z = c2
        if capacity:
            before = k.sb("tg_before", [P, P], ctx=ctx)
            tot = k.sb("tg_tot", [P, 2, B, NE], ctx=ctx)
            loc = k.sb("tg_loc", [P, 2, B, NE], ctx=ctx)
            run = k.sb("tg_run", [P, NE, B], ctx=ctx)
            zero = k.sb("tg_zero", [P, B], ctx=ctx)
        chain = k.sig("dve_step", 400)
        chosen = k.sig("chosen", 1)
        shifted = k.sig("shifted", 1)
        expd = k.sig("exp_done", 1)
        if capacity:
            counted = k.sig("counted", 1)
            loaded = k.sig("dma_landed", 1)
        with nc.Block() as block:
            if capacity:
                @block.sync
                def _(sp):
                    sp.dma_start(before[:, :], k.d["before"]).then_inc(loaded.sem, 16)

                @block.tensor
                def _(pe):
                    pe.wait_ge(loaded.sem, loaded.upto(1))
                    pe.wait_ge(chosen.sem, chosen.upto(1))
                    for i, one in enumerate((first, second)):
                        flat = one[:, :, :].rearrange("p t e -> p (t e)")
                        pe.matmul(k.ps[:, 2 * i, :], before[:, :], flat, start=True, stop=True)
                        mm = pe.matmul(k.ps[:, 2 * i + 1, :], k.ones[:, :], flat, start=True, stop=True)
                    mm.then_inc(counted.sem, 1)

            @block.scalar
            def _(act):
                act.wait_ge(shifted.sem, shifted.upto(1))
                act.activation(prob[:, :, :], c[:, :, :], ACT.Exp).then_inc(expd.sem, 1)

            @block.vector
            def _(dve):
                link = Chain(dve, chain)

                def wide(col):
                    return bc(col[:, :].unsqueeze(2), S3)

                def pick(values, onehot):
                    link(dve.tensor_reduce(s[:, :], values[:, :, :], X, ALU.max))
                    link(dve.tensor_tensor(b[:, :, :], values[:, :, :], wide(s), ALU.is_equal))
                    link(dve.tensor_tensor(b[:, :, :], b[:, :, :], bc(k.rank[:, :].unsqueeze(1), S3), ALU.mult))
                    link(dve.tensor_reduce(z[:, :], b[:, :, :], X, ALU.max))
                    link(dve.tensor_tensor(onehot[:, :, :], b[:, :, :], wide(z), ALU.is_equal))

                lg = k.logits
                link(dve.tensor_reduce(m[:, :], lg[:, :, :], X, ALU.max))
                dve.tensor_tensor(c[:, :, :], lg[:, :, :], wide(m), ALU.subtract).then_inc(shifted.sem, 1)
                pick(lg, first)
                link(dve.scalar_tensor_tensor(a[:, :, :], first[:, :, :], -1e30, lg[:, :, :], ALU.mult, ALU.add))
                pick(a, second)
                link(dve.tensor_copy(m[:, 0:1], m[:, 0:1]))
                chosen_now = dve.tensor_tensor(a[:, :, :], first[:, :, :], second[:, :, :], ALU.add)
                chosen_now.then_inc(chosen.sem, 1)
                dve.wait_ge(chosen.sem, chosen.upto(1))
                dve.wait_ge(expd.sem, expd.upto(1))
                link(dve.tensor_reduce(z[:, :], prob[:, :, :], X, ALU.add))
                link(dve.reciprocal(s[:, :], z[:, :]))
                link(dve.tensor_tensor(prob[:, :, :], prob[:, :, :], wide(s), ALU.mult))
                link(dve.tensor_tensor(b[:, :, :], prob[:, :, :], a[:, :, :], ALU.mult))
                link(dve.tensor_reduce(z[:, :], b[:, :, :], X, ALU.add))
                if plus:
                    link(dve.tensor_scalar(z[:, :], z[:, :], plus, None, ALU.add))
                if least:
                    link(dve.tensor_scalar(z[:, :], z[:, :], least, None, ALU.max))
                link(dve.reciprocal(s[:, :], z[:, :]))
                link(dve.tensor_scalar(s[:, :], s[:, :], gate_col, None, ALU.mult))
                if capacity:
                    link(dve.memset(zero[:, :], 0.0))
                    dve.wait_ge(counted.sem, counted.upto(1))
                    for i in range(2):
                        link(dve.tensor_copy(tot[:, i].rearrange("p t e -> p (t e)"), k.ps[:, 2 * i + 1, :]))
                        for e in range(NE):
                            start = 0.0 if i == 0 else z[:, e:e + 1]
                            link(dve.tensor_tensor_scan(run[:, e, :], tot[:, i, :, e], zero[:, :], start, ALU.add,
                                                        ALU.add))
                        link(dve.tensor_copy(z[:, 0:NE], run[:, :, B - 1]))
                        link(dve.tensor_tensor(c[:, :, :], run[:, :, :].rearrange("p e t -> p t e"), tot[:, i],
                                               ALU.subtract))
                        link(dve.tensor_tensor(loc[:, i], c[:, :, :],
                                               k.ps[:, 2 * i, :].rearrange("p (t e) -> p t e", e=NE), ALU.add))
                        one = first if i == 0 else second
                        link(dve.scalar_tensor_tensor(one[:, :, :], loc[:, i], float(capacity), one[:, :, :],
                                                      ALU.is_lt, ALU.mult))
                    link(dve.tensor_tensor(a[:, :, :], first[:, :, :], second[:, :, :], ALU.add))
                    link(dve.tensor_tensor(b[:, :, :], prob[:, :, :], a[:, :, :], ALU.mult))
                link(dve.tensor_tensor(k.gates[:, 0:NE, :].rearrange("p e t -> p t e"), b[:, :, :], wide(s), ALU.mult))
                for e in range(shared):
                    link(dve.tensor_scalar(k.gates[:, NE + e, :], m[:, :], 0.0, gate_col, ALU.mult, ALU.add))
                chain.per = chain.each = link.n


def ssm_kernel(k, ww, conv_dram):
    nc = k.nc
    N, L = 64, P
    re = k.nx_all[:, :, :]
    im = k.nxT_all[:, :].rearrange("p (n l) -> p n l", l=L)
    with ExitStack() as ctx:
        inp = k.sb("sk_in", [P, 4 * N + 2], ctx=ctx)
        t = [k.sb(f"sk_{i}", [P, N], ctx=ctx) for i in range(12)]
        t1 = k.sb("sk_t1", [P, N, L // 2], ctx=ctx)
        t2 = k.sb("sk_t2", [P, N, L // 2], ctx=ctx)
        row = k.sb("sk_row", [P, 2 * P], ctx=ctx)
        loaded = k.sig("dma_landed", 1)
        stored = k.sig("dma_stored", 1)
        chain = k.sig("dve_step", 400)
        to_sin = k.sig("angles_ready", 2)
        sins = k.sig("sines_done", 2)
        finished = k.sig("kernel_ready", 1)
        with nc.Block() as block:
            @block.sync
            def _(sp):
                sp.dma_start(inp[:, :], ww["ssm"]).then_inc(loaded.sem, 16)
                sp.wait_ge(finished.sem, finished.upto(1))
                sp.dma_start(conv_dram, row[:, :]).then_inc(stored.sem, 16)
                sp.wait_ge(stored.sem, stored.upto(1))

            @block.scalar
            def _(act):
                for i in range(2):
                    act.wait_ge(to_sin.sem, to_sin.upto(i + 1))
                    act.activation(t[2 + i][:, :], t[i][:, :], ACT.Sin).then_inc(sins.sem, 1)

            @block.vector
            def _(dve):
                link = Chain(dve, chain)
                A_re, A_im, C_re, C_im = (inp[:, i * N:(i + 1) * N] for i in range(4))
                log_dt, skip = inp[:, 4 * N:4 * N + 1], inp[:, 4 * N + 1:4 * N + 2]

                def exps(x, w, p2, u, r, f, em1=None, ex=None):
                    link(dve.tensor_scalar(r, x, 80.0, -80.0, ALU.min, ALU.max))
                    link(dve.tensor_scalar(p2, r, 1.4426950408889634, None, ALU.mult))
                    link(dve.tensor_scalar(p2, p2, MAGIC + 127.0, None, ALU.add))
                    link(dve.tensor_scalar(f, p2, MAGIC + 127.0, None, ALU.subtract))
                    link(dve.scalar_tensor_tensor(r, f, -0.693359375, r, ALU.mult, ALU.add))
                    link(dve.scalar_tensor_tensor(r, f, 2.12194440e-4, r, ALU.mult, ALU.add))
                    link(dve.tensor_scalar(u, r, 1.0 / 8, 1.0, ALU.mult, ALU.add))
                    for j in range(7, 1, -1):
                        link(dve.scalar_tensor_tensor(u, u, 1.0 / j, r, ALU.mult, ALU.mult))
                        link(dve.tensor_scalar(u, u, 1.0, None, ALU.add))
                    link(dve.tensor_tensor(u, u, r, ALU.mult))
                    link(dve.tensor_scalar(p2.bitcast(I32), p2.bitcast(I32), 23, None, ALU.logical_shift_left))
                    link(dve.tensor_tensor(u, u, p2, ALU.mult))
                    if ex is not None:
                        link(dve.tensor_tensor(ex, u, p2, ALU.add))
                    if em1 is not None:
                        link(dve.tensor_scalar(p2, p2, 1.0, None, ALU.subtract))
                        link(dve.tensor_tensor(em1, u, p2, ALU.add))

                def col(i, w=N):
                    return t[i][:, 0:w]

                dve.wait_ge(loaded.sem, loaded.upto(1))
                exps(log_dt, 1, col(4, 1), col(5, 1), col(6, 1), col(7, 1), ex=col(8, 1))
                dt = t[8][:, 0:1]
                link(dve.tensor_scalar(col(9), A_im, dt, 0.5, ALU.mult, ALU.mult))
                for i in range(2):
                    link(dve.tensor_scalar(col(4), col(9), 0.15915494309189535, 0.25 * i, ALU.mult, ALU.add))
                    link(dve.tensor_scalar(col(4), col(4), MAGIC, None, ALU.add))
                    link(dve.tensor_scalar(col(4), col(4), MAGIC, None, ALU.subtract))
                    link(dve.scalar_tensor_tensor(col(i), col(4), -6.28125, col(9), ALU.mult, ALU.add))
                    link(dve.scalar_tensor_tensor(col(i), col(4), -1.9353071795864769e-3, col(i), ALU.mult, ALU.add))
                    if i:
                        link(dve.tensor_scalar(col(i), col(i), 1.5707963267948966, None, ALU.add))
                    last = dve.tensor_scalar(col(i), col(i), 3.1415925, -3.1415925, ALU.min, ALU.max)
                    last.then_inc(to_sin.sem, 1)
                link(dve.tensor_scalar(col(10), A_re, dt, None, ALU.mult))
                exps(col(10), N, col(4), col(5), col(6), col(7), em1=col(11), ex=col(9))
                dve.wait_ge(sins.sem, sins.upto(2))
                s, c = col(2), col(3)
                link(dve.scalar_tensor_tensor(col(4), s, -2.0, s, ALU.mult, ALU.mult))
                link(dve.scalar_tensor_tensor(col(5), s, 2.0, c, ALU.mult, ALU.mult))
                link(dve.tensor_scalar(col(6), col(4), 1.0, None, ALU.add))
                zi = col(0)
                link(dve.tensor_tensor(zi, col(9), col(5), ALU.mult))
                link(dve.tensor_tensor(col(7), col(11), col(6), ALU.mult))
                link(dve.tensor_tensor(col(7), col(7), col(4), ALU.add))
                zr = col(1)
                link(dve.tensor_tensor(zr, col(9), col(6), ALU.mult))
                link(dve.tensor_tensor(col(2), A_re, A_re, ALU.mult))
                link(dve.tensor_tensor(col(3), A_im, A_im, ALU.mult))
                link(dve.tensor_tensor(col(2), col(2), col(3), ALU.add))
                link(dve.reciprocal(col(2), col(2)))

                def cmul(orr, oi, ar, ai, br, bi, x, y, conj=1.0):
                    link(dve.tensor_tensor(x, ar, br, ALU.mult))
                    link(dve.scalar_tensor_tensor(y, ai, -conj, bi, ALU.mult, ALU.mult))
                    link(dve.tensor_tensor(orr, x, y, ALU.add))
                    link(dve.scalar_tensor_tensor(x, ar, conj, bi, ALU.mult, ALU.mult))
                    link(dve.tensor_tensor(y, ai, br, ALU.mult))
                    link(dve.tensor_tensor(oi, x, y, ALU.add))

                cmul(col(8), col(9), C_re, C_im, col(7), zi, col(3), col(4))
                cmul(col(10), col(11), col(8), col(9), A_re, A_im, col(3), col(4), conj=-1.0)
                link(dve.tensor_tensor(re[:, :, 0], col(10), col(2), ALU.mult))
                link(dve.tensor_tensor(im[:, :, 0], col(11), col(2), ALU.mult))
                m = 1
                while m < L:
                    shape = [P, N, m]
                    a, b = re[:, :, 0:m], im[:, :, 0:m]
                    x, y = t1[:, :, 0:m], t2[:, :, 0:m]
                    zrb, zib = bc(zr.unsqueeze(2), shape), bc(zi.unsqueeze(2), shape)
                    link(dve.tensor_tensor(x, a, zrb, ALU.mult))
                    link(dve.tensor_tensor(y, b, zib, ALU.mult))
                    link(dve.tensor_tensor(re[:, :, m:2 * m], x, y, ALU.subtract))
                    link(dve.tensor_tensor(x, a, zib, ALU.mult))
                    link(dve.tensor_tensor(y, b, zrb, ALU.mult))
                    link(dve.tensor_tensor(im[:, :, m:2 * m], x, y, ALU.add))
                    link(dve.scalar_tensor_tensor(col(5), zr, 2.0, zi, ALU.mult, ALU.mult))
                    link(dve.tensor_tensor(col(3), zr, zr, ALU.mult))
                    link(dve.tensor_tensor(col(4), zi, zi, ALU.mult))
                    link(dve.tensor_tensor(zr, col(3), col(4), ALU.subtract))
                    link(dve.tensor_copy(zi, col(5)))
                    m *= 2
                link(dve.memset(row[:, :], 0.0))
                kk = row[:, P - 1:2 * P - 1]
                link(dve.tensor_reduce(kk, re.rearrange("p n l -> p l n"), X, ALU.add))
                link(dve.tensor_scalar(kk, kk, 2.0, None, ALU.mult))
                link(dve.tensor_scalar(kk[:, 0:1], kk[:, 0:1], skip, None, ALU.add))
                dve.tensor_copy(row[:, 2 * P - 1:2 * P], row[:, 0:1]).then_inc(finished.sem, 1)
                chain.per = chain.each = link.n


def affine(k, target, g_dram, b_dram):
    nc = k.nc
    with ExitStack() as ctx:
        gr = k.sb("af_g", [P, P], ctx=ctx)
        br = k.sb("af_b", [P, P], ctx=ctx)
        loaded = k.sig("dma_landed", 2)
        chain = k.sig("dve_step", 2)
        with nc.Block() as block:
            @block.sync
            def _(sp):
                sp.dma_start(gr[:, :], g_dram.partition_broadcast(P)).then_inc(loaded.sem, 16)
                sp.dma_start(br[:, :], b_dram.partition_broadcast(P)).then_inc(loaded.sem, 16)

            @block.vector
            def _(dve):
                link = Chain(dve, chain)
                dve.wait_ge(loaded.sem, loaded.upto(2))
                for row, op in ((gr, ALU.mult), (br, ALU.add)):
                    link(dve.tensor_tensor(target[:, :, :], target[:, :, :], bc(row[:, :].unsqueeze(1), [P, B, P]), op))


def film_rows(k, block_dve, link, mg, brow, film):
    dve = block_dve
    link(dve.tensor_scalar(film[:, :], brow[:, :], mg, None, ALU.mult))
    link(dve.tensor_scalar(film[:, 0:P], film[:, 0:P], 1.0, None, ALU.add))


def sparse_attention(k, ww, wide):
    nc = k.nc
    H, DH, TOP = 4, 32, 32
    W = H * TG
    with ExitStack() as ctx:
        def sb(name, shape, dt=F32):
            return k.sb("sa_" + name, shape, dt, ctx=ctx)

        w = sb("w", [P, 3, P])
        wf = sb("wf", [P, 2 * P])
        brow = sb("brow", [P, 2 * P])
        film = sb("film", [P, 2 * P])
        mg = sb("mg", [P, 1])
        vm = sb("vm", [P, B * NK], U8)
        tm8 = sb("tm8", [P, B], U8)
        tm = sb("tm", [P, B])
        xT = sb("xT", [P, TG * P])
        kv = sb("kv", [P, TG * NK])
        q_sb = sb("q", [P, TG * P])
        k_sb = sb("k", [P, TG * NK])
        v_sb = sb("v", [P, TG, P])
        mb = sb("mb", [P, TG * NK])
        sm = sb("sm", [P, W, NK])
        wk = sb("wk", [P, W, NK])
        m0 = sb("m0", [P, W, 8])
        m8 = sb("m8", [P, W, 8])
        pad = sb("pad", [P, 1])
        rec = sb("rec", [P, W])
        av = sb("av", [P, TG, NK])
        aT = sb("aT", [P, TG * P])
        cT = sb("cT", [P, TG * P])
        fs = sm[:, :, :].rearrange("p w n -> p (w n)")[:, 0:TG * 2 * P].rearrange("p (t c) -> p t c", t=TG)

        R = G
        NL = 6
        loaded = k.sig("dma_landed", NL)
        setup = k.sig("setup_step", 3)
        ready = k.sig("x_ready", 1, R)
        q_ps, k_ps, v_ps = (k.sig(f"{n}_made", 1, R) for n in "qkv")
        q_in, k_in, v_in = (k.sig(f"{n}_in_sbuf", 1, R) for n in "qkv")
        s_ps = k.sig("scores_made", 1, R)
        s_in = k.sig("scores_masked", 1, R)
        CH = 21
        chain = k.sig("dve_step", CH, R)
        shifted = k.sig("shifted", 1, R)
        ex = k.sig("exp_done", 1, R)
        mean = k.sig("probs_averaged", 1, R)
        t_ps = k.sig("probs_turned", 1, R)
        t_in = k.sig("probsT_in_sbuf", 1, R)
        c_ps = k.sig("c_made", 1, R)
        c_in = k.sig("c_in_sbuf", 1, R)
        f_ps = k.sig("film_made", 1, R)
        f_in = k.sig("film_read", 1, R)
        with nc.Block() as block:
            @block.sync
            def _(sp):
                for to, of in ((w[:, :, :], ww["sa_w"]), (wf[:, :], ww["film_in"]),
                               (brow[:, :], ww["b_film_in"].partition_broadcast(P)),
                               (mg[:, :], ww["mod_gate"].partition_broadcast(P)),
                               (vm[:, :], k.d["vision_mask"].partition_broadcast(P)),
                               (tm8[:, :], k.d["text_mask"]), ):
                    sp.dma_start(to, of).then_inc(loaded.sem, 16)

            def each(eng):
                with eng.Fori(0, G) as g:
                    yield g

            @block.gpsimd
            def _(pool):
                for g in each(pool):
                    pool.wait_ge(v_ps.sem, v_ps.upto(0, g))
                    pool.tensor_copy(xT[:, :], k.nxT_all[:, ds(g * (TG * P), TG * P)])
                    pool.tensor_copy(kv[0:CK, :], k.ctxT[:, ds(g * (TG * NK), TG * NK)]).then_inc(ready.sem, 1)

            @block.tensor
            def _(pe):
                pe.wait_ge(loaded.sem, loaded.upto(NL))
                for g in each(pe):
                    pe.wait_ge(ready.sem, ready.upto(1, g))
                    pe.wait_ge(t_in.sem, t_in.upto(0, g))
                    pe.matmul(k.ps[:, 4, :], w[:, 0, :], xT[:, :], start=True, stop=True).then_inc(q_ps.sem, 1)
                    pe.wait_ge(k_in.sem, k_in.upto(0, g))
                    pe.matmul(k.ps[:, 5, 0:TG * NK], w[0:CK, 1, :], kv[0:CK, :], start=True,
                              stop=True).then_inc(k_ps.sem, 1)
                    pe.wait_ge(v_in.sem, v_in.upto(0, g))
                    for t in range(TG):
                        mm = pe.matmul(k.ps[0:NK, 6, t * P:(t + 1) * P], kv[0:CK, t * NK:(t + 1) * NK], w[0:CK, 2, :],
                                       start=True, stop=True)
                    mm.then_inc(v_ps.sem, 1)
                    pe.wait_ge(q_in.sem, q_in.upto(1, g))
                    pe.wait_ge(k_in.sem, k_in.upto(1, g))
                    pe.wait_ge(f_in.sem, f_in.upto(0, g))
                    for h in range(H):
                        rows = slice(DH * h, DH * (h + 1))
                        for t in range(TG):
                            mm = pe.matmul(k.ps[:, h, t * NK:(t + 1) * NK], q_sb[rows, t * P:(t + 1) * P],
                                           k_sb[rows, t * NK:(t + 1) * NK], start=True, stop=True)
                    mm.then_inc(s_ps.sem, 1)
                    pe.wait_ge(mean.sem, mean.upto(1, g))
                    for t in range(TG):
                        mm = pe.transpose(k.ps[0:NK, 4, t * P:(t + 1) * P], av[:, t, :], k.ident[:, :])
                    mm.then_inc(t_ps.sem, 1)
                    pe.wait_ge(t_in.sem, t_in.upto(1, g))
                    pe.wait_ge(v_in.sem, v_in.upto(1, g))
                    pe.wait_ge(c_in.sem, c_in.upto(0, g))
                    for t in range(TG):
                        mm = pe.matmul(k.ps[:, 7, t * P:(t + 1) * P], v_sb[0:NK, t, :], aT[0:NK, t * P:(t + 1) * P],
                                       start=True, stop=True)
                    mm.then_inc(c_ps.sem, 1)
                    pe.wait_ge(c_in.sem, c_in.upto(1, g))
                    for t in range(TG):
                        mm = pe.matmul(k.ps[:, t // 2, (t % 2) * 2 * P:(t % 2 + 1) * 2 * P], cT[:, t * P:(t + 1) * P],
                                       wf[:, :], start=True, stop=True)
                    mm.then_inc(f_ps.sem, 1)

            @block.scalar
            def _(act):
                for g in each(act):
                    act.wait_ge(q_ps.sem, q_ps.upto(1, g))
                    act.mul(q_sb[:, :], k.ps[:, 4, :], float(DH) ** -0.5).then_inc(q_in.sem, 1)
                    act.wait_ge(k_ps.sem, k_ps.upto(1, g))
                    act.copy(k_sb[:, :], k.ps[:, 5, 0:TG * NK]).then_inc(k_in.sem, 1)
                    act.wait_ge(v_ps.sem, v_ps.upto(1, g))
                    act.copy(v_sb[0:NK, :, :].rearrange("p t c -> p (t c)"), k.ps[0:NK, 6, :]).then_inc(v_in.sem, 1)
                    act.wait_ge(shifted.sem, shifted.upto(1, g))
                    act.activation(sm[:, :, :], sm[:, :, :], ACT.Exp).then_inc(ex.sem, 1)
                    act.wait_ge(t_ps.sem, t_ps.upto(1, g))
                    act.copy(aT[0:NK, :], k.ps[0:NK, 4, :]).then_inc(t_in.sem, 1)
                    act.wait_ge(c_ps.sem, c_ps.upto(1, g))
                    act.copy(cT[:, :], k.ps[:, 7, :])
                    act.copy(k.nxT_all[:, ds(g * (TG * P), TG * P)], k.ps[:, 7, :]).then_inc(c_in.sem, 1)

            @block.vector
            def _(dve):
                dve.wait_ge(loaded.sem, loaded.upto(NL))
                first = Chain(dve, setup)
                first(dve.tensor_copy(tm[:, :], tm8[:, :]))
                film_rows(k, dve, first, mg[:, :], brow, film)
                link = Chain(dve, chain)
                for g in each(dve):
                    link(dve.tensor_scalar(mb[:, :], vm[:, ds(g * (TG * NK), TG * NK)], 1.0, -NEG, ALU.subtract,
                                           ALU.mult), g)
                    dve.wait_ge(s_ps.sem, s_ps.upto(1, g))
                    for h in range(H):
                        last = dve.tensor_tensor(sm[:, TG * h:TG * (h + 1), :].rearrange("p t n -> p (t n)"),
                                                 k.ps[:, h, 0:TG * NK], mb[:, :], ALU.add)
                    last.then_inc(s_in.sem, 1)
                    dve.wait_ge(s_in.sem, s_in.upto(1, g))
                    for n in range(TOP // 8):
                        top = m8 if n else m0
                        dve.memset(pad[:, :], 0.0)
                        src = wk if n else sm
                        for i in range(W):
                            last = dve.max(top[:, i, :], src[:, i, :])
                        link(last, g)
                        dve.memset(pad[:, :], 0.0)
                        for i in range(W):
                            last = dve.match_replace(wk[:, i, :], top[:, i, :], src[:, i, :], TAKEN)
                        link(last, g)
                    dve.tensor_tensor(sm[:, :, :], sm[:, :, :], bc(m0[:, :, 0:1], [P, W, NK]),
                                      ALU.subtract).then_inc(shifted.sem, 1)
                    dve.wait_ge(ex.sem, ex.upto(1, g))
                    link(dve.scalar_tensor_tensor(sm[:, :, :], wk[:, :, :], TAKEN, sm[:, :, :], ALU.is_equal,
                                                  ALU.mult), g)
                    link(dve.tensor_reduce(rec[:, :], sm[:, :, :], X, ALU.add), g)
                    link(dve.reciprocal(rec[:, :], rec[:, :]), g)
                    r2 = rec[:, :].rearrange("p (h t) -> p h t", h=H)
                    link(dve.tensor_tensor(r2, r2, bc(tm[:, ds(g * TG, TG)].unsqueeze(1), [P, H, TG]), ALU.mult), g)
                    link(dve.tensor_scalar(rec[:, :], rec[:, :], 1.0 / H, None, ALU.mult), g)
                    link(dve.tensor_tensor(sm[:, :, :], sm[:, :, :], bc(rec[:, :].unsqueeze(2), [P, W, NK]),
                                           ALU.mult), g)
                    dve.tensor_reduce(av[:, :, :], sm[:, :, :].rearrange("p (h t) n -> p t n h", h=H), X,
                                      ALU.add).then_inc(mean.sem, 1)
                    dve.wait_ge(f_ps.sem, f_ps.upto(1, g))
                    for a in range(2):
                        last = dve.scalar_tensor_tensor(fs[:, 2 * a:2 * a + 2, :],
                                                        k.ps[:, a, :].rearrange("p (t c) -> p t c", t=2), mg[:, :],
                                                        bc(film[:, :].unsqueeze(1), [P, 2, 2 * P]), ALU.mult, ALU.add)
                    last.then_inc(f_in.sem, 1)
                    dve.wait_ge(f_in.sem, f_in.upto(1, g))
                    xw = wide[:, ds(g * TG, TG), :]
                    link(dve.tensor_tensor(xw, xw, fs[:, :, 0:P], ALU.mult), g)
                    link(dve.tensor_tensor(xw, xw, fs[:, :, P:2 * P], ALU.add), g)
                    while link.n < CH:
                        link(dve.tensor_copy(rec[:, 0:1], rec[:, 0:1]), g)
                    link.end_round()


def reverse_tokens(k, wide):
    nc = k.nc
    with ExitStack() as ctx:
        rev = k.sb("rv", [P, P], ctx=ctx)
        loaded = k.sig("dma_landed", 1)
        turned = k.sig("turned", 1, G)
        copied = k.sig("copied", 1, G)
        with nc.Block() as block:
            @block.sync
            def _(sp):
                sp.dma_start(rev[:, :], k.d["reversed"]).then_inc(loaded.sem, 16)

            @block.tensor
            def _(pe):
                pe.wait_ge(loaded.sem, loaded.upto(1))
                for _, r, u, g in rounds(pe):
                    if u == 0:
                        pe.wait_ge(copied.sem, copied.upto(0, r))
                    pe.matmul(k.ps[:, u, :], rev[:, :], wide[:, ds(g * TG, TG), :].rearrange("p t c -> p (t c)"),
                              start=True, stop=True).then_inc(turned.sem, 1)

            @block.scalar
            def _(act):
                for _, r, u, g in rounds(act):
                    act.wait_ge(turned.sem, turned.upto(1, r))
                    act.copy(wide[:, ds(g * TG, TG), :].rearrange("p t c -> p (t c)"), k.ps[:, u, :]
                             ).then_inc(copied.sem, 1)


def convolve(k, wide, conv_tensor):
    nc = k.nc
    CC = 16
    NC = P // CC
    with ExitStack() as ctx:
        hk = k.sb("cv_h", [P, 2, CC, P], ctx=ctx)
        loaded = [k.sig(f"taps_landed_{i}", 1, NC // 2) for i in range(2)]
        made = k.sig("turned", 1, NC)
        taken_a = k.sig("outs_taken_act", 1, NC)
        taken_d = k.sig("outs_taken_dve", 1, NC)
        with nc.Block() as block:
            @block.sync
            def _(sp):
                for c in range(NC):
                    if c >= 2:
                        sp.wait_ge(made.sem, made.upto(1, c - 2))
                    src = bass.AP(conv_tensor, c * CC * 2 * P, [[1, P], [2 * P, CC], [1, P]])
                    sp.dma_start(hk[:, c % 2], src).then_inc(loaded[c % 2].sem, 16)

            @block.tensor
            def _(pe):
                for c in range(NC):
                    pe.wait_ge(loaded[c % 2].sem, loaded[c % 2].upto(c // 2 + 1))
                    if c >= 2:
                        pe.wait_ge(taken_a.sem, taken_a.upto(1, c - 2))
                        pe.wait_ge(taken_d.sem, taken_d.upto(1, c - 2))
                    for i in range(CC):
                        mm = pe.matmul(k.ps[:, 2 * (c % 2) + i // 8, (i % 8) * B:(i % 8 + 1) * B], hk[:, c % 2, i, :],
                                       wide[:, :, c * CC + i], start=True, stop=True)
                    mm.then_inc(made.sem, 1)

            @block.scalar
            def _(act):
                for c in range(NC):
                    act.wait_ge(made.sem, made.upto(1, c))
                    act.copy(wide[:, :, c * CC:c * CC + 8].rearrange("p b d -> p d b"),
                             k.ps[:, 2 * (c % 2), :].rearrange("p (d b) -> p d b", b=B)).then_inc(taken_a.sem, 1)

            @block.vector
            def _(dve):
                for c in range(NC):
                    dve.wait_ge(made.sem, made.upto(1, c))
                    dve.tensor_copy(wide[:, :, c * CC + 8:c * CC + 16].rearrange("p b d -> p d b"),
                                    k.ps[:, 2 * (c % 2) + 1, :].rearrange("p (d b) -> p d b", b=B)
                                    ).then_inc(taken_d.sem, 1)


def modulate_out(k, ww, wide):
    nc = k.nc
    with ExitStack() as ctx:
        wf = k.sb("mo_wf", [P, 2 * P], ctx=ctx)
        brow = k.sb("mo_brow", [P, 2 * P], ctx=ctx)
        film = k.sb("mo_film", [P, 2 * P], ctx=ctx)
        mg = k.sb("mo_mg", [P, 1], ctx=ctx)
        cT = k.sb("mo_cT", [P, 2, TG * P], ctx=ctx)
        fs = k.sb("mo_fs", [P, TG, 2 * P], ctx=ctx)
        loaded = k.sig("dma_landed", 3)
        setup = k.sig("setup_step", 2)
        ready = k.sig("x_ready", 1, G)
        f_ps = k.sig("film_made", 1, G)
        f_in = k.sig("film_read", 1, G)
        chain = k.sig("dve_step", 3, G)
        with nc.Block() as block:
            @block.sync
            def _(sp):
                for to, of in ((wf[:, :], ww["film_out"]), (brow[:, :], ww["b_film_out"].partition_broadcast(P)),
                               (mg[:, :], ww["mod_gate"].partition_broadcast(P))):
                    sp.dma_start(to, of).then_inc(loaded.sem, 16)

            @block.gpsimd
            def _(pool):
                for _, r, u, g in rounds(pool):
                    if u == 0:
                        pool.wait_ge(f_ps.sem, f_ps.upto(0, r))
                    pool.tensor_copy(cT[:, u], k.nxT_all[:, ds(g * (TG * P), TG * P)]).then_inc(ready.sem, 1)

            @block.tensor
            def _(pe):
                pe.wait_ge(loaded.sem, loaded.upto(3))
                for _, r, u, g in rounds(pe):
                    pe.wait_ge(ready.sem, ready.upto(1, r))
                    if u == 0:
                        pe.wait_ge(f_in.sem, f_in.upto(0, r))
                    for t in range(TG):
                        mm = pe.matmul(k.ps[:, 2 * u + t // 2, (t % 2) * 2 * P:(t % 2 + 1) * 2 * P],
                                       cT[:, u, t * P:(t + 1) * P], wf[:, :], start=True, stop=True)
                    mm.then_inc(f_ps.sem, 1)

            @block.vector
            def _(dve):
                dve.wait_ge(loaded.sem, loaded.upto(3))
                first = Chain(dve, setup)
                film_rows(k, dve, first, mg[:, :], brow, film)
                link = Chain(dve, chain)
                for _, r, u, g in rounds(dve):
                    dve.wait_ge(f_ps.sem, f_ps.upto(1, r))
                    for a in range(2):
                        last = dve.scalar_tensor_tensor(fs[:, 2 * a:2 * a + 2, :],
                                                        k.ps[:, 2 * u + a, :].rearrange("p (t c) -> p t c", t=2),
                                                        mg[:, :], bc(film[:, :].unsqueeze(1), [P, 2, 2 * P]),
                                                        ALU.mult, ALU.add)
                    last.then_inc(f_in.sem, 1)
                    dve.wait_ge(f_in.sem, f_in.upto(1, r))
                    xw = wide[:, ds(g * TG, TG), :]
                    link(dve.tensor_tensor(xw, xw, fs[:, :, 0:P], ALU.mult), r)
                    link(dve.tensor_tensor(xw, xw, fs[:, :, P:2 * P], ALU.add), r)
                    link(dve.tensor_tensor(xw, xw, k.nx_all[:, ds(g * TG, TG), :], ALU.add), r)
                    link.end_round()


def add_scaled(k, src, gate_col):
    chain = k.sig("dve_step", 1)
    with k.nc.Block() as block:
        @block.vector
        def _(dve):
            link = Chain(dve, chain)
            flat = k.x_all[:, :, :].rearrange("p b c -> p (b c)")
            link(dve.scalar_tensor_tensor(flat, src[:, :, :].rearrange("p b c -> p (b c)"), gate_col, flat,
                                          ALU.mult, ALU.add))


def load_context(k):
    loaded = k.sig("dma_landed", 1)
    with k.nc.Block() as block:
        @block.sync
        def _(sp):
            sp.dma_start(k.ctxT[:, :], k.d["ctxT"]).then_inc(loaded.sem, 16)
            sp.wait_ge(loaded.sem, loaded.upto(1))


def store_output(k, out):
    stored = k.sig("dma_stored", 4)
    with k.nc.Block() as block:
        @block.sync
        def _(sp):
            for q in range(4):
                s = slice(16 * q, 16 * q + 16)
                sp.dma_start(out[s].rearrange("b s c -> s b c"), k.x_all[:, s, :]).then_inc(stored.sem, 16)
            sp.wait_ge(stored.sem, stored.upto(4))


def build(nc, d, out, stages=range(1, 9)):
    conv = nc.dram_tensor("conv_rows", [P, 2 * P], F32, kind="Internal")
    with ExitStack() as ctx:
        k = Kernel(nc, d, ctx)
        k.rank_i = k.sb("rank_i", [P, 8], I32)
        tgc = [k.tg[:, i:i + 1] for i in range(8)]

        def att(name):
            return {"w": d[name + "_w"], "bcol": d[name + "_bcol"], "rows": d[name + "_rows"]}

        def exp_w(name, up):
            r = {"w1": d[name + "_w1"], "w2": d[name + "_w2"], "bcol": d[name + "_bcol"], "brow": d[name + "_brow"]}
            if up:
                r["w3"] = d[name + "_w3"]
            return r

        prime_signals(k)
        load_inputs(k)
        if 3 in stages:
            ssm_kernel(k, d, conv.ap())
        k.ctxT = k.sb("ctxT", [CK, B * NK])
        load_context(k)

        if 1 in stages:
            layer_norm(k, k.x_all, k.nx_all, P)
            transpose_rows(k)
            attention(k, 16, 1, NK, 8 ** -0.5, att("a0"), tgc[0], clip=10000.0)
        if 2 in stages:
            with ExitStack() as inner:
                gate_arrays(k, inner)
                layer_norm(k, k.x_all, k.nx_all, P)
                with ExitStack() as inmost:
                    h_all = k.sb("h_all", [P, B, 64], ctx=inmost)
                    transpose_rows(k, (d["m0_rw1"], d["m0_rb1"], 64, h_all))
                    layer_norm(k, h_all, h_all, 64)
                    router_logits(k, h_all, 64, {n: d["m0_r_" + n] for n in ("w2", "b2", "g", "b")})
                top_two_gates(k, tgc[4])
                attention(k, 16, 8, P, 8 ** -0.5, att("m0"), None, gated=True)
        if 3 in stages:
            layer_norm(k, k.x_all, k.nx_all, P)
            transpose_rows(k)
            with ExitStack() as inner:
                wide = k.sb("wide", [P, B, P], ctx=inner)
                layer_norm(k, k.nx_all, wide, P)
                affine(k, wide, d["g_norm_in"], d["b_norm_in"])
                sparse_attention(k, d, wide)
                reverse_tokens(k, wide)
                convolve(k, wide, conv)
                modulate_out(k, d, wide)
                layer_norm(k, wide, k.nx_all, P)
                affine(k, k.nx_all, d["g_ffn_ln"], d["b_ffn_ln"])
                transpose_rows(k)
                experts(k, 1, 4, ACT.Gelu, exp_w("mlp", False), wide, up=False, gate_col=k.cols[:, 1:2], gated=False)
                layer_norm(k, wide, k.nx_all, P)
                affine(k, k.nx_all, d["g_norm_out"], d["b_norm_out"])
                add_scaled(k, k.nx_all, tgc[1])
        if 4 in stages:
            with ExitStack() as inner:
                gate_arrays(k, inner)
                layer_norm(k, k.x_all, k.nx_all, P)
                transpose_rows(k, (d["m1_rw"], d["m1_rb"], 8, k.logits))
                top_two_gates(k, tgc[5], shared=2)
                experts(k, 5, 1, ACT.Silu, exp_w("m1", True), k.x_all, up=True, pair=True)
        if 5 in stages:
            layer_norm(k, k.x_all, k.nx_all, P)
            transpose_rows(k)
            attention(k, 2, 8, NK, 64 ** -0.5, att("a2"), tgc[2])
        if 6 in stages:
            with ExitStack() as inner:
                gate_arrays(k, inner)
                layer_norm(k, k.x_all, k.nx_all, P)
                transpose_rows(k, (d["m2_rw"], d["zero_row"], 8, k.logits))
                top_two_gates(k, tgc[6], plus=1e-8)
                experts(k, 8, 2, ACT.Silu, exp_w("m2", True), k.x_all, up=True)
        if 7 in stages:
            layer_norm(k, k.x_all, k.nx_all, P)
            transpose_rows(k)
            attention(k, 2, 8, NK, 64 ** -0.5, att("a3"), tgc[3])
        if 8 in stages:
            with ExitStack() as inner:
                gate_arrays(k, inner)
                layer_norm(k, k.x_all, k.nx_all, P)
                transpose_rows(k, (d["m3_rw"], d["zero_row"], 8, k.logits))
                top_two_gates(k, tgc[7], least=1e-9, capacity=2 * B * P // 8)
                experts(k, 8, 4, ACT.Gelu, exp_w("m3", False), k.x_all, up=False)
        store_output(k, out)


def layouts(i):
    import numpy as np
    a = {n: np.asarray(v) for n, v in i.items()}
    f = np.float32
    d = {}
    d["x"] = a["x"]
    d["ctxT"] = np.transpose(a["ctx_768"], (2, 0, 1)).reshape(CK, B * NK)
    d["ident"] = np.eye(P, dtype=f)
    d["reversed"] = np.eye(P, dtype=f)[::-1]
    d["ones"] = np.ones((P, P), f)
    d["before"] = np.triu(np.ones((P, P), f), 1)
    d["zero_row"] = np.zeros((8,), f)
    cols = np.zeros((P, 16), f)
    cols[:, 0] = EPS
    cols[:, 1] = 1.0
    for m in range(4):
        cols[:, 2 + m] = (np.arange(P) // 8) % 4 == m
    d["cols"] = cols
    d["g_rows"] = np.concatenate([a["g_xattn"], a["g_ffn"]])
    d["text_mask"] = a["mask_BxS_bf1"].view(np.uint8).T
    d["vision_mask"] = a["mask_BxS2_bf1"].view(np.uint8).reshape(-1)

    def attn(name, wq, wk, wv, wo, bq=None, bk=None, bv=None, bo=None):
        E = wq.shape[0]
        w = np.zeros((E, P, 4, P), f)
        for n, m in enumerate((wq, wk, wv, wo)):
            w[:, :m.shape[1], n, :] = m
        d[name + "_w"] = w
        bcol = np.zeros((E, P, 2), f)
        rows = np.zeros((E, 2, P), f)
        for to, b in ((bcol[:, :, 0], bq), (bcol[:, :, 1], bk), (rows[:, 0], bv)):
            if b is not None:
                to[:] = b
        if bo is not None:
            rows[:len(bo), 1] = bo
        d[name + "_bcol"], d[name + "_rows"] = bcol, rows

    L = "L0_xattn_"
    attn("a0", *(a[L + n][None] for n in ("Wq", "Wk", "Wv", "Wo", "bq", "bk", "bv", "bo")))
    L = "L0_ffn_"
    attn("m0", *(np.transpose(a[L + n], (0, 2, 1)) for n in ("qW", "kW", "vW", "oW")),
         *(a[L + n] for n in ("qb", "kb", "vb", "ob")))

    def cut(w):
        return np.transpose(w.reshape(w.shape[0], 8, P), (1, 0, 2))

    attn("a2", cut(a["L2_xattn_Wq"]), cut(a["L2_xattn_Wk"]), cut(a["L2_xattn_Wv"]),
         a["L2_xattn_Wo"].reshape(8, P, P), bo=a["L2_xattn_bo"][None])
    kv = a["L3_xattn_w_kv"]
    attn("a3", cut(a["L3_xattn_w_q"]), cut(kv[:, :1024]), cut(kv[:, 1024:]), a["L3_xattn_w_out"].reshape(8, P, P),
         bo=a["L3_xattn_b_out"][None])

    L = "L0_ffn_"
    d["m0_rw1"], d["m0_rb1"] = a[L + "rW1"].T, a[L + "rb1"]
    d["m0_r_w2"], d["m0_r_b2"], d["m0_r_g"], d["m0_r_b"] = a[L + "rW2"].T, a[L + "rb2"], a[L + "ln_g"], a[L + "ln_b"]

    L = "L1_xattn_"
    w = np.zeros((P, 3, P), f)
    for n, m in enumerate(("Wq", "Wk", "Wv")):
        w[:a[L + m].shape[0], n] = a[L + m]
    d["sa_w"] = w
    d["film_in"], d["b_film_in"] = a[L + "W_film_in"], a[L + "b_film_in"]
    d["film_out"], d["b_film_out"] = a[L + "W_film_out"], a[L + "b_film_out"]
    d["mod_gate"] = a[L + "mod_gate"].reshape(1)
    d["g_norm_in"], d["b_norm_in"] = a[L + "g_norm_in"], a[L + "b_norm_in"]
    d["g_ffn_ln"], d["b_ffn_ln"] = a[L + "g_ffn"], a[L + "b_ffn"]
    d["g_norm_out"], d["b_norm_out"] = a[L + "g_norm_out"], a[L + "b_norm_out"]
    d["ssm"] = np.concatenate([a[L + n] for n in ("A_re", "A_im", "C_re", "C_im")]
                              + [a[L + "log_dt"][:, None], a[L + "D_skip"][:, None]], axis=1)

    def moe(name, w1, w2, w3=None, b1=None, b3=None, b2=None):
        E, _, M = w1.shape
        MC = M // P
        d[name + "_w1"] = w1
        d[name + "_w2"] = np.transpose(w2.reshape(E, MC, P, P), (0, 2, 1, 3))
        if w3 is not None:
            d[name + "_w3"] = w3
        bcol = np.zeros((E, P, 2 * MC), f)
        for n, b in enumerate((b1, b3)):
            if b is not None:
                bcol[:, :, n * MC:(n + 1) * MC] = np.transpose(b.reshape(E, MC, P), (0, 2, 1))
        d[name + "_bcol"] = bcol
        d[name + "_brow"] = b2 if b2 is not None else np.zeros((E, P), f)

    moe("mlp", a[L + "W1"][None], a[L + "W2"][None], b1=a[L + "b1"][None], b2=a[L + "b2"][None])
    L = "L1_ffn_"
    w1, w3, w2 = (np.concatenate([a[L + "routed_" + n], a[L + "shared_" + n]]) for n in ("w1", "w3", "w2"))

    def two(w):
        return np.transpose(w.reshape(5, 2, P, 64), (0, 2, 1, 3)).reshape(5, P, P)

    moe("m1", two(w1), w2.reshape(5, P, P), two(w3))
    d["m1_rw"], d["m1_rb"] = a[L + "router_w"], a[L + "router_b"]
    L = "L2_ffn_"
    moe("m2", a[L + "W_gate"], a[L + "W_out"], a[L + "W_up"], a[L + "b_gate"], a[L + "b_up"], a[L + "b_out"])
    d["m2_rw"] = a[L + "W_router"]
    L = "L3_ffn_"
    moe("m3", a[L + "w_gate"], a[L + "w_down"])
    d["m3_rw"] = a[L + "wg"]
    return {n: np.ascontiguousarray(v) for n, v in d.items()}


STAGES = range(1, 9)


def kernel(**inputs):
    import concourse.bacc as bacc
    from concourse.bass_utils import run_bass_kernel_spmd as run

    nc = bacc.Bacc("TRN2", target_bir_lowering=False, num_devices=1)
    arrays, dram = {}, {}
    for name, v in layouts(inputs).items():
        arrays["in_" + name] = v
        dram[name] = nc.dram_tensor("in_" + name, v.shape, mybir.dt.from_np(v.dtype), kind="ExternalInput").ap()
    out = nc.dram_tensor("out_0", (B, P, P), F32, kind="ExternalOutput").ap()
    build(nc, dram, out, STAGES)
    return run(nc, [arrays], core_ids=[0]).results[0]["out_0"]
```

```python
from contextlib import ExitStack

import concourse.bass as bass
from concourse import mybir

ALU = mybir.AluOpType
ACT = mybir.ActivationFunctionType
F32 = mybir.dt.float32
I32 = mybir.dt.int32
U8 = mybir.dt.uint8
X = mybir.AxisListType.X
ds = bass.ds

P = 128
B = 64
NK = 120
CK = 96
TG = 4
G = B // TG
EPS = 1e-5
NEG = -3e38
TAKEN = -3.3e38
MAGIC = 12582912.0


SIGNALS = """
    dma_landed act_step dve_step centred squared squares_summed
    rooted staged turned copied stored routed
    routes_taken x_ready scores_made max_found exp_done probs_turned
    outputs_made sums_inverted outputs_scaled outputs_turned y_made y_added
    gates_copied scores_clipped ones_column_set h1_made h3_made h1_activated
    hidden_in_sbuf chosen shifted counted dma_stored angles_ready
    sines_done kernel_ready setup_step scores_masked probs_averaged c_made
    c_in_sbuf film_made film_read outs_taken_act outs_taken_dve pool_step
    weights_copied k_masked_dve k_masked_pool outputs_copied outputs_turned_back
    probsT_in_sbuf outputsT_in_sbuf q_made k_made v_made q_in_sbuf k_in_sbuf v_in_sbuf taps_landed_0 taps_landed_1
""".split()
FROM_DMA = ("dma_landed", "dma_stored", "taps_landed_0", "taps_landed_1")


class Signal:

    def __init__(self, sem, step=1):
        self.sem, self.step, self.base, self.per = sem, step, 1, 0

    def stage(self, per, rounds=1):
        self.base += self.per
        self.each, self.per = per, per * rounds
        return self

    def upto(self, n, r=0):
        return (self.base + n) * self.step + r * (self.each * self.step)


class Chain:

    def __init__(self, eng, steps):
        self.eng, self.steps, self.n = eng, steps, 0

    def __call__(self, instruction, r=0):
        self.n += 1
        instruction.then_inc(self.steps.sem, 1)
        self.eng.wait_ge(self.steps.sem, self.steps.upto(self.n, r))

    def end_round(self):
        assert self.n == self.steps.each, (self.n, self.steps.each)
        self.n = 0


class Kernel:
    def __init__(self, nc, dram, ctx):
        self.nc, self.d, self.ctx = nc, dram, ctx
        self.events = {n: Signal(ctx.enter_context(nc.semaphore(n)), 16 if n in FROM_DMA else 1) for n in SIGNALS}
        self.names = {}
        sb = self.sb
        self.x_all = sb("x_all", [P, B, P])
        self.nx_all = sb("nx_all", [P, B, P])
        self.nxT_all = sb("nxT_all", [P, B * P])
        self.ident = sb("ident", [P, P])
        self.ones = sb("ones", [P, P])
        self.cols = sb("cols", [P, 32])
        self.rank = sb("rank", [P, 8])
        self.tg = sb("tg", [P, 8])
        self.ps = ctx.enter_context(nc.psum_tensor("ps", [P, 8, 512], F32))

    def sb(self, name, shape, dt=F32, ctx=None):
        self.names[name] = self.names.get(name, 0) + 1
        name = f"{name}_{self.names[name]}" if self.names[name] > 1 else name
        return (ctx or self.ctx).enter_context(self.nc.sbuf_tensor(name, shape, dt))

    def sig(self, name, per, rounds=1, step=1):
        return self.events[name].stage(per, rounds)


def bc(ap, shape):
    return ap.to_broadcast(shape)


def rounds(eng, outer=1):
    if outer == 1:
        with eng.Fori(0, G // 2) as i:
            for u in range(2):
                yield 0, 2 * i + u, u, 2 * i + u
    else:
        with eng.Fori(0, outer) as e:
            with eng.Fori(0, G // 2) as i:
                for u in range(2):
                    yield e, e * G + 2 * i + u, u, 2 * i + u


def gate_arrays(k, ctx):
    k.logits = k.sb("logits", [P, B, 8], ctx=ctx)
    k.gates = k.sb("gates", [P, 10, B], ctx=ctx)


def prime_signals(k):
    with k.nc.Block() as block:
        @block.sync
        def _(sp):
            for s in k.events.values():
                sp.sem_inc(s.sem, s.step)


def load_inputs(k):
    nc, d = k.nc, k.d
    n = 8
    landed = k.sig("dma_landed", n)
    step = k.sig("act_step", 1)
    made = k.sig("pool_step", 1)
    with nc.Block() as block:
        @block.sync
        def _(sp):
            for q in range(4):
                s = slice(16 * q, 16 * q + 16)
                sp.dma_start(k.x_all[:, s, :], d["x"][s].rearrange("b s c -> s b c")).then_inc(landed.sem, 16)
            sp.dma_start(k.ident[:, :], d["ident"]).then_inc(landed.sem, 16)
            sp.dma_start(k.ones[:, :], d["ones"]).then_inc(landed.sem, 16)
            sp.dma_start(k.cols[:, :], d["cols"]).then_inc(landed.sem, 16)
            sp.dma_start(k.tg[:, :], d["g_rows"].partition_broadcast(P)).then_inc(landed.sem, 16)

        @block.gpsimd
        def _(pool):
            pool.iota(k.rank_i[:, :], [[-1, 8]], base=8, channel_multiplier=0).then_inc(made.sem, 1)
            pool.wait_ge(made.sem, made.upto(1))
            pool.tensor_copy(k.rank[:, :], k.rank_i[:, :])

        @block.scalar
        def _(act):
            act.wait_ge(landed.sem, landed.upto(n))
            act.activation(k.tg[:, :], k.tg[:, :], ACT.Tanh).then_inc(step.sem, 1)
            act.wait_ge(step.sem, step.upto(1))


def layer_norm(k, src, dst, n):
    nc = k.nc
    Q = 4
    BQ = B // Q
    with ExitStack() as ctx:
        st = [k.sb(f"ln_{i}", [P, B], ctx=ctx) for i in range(3)]
        sq = k.sb("ln_sq", [P, 2, BQ, n], ctx=ctx)
        total, mean, rstd = st
        chain = k.sig("dve_step", 4 + Q)
        centred = k.sig("centred", Q)
        squared = k.sig("squared", Q)
        summed = k.sig("squares_summed", Q)
        rooted = k.sig("rooted", 1)
        with nc.Block() as block:
            @block.vector
            def _(dve):
                link = Chain(dve, chain)
                link(dve.tensor_reduce(total[:, :], src[:, :, :n], X, ALU.add))
                link(dve.tensor_scalar(mean[:, :], total[:, :], 1.0 / n, None, ALU.mult))
                for q in range(Q):
                    s = slice(BQ * q, BQ * (q + 1))
                    dve.tensor_tensor(dst[:, s, :n], src[:, s, :n], bc(mean[:, s].unsqueeze(2), [P, BQ, n]),
                                      ALU.subtract).then_inc(centred.sem, 1)
                for q in range(Q):
                    dve.wait_ge(squared.sem, squared.upto(q + 1))
                    dve.tensor_reduce(total[:, BQ * q:BQ * (q + 1)], sq[:, q % 2], X, ALU.add).then_inc(summed.sem, 1)
                dve.wait_ge(rooted.sem, rooted.upto(1))
                link(dve.reciprocal(rstd[:, :], mean[:, :]))
                for q in range(Q):
                    s = slice(BQ * q, BQ * (q + 1))
                    link(dve.tensor_tensor(dst[:, s, :n], dst[:, s, :n], bc(rstd[:, s].unsqueeze(2), [P, BQ, n]),
                                           ALU.mult))
                link(dve.tensor_copy(total[:, 0:1], rstd[:, 0:1]))

            @block.scalar
            def _(act):
                for q in range(Q):
                    act.wait_ge(centred.sem, centred.upto(q + 1))
                    if q >= 2:
                        act.wait_ge(summed.sem, summed.upto(q - 1))
                    act.activation(sq[:, q % 2], dst[:, BQ * q:BQ * (q + 1), :n], ACT.Square).then_inc(squared.sem, 1)
                act.wait_ge(summed.sem, summed.upto(Q))
                act.activation(mean[:, :], total[:, :], ACT.Sqrt, bias=k.cols[:, 0:1],
                               scale=1.0 / n).then_inc(rooted.sem, 1)


def transpose_rows(k, router=None):
    nc = k.nc
    with ExitStack() as ctx:
        rows = k.sb("tr_rows", [P, 2, TG, P], ctx=ctx)
        cols = k.sb("tr_cols", [P, 2, TG * P], ctx=ctx)
        staged = k.sig("staged", 1, G)
        turned = k.sig("turned", 1, G)
        copied = k.sig("copied", 1, G)
        stored = k.sig("stored", 1, G)
        if router:
            routed = k.sig("routed", 1, G)
            taken = k.sig("routes_taken", 1, G)
            loaded = k.sig("dma_landed", 2)
            w_dram, b_dram, W, target = router
            w = k.sb("tr_w", [P, W], ctx=ctx)
            b = k.sb("tr_b", [P, W], ctx=ctx)
        with nc.Block() as block:
            if router:
                @block.sync
                def _(sp):
                    sp.dma_start(w[:, :], w_dram).then_inc(loaded.sem, 16)
                    sp.dma_start(b[:, :], b_dram.partition_broadcast(P)).then_inc(loaded.sem, 16)

            @block.gpsimd
            def _(pool):
                for _, r, u, g in rounds(pool):
                    if u == 0:
                        pool.wait_ge(turned.sem, turned.upto(0, r))
                    pool.tensor_copy(rows[:, u], k.nx_all[:, ds(g * TG, TG), :]).then_inc(staged.sem, 1)

            @block.tensor
            def _(pe):
                if router:
                    pe.wait_ge(loaded.sem, loaded.upto(2))
                for _, r, u, g in rounds(pe):
                    pe.wait_ge(staged.sem, staged.upto(1, r))
                    if u == 0:
                        pe.wait_ge(copied.sem, copied.upto(0, r))
                    for t in range(TG):
                        mm = pe.transpose(k.ps[:, u, t * P:(t + 1) * P], rows[:, u, t, :], k.ident[:, :])
                    mm.then_inc(turned.sem, 1)
                    if router:
                        pe.wait_ge(copied.sem, copied.upto(1, r))
                        if u == 0:
                            pe.wait_ge(taken.sem, taken.upto(0, r))
                        for t in range(TG):
                            mm = pe.matmul(k.ps[:, 2 + u, t * W:(t + 1) * W], cols[:, u, t * P:(t + 1) * P], w[:, :],
                                           start=True, stop=True)
                        mm.then_inc(routed.sem, 1)

            @block.scalar
            def _(act):
                for _, r, u, g in rounds(act):
                    act.wait_ge(turned.sem, turned.upto(1, r))
                    if u == 0:
                        act.wait_ge(stored.sem, stored.upto(0, r))
                        if router:
                            act.wait_ge(routed.sem, routed.upto(0, r))
                    act.copy(cols[:, u], k.ps[:, u, :]).then_inc(copied.sem, 1)

            @block.vector
            def _(dve):
                if router:
                    dve.wait_ge(loaded.sem, loaded.upto(2))
                for _, r, u, g in rounds(dve):
                    dve.wait_ge(copied.sem, copied.upto(1, r))
                    dve.tensor_copy(k.nxT_all[:, ds(g * (TG * P), TG * P)], cols[:, u]).then_inc(stored.sem, 1)
                    if router:
                        dve.wait_ge(routed.sem, routed.upto(1, r))
                        dve.tensor_tensor(target[:, ds(g * TG, TG), :],
                                          k.ps[:, 2 + u, 0:TG * W].rearrange("p (t w) -> p t w", w=W),
                                          bc(b[:, :].unsqueeze(1), [P, TG, W]), ALU.add).then_inc(taken.sem, 1)


def attention(k, heads, E, nk, scale, weights, gate_col, clip=None, gated=False):
    nc = k.nc
    dh = P // heads
    narrow = dh < 32
    NS = TG * heads // 4
    per_norm = 4 if narrow else 1
    NN = NS // per_norm
    nh = 16 if narrow else TG
    self_attn = nk == P
    R = E * G
    with ExitStack() as ctx:
        xT = k.sb("at_xT", [P, 2, TG * P], ctx=ctx)
        kv = xT if self_attn else k.sb("at_kv", [P, 2, TG * nk], ctx=ctx)
        w = k.sb("at_w", [P, 4, P], ctx=ctx)
        bcol = k.sb("at_bcol", [P, 2], ctx=ctx)
        vrow = k.sb("at_vrow", [P, P], ctx=ctx)
        orow = k.sb("at_orow", [1, P], ctx=ctx)
        q_sb = k.sb("at_q", [P, TG * P], ctx=ctx)
        NM = 4 if narrow else 1
        k_sb = k.sb("at_k", [P, NM, TG, nk], ctx=ctx)
        v_sb = k.sb("at_v", [P, TG, heads, dh + 1], ctx=ctx)
        clipped = k.sb("at_clip", [P, 2, 4 * nk], ctx=ctx) if clip else None
        negmax = k.sb("at_max", [P, 2, 4], ctx=ctx)
        probs = k.sb("at_p", [P, 2, 4, nk], ctx=ctx)
        pT = k.sb("at_pT", [P, 2, 4 * P], ctx=ctx)
        rec = k.sb("at_rec", [P, nh], ctx=ctx)
        o_sb = k.sb("at_o", [P, TG, P], ctx=ctx)
        oT = k.sb("at_oT", [P, TG * P], ctx=ctx)
        gcur = k.sb("at_g", [P, TG], ctx=ctx)

        loaded = k.sig("dma_landed", 4, E)
        ready = k.sig("x_ready", 1, R)
        q_ps, k_ps, v_ps = (k.sig(f"{n}_made", 1, R) for n in "qkv")
        q_in, k_in, v_in = (k.sig(f"{n}_in_sbuf", 1, R) for n in "qkv")
        s_ps = k.sig("scores_made", NS, R)
        mx = k.sig("max_found", NS, R)
        ex = k.sig("exp_done", NS, R)
        t_ps = k.sig("probs_turned", NS, R)
        t_in = k.sig("probsT_in_sbuf", NS, R)
        pv = k.sig("outputs_made", NS, R)
        rc = k.sig("sums_inverted", NN, R)
        nrm = k.sig("outputs_scaled", NN, R)
        ot_ps = k.sig("outputs_turned", 1, R)
        ot_in = k.sig("outputsT_in_sbuf", 1, R)
        y_ps = k.sig("y_made", 1, R)
        added = k.sig("y_added", 1, R)
        gsel = k.sig("gates_copied", 1, R) if gated else None
        clp = k.sig("scores_clipped", NS, R) if clip else None
        onesc = k.sig("ones_column_set", 1)
        A0, T0, PQ, PK, PO, PY = 0, 2, 4, 5, 6, 7

        with nc.Block() as block:
            @block.sync
            def _(sp):
                with sp.Fori(0, E) as e:
                    sp.wait_ge(added.sem, added.upto(0, e * G))
                    sp.dma_start(w[:, :, :], weights["w"][ds(e, 1)].rearrange("a p n c -> p (a n) c")
                                 ).then_inc(loaded.sem, 16)
                    sp.dma_start(bcol[:, :], weights["bcol"][ds(e, 1)].rearrange("a p n -> p (a n)")
                                 ).then_inc(loaded.sem, 16)
                    sp.dma_start(vrow[:, :], weights["rows"][ds(e, 1), 0, :].rearrange("a c -> (a c)")
                                 .partition_broadcast(P)).then_inc(loaded.sem, 16)
                    sp.dma_start(orow[:, :], weights["rows"][ds(e, 1), 1, :]).then_inc(loaded.sem, 16)

            @block.gpsimd
            def _(pool):
                for e, r, u, g in rounds(pool, E):
                    if u == 0:
                        pool.wait_ge(v_ps.sem, v_ps.upto(0, r))
                    last = pool.tensor_copy(xT[:, u], k.nxT_all[:, ds(g * (TG * P), TG * P)])
                    if not self_attn:
                        last = pool.tensor_copy(kv[0:CK, u], k.ctxT[:, ds(g * (TG * nk), TG * nk)])
                    last.then_inc(ready.sem, 1)

            @block.tensor
            def _(pe):
                ck = P if self_attn else CK

                def scores(r, s):
                    if s >= 2:
                        free = clp or ex
                        pe.wait_ge(free.sem, free.upto(s - 1, r))
                    elif s == 0:
                        free = clp or ex
                        pe.wait_ge(free.sem, free.upto(0, r))
                    bank = k.ps[:, A0 + s % 2, 0:4 * nk]
                    if narrow:
                        t, rg = divmod(s, 4)
                        rows = slice(32 * rg, 32 * rg + 32)
                        mm = pe.matmul(bank.rearrange("p (h n) -> p h n", n=nk), q_sb[rows, t * P:(t + 1) * P],
                                       k_sb[rows, :, t, :], start=True, stop=True)
                    else:
                        rows = slice(dh * s, dh * s + dh)
                        for t in range(TG):
                            mm = pe.matmul(k.ps[:, A0 + s % 2, t * nk:(t + 1) * nk], q_sb[rows, t * P:(t + 1) * P],
                                           k_sb[rows, 0, t, :], start=True, stop=True)
                    mm.then_inc(s_ps.sem, 1)

                def turn(r, s):
                    pe.wait_ge(ex.sem, ex.upto(s + 1, r))
                    pe.wait_ge(t_in.sem, t_in.upto(max(s - 1, 0), r))
                    for j in range(4):
                        mm = pe.transpose(k.ps[0:nk, T0 + s % 2, j * P:(j + 1) * P], probs[:, s % 2, j, :],
                                          k.ident[:, :])
                    mm.then_inc(t_ps.sem, 1)

                def outputs(r, s):
                    pe.wait_ge(t_in.sem, t_in.upto(s + 1, r))
                    if s == 0:
                        pe.wait_ge(v_in.sem, v_in.upto(1, r))
                    if s % per_norm == 0:
                        pe.wait_ge(nrm.sem, nrm.upto(s // per_norm, r))
                    for j in range(4):
                        if narrow:
                            t, h = s // 4, 4 * (s % 4) + j
                            slot = h
                        else:
                            t, h = j, s
                            slot = t
                        mm = pe.matmul(k.ps[:, PO, slot * (dh + 1):(slot + 1) * (dh + 1)],
                                       pT[0:nk, s % 2, j * P:(j + 1) * P], v_sb[0:nk, t, h, :], start=True, stop=True)
                    mm.then_inc(pv.sem, 1)

                for e, r, u, g in rounds(pe, E):
                    if u == 0:
                        pe.wait_ge(loaded.sem, loaded.upto(4, e))
                    pe.wait_ge(ready.sem, ready.upto(1, r))
                    pe.wait_ge(ot_in.sem, ot_in.upto(0, r))
                    pe.matmul(k.ps[:, PQ, :], w[:, 0, :], xT[:, u], start=True, stop=True).then_inc(q_ps.sem, 1)
                    pe.wait_ge(k_in.sem, k_in.upto(0, r))
                    pe.matmul(k.ps[:, PK, 0:TG * nk], w[0:ck, 1, :], kv[0:ck, u], start=True,
                              stop=True).then_inc(k_ps.sem, 1)
                    pe.wait_ge(added.sem, added.upto(0, r))
                    for t in range(TG):
                        mm = pe.matmul(k.ps[0:nk, PY, t * P:(t + 1) * P], kv[0:ck, u, t * nk:(t + 1) * nk],
                                       w[0:ck, 2, :], start=True, stop=True)
                    mm.then_inc(v_ps.sem, 1)
                    pe.wait_ge(q_in.sem, q_in.upto(1, r))
                    pe.wait_ge(k_in.sem, k_in.upto(1, r))
                    for s in range(NS + 2):
                        if s < NS:
                            scores(r, s)
                        if 1 <= s <= NS:
                            turn(r, s - 1)
                        if s >= 2:
                            outputs(r, s - 2)
                    pe.wait_ge(nrm.sem, nrm.upto(NN, r))
                    for t in range(TG):
                        mm = pe.transpose(k.ps[:, PQ, t * P:(t + 1) * P], o_sb[:, t, :], k.ident[:, :])
                    mm.then_inc(ot_ps.sem, 1)
                    pe.wait_ge(ot_in.sem, ot_in.upto(1, r))
                    for t in range(TG):
                        y = k.ps[:, PY, t * P:(t + 1) * P]
                        pe.matmul(y, k.ones[0:1, :], orow[0:1, :], start=True, stop=False)
                        mm = pe.matmul(y, oT[:, t * P:(t + 1) * P], w[:, 3, :], start=False, stop=True)
                    mm.then_inc(y_ps.sem, 1)

            @block.scalar
            def _(act):
                for e, r, u, g in rounds(act, E):
                    for s in range(NS):
                        act.wait_ge(mx.sem, mx.upto(s + 1, r))
                        act.wait_ge(t_ps.sem, t_ps.upto(max(s - 1, 0), r))
                        for j in range(4):
                            src = clipped[:, s % 2, j * nk:(j + 1) * nk] if clip else \
                                k.ps[:, A0 + s % 2, j * nk:(j + 1) * nk]
                            last = act.activation(probs[:, s % 2, j, :], src, ACT.Exp, bias=negmax[:, s % 2, j:j + 1])
                        last.then_inc(ex.sem, 1)
                    act.wait_ge(ot_ps.sem, ot_ps.upto(1, r))
                    act.copy(oT[:, :], k.ps[:, PQ, :]).then_inc(ot_in.sem, 1)

            @block.vector
            def _(dve):
                dve.memset(v_sb[:, :, :, dh:dh + 1], 1.0).then_inc(onesc.sem, 1)
                dve.wait_ge(onesc.sem, onesc.upto(1))

                def top(r, s):
                    dve.wait_ge(s_ps.sem, s_ps.upto(s + 1, r))
                    dve.wait_ge(ex.sem, ex.upto(max(s - 1, 0), r))
                    src = k.ps[:, A0 + s % 2, 0:4 * nk]
                    if clip:
                        dve.tensor_scalar(clipped[:, s % 2], src, clip, -clip, ALU.min, ALU.max).then_inc(clp.sem, 1)
                        dve.wait_ge(clp.sem, clp.upto(s + 1, r))
                        src = clipped[:, s % 2]
                    dve.tensor_reduce(negmax[:, s % 2], src.rearrange("p (h n) -> p h n", n=nk), X, ALU.max,
                                      negate=True).then_inc(mx.sem, 1)

                def fetch(r, s):
                    dve.wait_ge(t_ps.sem, t_ps.upto(s + 1, r))
                    dve.wait_ge(pv.sem, pv.upto(max(s - 1, 0), r))
                    dve.tensor_copy(pT[0:nk, s % 2, :], k.ps[0:nk, T0 + s % 2, :]).then_inc(t_in.sem, 1)

                def scale_outputs(r, s):
                    n = s // per_norm
                    dve.wait_ge(pv.sem, pv.upto(s + 1, r))
                    o = k.ps[:, PO, 0:nh * (dh + 1)].rearrange("p (h c) -> p h c", c=dh + 1)
                    dve.reciprocal(rec[:, :], o[:, :, dh]).then_inc(rc.sem, 1)
                    dve.wait_ge(rc.sem, rc.upto(n + 1, r))
                    out = o_sb[:, n, :].rearrange("p (h c) -> p h c", c=dh) if narrow \
                        else o_sb[:, :, n * dh:(n + 1) * dh]
                    dve.tensor_tensor(out, o[:, :, 0:dh], bc(rec[:, :].unsqueeze(2), [P, nh, dh]),
                                      ALU.mult).then_inc(nrm.sem, 1)

                for e, r, u, g in rounds(dve, E):
                    if u == 0:
                        dve.wait_ge(loaded.sem, loaded.upto(4, e))
                    dve.wait_ge(q_ps.sem, q_ps.upto(1, r))
                    dve.tensor_scalar(q_sb[:, :], k.ps[:, PQ, :], bcol[:, 0:1], scale, ALU.add,
                                      ALU.mult).then_inc(q_in.sem, 1)
                    dve.wait_ge(k_ps.sem, k_ps.upto(1, r))
                    for m in range(NM):
                        mask = k.cols[:, 2 + m:3 + m] if narrow else k.cols[:, 1:2]
                        last = dve.tensor_scalar(k_sb[:, m].rearrange("p t n -> p (t n)"), k.ps[:, PK, 0:TG * nk],
                                                 bcol[:, 1:2], mask, ALU.add, ALU.mult)
                    last.then_inc(k_in.sem, 1)
                    dve.wait_ge(v_ps.sem, v_ps.upto(1, r))
                    for t in range(TG):
                        last = dve.tensor_tensor(v_sb[0:nk, t, :, 0:dh],
                                                 k.ps[0:nk, PY, t * P:(t + 1) * P].rearrange("p (h c) -> p h c", c=dh),
                                                 vrow[0:nk, :].rearrange("p (h c) -> p h c", c=dh), ALU.add)
                    last.then_inc(v_in.sem, 1)
                    if gated:
                        dve.wait_ge(added.sem, added.upto(0, r))
                        dve.tensor_copy(gcur[:, :], k.gates[:, ds(e, 1), ds(g * TG, TG)].rearrange("p a t -> p (a t)")
                                        ).then_inc(gsel.sem, 1)
                    for s in range(NS + 2):
                        if s < NS:
                            top(r, s)
                        if 1 <= s <= NS:
                            fetch(r, s - 1)
                        if s >= 2 and (s - 2) % per_norm == per_norm - 1:
                            scale_outputs(r, s - 2)
                    dve.wait_ge(y_ps.sem, y_ps.upto(1, r))
                    if gated:
                        dve.wait_ge(gsel.sem, gsel.upto(1, r))
                    add_gated(k, dve, k.x_all, g, k.ps[:, PY, :], gcur if gated else None, gate_col, added)


def narrow_attention(k, E, nk, scale, weights, gate_col, clip=None, gated=False):
    nc = k.nc
    H, DH, DP = 16, 8, 32
    NS = TG * H // 4
    ND = 10
    self_attn = nk == P
    ck = P if self_attn else CK
    R = E * G
    SA, ST, SO, SM = 0, 3, 5, 7
    with ExitStack() as ctx:
        xT = k.sb("na_xT", [P, 2, TG * P], ctx=ctx)
        kv = xT if self_attn else k.sb("na_kv", [P, 2, TG * nk], ctx=ctx)
        w_next = k.sb("na_w_next", [P, 5 * P + 2], ctx=ctx)
        w_now = k.sb("na_w", [P, 5 * P + 2], ctx=ctx)
        orow_next = k.sb("na_orow_next", [1, P], ctx=ctx)
        orow = k.sb("na_orow", [1, P], ctx=ctx)
        w = w_now[:, 0:4 * P].rearrange("p (n c) -> p n c", c=P)
        vrow, bcol = w_now[:, 4 * P:5 * P], w_now[:, 5 * P:5 * P + 2]
        q_sb = k.sb("na_q", [P, 2, TG * P], ctx=ctx)
        k_all = k.sb("na_k", [P, TG * nk], ctx=ctx)
        k_heads = [k.nx_all[:, :, :].rearrange("p b c -> p (b c)")[:, 0:H * TG * nk],
                   k.sb("na_km", [P, H * TG * nk], ctx=ctx)[:, :]]
        k_heads = [a.rearrange("p (h t n) -> p h t n", h=H, t=TG) for a in k_heads]
        v_sb = k.sb("na_v", [P, 2, TG, H, DH + 1], ctx=ctx)
        clipped = k.sb("na_clip", [P, 3, 4 * nk], ctx=ctx) if clip else None
        negmax = k.sb("na_max", [P, 3, 4], ctx=ctx)
        probs = k.sb("na_p", [P, 2, 4, nk], ctx=ctx)
        pT = k.sb("na_pT", [P, 2, 4 * P], ctx=ctx)
        raw = k.sb("na_raw", [P, 4 * P], ctx=ctx)
        rec = k.sb("na_rec", [P, H], ctx=ctx)
        o_sb = k.sb("na_o", [P, TG, P], ctx=ctx)
        oT = k.sb("na_oT", [P, TG * P], ctx=ctx)
        gcur = k.sb("na_g", [P, TG], ctx=ctx)
        pad = k.sb("na_pad", [P, 3], ctx=ctx)

        loaded = k.sig("dma_landed", 4, E)
        w_in = k.sig("weights_copied", 1, E)
        ready = k.sig("x_ready", 1, R)
        q_ps, k_ps, v_ps = (k.sig(f"{n}_made", 1, R) for n in "qkv")
        q_in, k_in, v_in = (k.sig(f"{n}_in_sbuf", 1, R) for n in "qkv")
        masked_d, masked_p = k.sig("k_masked_dve", 1, R), k.sig("k_masked_pool", 1, R)
        s_ps, mx, ex = k.sig("scores_made", NS, R), k.sig("max_found", NS, R), k.sig("exp_done", NS, R)
        clp = k.sig("scores_clipped", NS, R) if clip else None
        t_ps, t_in = k.sig("probs_turned", NS, R), k.sig("probsT_in_sbuf", NS, R)
        pv = k.sig("outputs_made", NS, R)
        raw_in = k.sig("outputs_copied", TG, R)
        back = k.sig("outputs_turned_back", TG, R)
        rc, nrm = k.sig("sums_inverted", TG, R), k.sig("outputs_scaled", TG, R)
        ot_ps, ot_in = k.sig("outputs_turned", 1, R), k.sig("outputsT_in_sbuf", 1, R)
        y_ps, added = k.sig("y_made", 1, R), k.sig("y_added", 1, R)
        gsel = k.sig("gates_copied", 1, R) if gated else None
        set_up = k.sig("setup_step", 2)

        def slot(n):
            return (n % 32) % 3, (n - 3 if n % 32 >= 3 else n - 2 if n % 32 < 2 else n - 5)

        def sets(eng, start, body, end):
            def one(e):
                start(e, e * G)
                body(e, 0, True, False)
                with eng.Fori(1, G // 2 - 1) as i:
                    body(e, 2 * i, False, False)
                body(e, G - 2, False, True)
                end(e, e * G + (G - 1))
            if E == 1:
                one(0)
            else:
                with eng.Fori(0, E) as e:
                    one(e)

        def steps(e, g0, first, last):
            for u in range(2):
                for s in range(NS):
                    yield e * G + (g0 + u), g0 + u, u, s, NS * u + s, not (first and u == 0), not (last and u == 1)

        with nc.Block() as block:
            @block.sync
            def _(sp):
                with sp.Fori(0, E) as e:
                    sp.wait_ge(w_in.sem, w_in.upto(0, e))
                    sp.dma_start(w_next[:, 0:4 * P], weights["w"][ds(e, 1)].rearrange("a p n c -> p (a n c)")
                                 ).then_inc(loaded.sem, 16)
                    sp.dma_start(w_next[:, 5 * P:5 * P + 2], weights["bcol"][ds(e, 1)].rearrange("a p n -> p (a n)")
                                 ).then_inc(loaded.sem, 16)
                    sp.dma_start(w_next[:, 4 * P:5 * P], weights["rows"][ds(e, 1), 0, :].rearrange("a c -> (a c)")
                                 .partition_broadcast(P)).then_inc(loaded.sem, 16)
                    sp.dma_start(orow_next[:, :], weights["rows"][ds(e, 1), 1, :]).then_inc(loaded.sem, 16)

            @block.gpsimd
            def _(pool):
                def carry(n):
                    pool.tensor_tensor(pad[:, n:n + 1], k.cols[:, 0:1], k.cols[:, 0:1], ALU.mult)

                def copy(r, g, u, slot_used=True):
                    if slot_used:
                        pool.wait_ge(v_ps.sem, v_ps.upto(1, r - 2))
                    carry(0)
                    last = pool.tensor_copy(xT[:, u], k.nxT_all[:, ds(g * (TG * P), TG * P)])
                    if not self_attn:
                        last = pool.tensor_copy(kv[0:CK, u], k.ctxT[:, ds(g * (TG * nk), TG * nk)])
                    last.then_inc(ready.sem, 1)

                def mask(r, u, fresh):
                    pool.wait_ge(k_in.sem, k_in.upto(1, r))
                    if not fresh:
                        pool.wait_ge(s_ps.sem, s_ps.upto(0, r - 1))
                    carry(1)
                    for h in range(ND, H):
                        last = pool.tensor_scalar(k_heads[u][:, h].rearrange("p t n -> p (t n)"), k_all[:, :],
                                                  k.cols[:, 16 + h:17 + h], None, ALU.mult)
                    last.then_inc(masked_p.sem, 1)

                def start(e, r):
                    pool.wait_ge(y_ps.sem, y_ps.upto(0, r))
                    carry(2)
                    last = pool.tensor_copy(xT[:, 0], k.nxT_all[:, 0:TG * P])
                    if not self_attn:
                        last = pool.tensor_copy(kv[0:CK, 0], k.ctxT[:, 0:TG * nk])
                    last.then_inc(ready.sem, 1)
                    copy(r + 1, 1, 1, False)
                    mask(r, 0, True)

                def body(e, g0, first, last):
                    for r, g, u, s, n, before, after in steps(e, g0, first, last):
                        if s == 0 and after:
                            mask(r + 1, 1 - u, not before)
                            if not last:
                                copy(r + 2, g + 2, u)

                sets(pool, start, body, lambda e, r: None)

            @block.tensor
            def _(pe):
                def project_k(r, u):
                    pe.wait_ge(ready.sem, ready.upto(1, r))
                    pe.wait_ge(v_in.sem, v_in.upto(0, r))
                    pe.matmul(k.ps[:, SM, 0:TG * nk], w[0:ck, 1, :], kv[0:ck, u], start=True,
                              stop=True).then_inc(k_ps.sem, 1)

                def project_q(r, u, before):
                    if before:
                        pe.wait_ge(added.sem, added.upto(1, r - 2))
                    else:
                        pe.wait_ge(k_in.sem, k_in.upto(1, r))
                    pe.matmul(k.ps[:, SM, :], w[:, 0, :], xT[:, u], start=True, stop=True).then_inc(q_ps.sem, 1)

                def project_v(r, u):
                    pe.wait_ge(q_in.sem, q_in.upto(1, r))
                    for t in range(TG):
                        mm = pe.matmul(k.ps[0:nk, SM, t * P:(t + 1) * P], kv[0:ck, u, t * nk:(t + 1) * nk],
                                       w[0:ck, 2, :], start=True, stop=True)
                    mm.then_inc(v_ps.sem, 1)

                def scores(r0, n, u, fresh):
                    b, before = slot(n)
                    s = n % NS
                    r = r0 + n // NS
                    if s == 0:
                        pe.wait_ge(q_in.sem, q_in.upto(1, r))
                        pe.wait_ge(masked_d.sem, masked_d.upto(1, r))
                        pe.wait_ge(masked_p.sem, masked_p.upto(1, r))
                    if not fresh:
                        pe.wait_ge(ex.sem, ex.upto(before + 1, r0))
                    t, rg = divmod(s, 4)
                    pe.matmul(k.ps[:, SA + b, 0:4 * nk].rearrange("p (h n) -> p h n", n=nk),
                              q_sb[:, u, t * P:(t + 1) * P], k_heads[u][:, 4 * rg:4 * rg + 4, t, :], start=True,
                              stop=True).then_inc(s_ps.sem, 1)

                def turn(r, s, fresh):
                    pe.wait_ge(ex.sem, ex.upto(s + 1, r))
                    if not fresh:
                        pe.wait_ge(t_in.sem, t_in.upto(s - 1, r))
                    for j in range(4):
                        mm = pe.transpose(k.ps[0:nk, ST + s % 2, j * P:(j + 1) * P], probs[:, s % 2, j, :],
                                          k.ident[:, :])
                    mm.then_inc(t_ps.sem, 1)

                def outputs(r, u, s, fresh):
                    t, rg = divmod(s, 4)
                    pe.wait_ge(t_in.sem, t_in.upto(s + 1, r))
                    if s == 0:
                        pe.wait_ge(v_in.sem, v_in.upto(1, r))
                    if rg == 0 and not (fresh and t < 2):
                        pe.wait_ge(nrm.sem, nrm.upto(t - 1, r))
                    for j in range(4):
                        mm = pe.matmul(k.ps[DP * j:DP * j + DH + 1, SO + t % 2, rg * P:(rg + 1) * P],
                                       v_sb[0:nk, u, t, 4 * rg + j, :], pT[0:nk, s % 2, j * P:(j + 1) * P],
                                       start=True, stop=True)
                    mm.then_inc(pv.sem, 1)

                def turn_back(r, t):
                    pe.wait_ge(raw_in.sem, raw_in.upto(t + 1, r))
                    for c in range(4):
                        mm = pe.transpose(k.ps[:, SO + t % 2, c * P:(c + 1) * P], raw[:, c * P:(c + 1) * P], k.ident[:, :])
                    mm.then_inc(back.sem, 1)

                def turn_outputs(r, after):
                    pe.wait_ge(nrm.sem, nrm.upto(TG, r))
                    if after:
                        pe.wait_ge(k_in.sem, k_in.upto(1, r + 2))
                    else:
                        pe.wait_ge(v_in.sem, v_in.upto(1, r))
                    for t in range(TG):
                        mm = pe.transpose(k.ps[:, SM, t * P:(t + 1) * P], o_sb[:, t, :], k.ident[:, :])
                    mm.then_inc(ot_ps.sem, 1)

                def project_out(r):
                    pe.wait_ge(ot_in.sem, ot_in.upto(1, r))
                    for t in range(TG):
                        y = k.ps[:, SM, t * P:(t + 1) * P]
                        if not gated:
                            pe.matmul(y, k.ones[0:1, :], orow[0:1, :], start=True, stop=False)
                        mm = pe.matmul(y, oT[:, t * P:(t + 1) * P], w[:, 3, :], start=gated, stop=True)
                    mm.then_inc(y_ps.sem, 1)

                def start(e, r):
                    pe.wait_ge(w_in.sem, w_in.upto(1, e))
                    project_k(r, 0)
                    project_q(r, 0, False)
                    project_v(r, 0)
                    scores(r, 0, 0, True)
                    scores(r, 1, 0, True)

                def body(e, g0, first, last):
                    r0 = e * G + g0
                    for r, g, u, s, n, before, after in steps(e, g0, first, last):
                        if s + 2 < NS or after:
                            scores(r0, n + 2, ((n + 2) // NS) % 2, first and n + 2 < 3)
                        turn(r, s, s == 0 and not before)
                        if s >= 1:
                            outputs(r, u, s - 1, not before)
                        elif before:
                            outputs(r - 1, 1 - u, NS - 1, False)
                        if s == 1 and after:
                            project_k(r + 1, 1 - u)
                        if s == 2 and before:
                            turn_back(r - 1, TG - 1)
                        if s == 4 and before:
                            turn_outputs(r - 1, after)
                        if s == 6 and before:
                            project_out(r - 1)
                        if s % 4 == 2 and s > 2:
                            turn_back(r, s // 4 - 1)
                        if s == 9 and after:
                            project_q(r + 1, 1 - u, before)
                        if s == 12 and after:
                            project_v(r + 1, 1 - u)

                def end(e, r):
                    outputs(r, 1, NS - 1, False)
                    turn_back(r, TG - 1)
                    turn_outputs(r, False)
                    project_out(r)

                sets(pe, start, body, end)

            @block.scalar
            def _(act):
                def exps(r0, n, fresh=False):
                    b, _ = slot(n)
                    act.wait_ge(mx.sem, mx.upto(n + 1, r0))
                    if not fresh:
                        act.wait_ge(t_ps.sem, t_ps.upto(n - 1, r0))
                    for j in range(4):
                        src = clipped[:, b, j * nk:(j + 1) * nk] if clip else \
                            k.ps[:, SA + b, j * nk:(j + 1) * nk]
                        last = act.activation(probs[:, n % 2, j, :], src, ACT.Exp, bias=negmax[:, b, j:j + 1])
                    last.then_inc(ex.sem, 1)

                def fetch(r, s, fresh):
                    act.wait_ge(t_ps.sem, t_ps.upto(s + 1, r))
                    if not fresh:
                        act.wait_ge(pv.sem, pv.upto(s - 1, r))
                    act.copy(pT[0:nk, s % 2, :], k.ps[0:nk, ST + s % 2, :]).then_inc(t_in.sem, 1)

                def start(e, r):
                    act.wait_ge(loaded.sem, loaded.upto(4, e))
                    act.wait_ge(added.sem, added.upto(0, r))
                    act.copy(w_now[:, :], w_next[:, :])
                    act.copy(orow[:, :], orow_next[:, :]).then_inc(w_in.sem, 1)
                    exps(r, 0, True)

                def body(e, g0, first, last):
                    r0 = e * G + g0
                    for r, g, u, s, n, before, after in steps(e, g0, first, last):
                        if s + 1 < NS or after:
                            exps(r0, n + 1)
                        fetch(r, s, s == 0 and not before)

                sets(act, start, body, lambda e, r: None)

            @block.vector
            def _(dve):
                def top(r0, n):
                    b, _ = slot(n)
                    dve.wait_ge(s_ps.sem, s_ps.upto(n + 1, r0))
                    src = k.ps[:, SA + b, 0:4 * nk]
                    if clip:
                        dve.tensor_scalar(clipped[:, b], src, clip, -clip, ALU.min, ALU.max).then_inc(clp.sem, 1)
                        dve.wait_ge(clp.sem, clp.upto(n + 1, r0))
                        src = clipped[:, b]
                    dve.tensor_reduce(negmax[:, b], src.rearrange("p (h n) -> p h n", n=nk), X, ALU.max,
                                      negate=True).then_inc(mx.sem, 1)

                def take_k(r):
                    dve.wait_ge(k_ps.sem, k_ps.upto(1, r))
                    dve.wait_ge(masked_d.sem, masked_d.upto(0, r))
                    dve.wait_ge(masked_p.sem, masked_p.upto(0, r))
                    dve.tensor_scalar(k_all[:, :], k.ps[:, SM, 0:TG * nk], bcol[:, 1:2], None,
                                      ALU.add).then_inc(k_in.sem, 1)

                def mask(r, u, h, fresh):
                    if h == 0:
                        dve.wait_ge(k_in.sem, k_in.upto(1, r))
                    if h == 0 and not fresh:
                        dve.wait_ge(s_ps.sem, s_ps.upto(0, r - 1))
                    last = dve.tensor_scalar(k_heads[u][:, h].rearrange("p t n -> p (t n)"), k_all[:, :],
                                             k.cols[:, 16 + h:17 + h], None, ALU.mult)
                    if h == ND - 1:
                        last.then_inc(masked_d.sem, 1)

                def take_q(r, u):
                    dve.wait_ge(q_ps.sem, q_ps.upto(1, r))
                    dve.tensor_scalar(q_sb[:, u], k.ps[:, SM, :], bcol[:, 0:1], scale, ALU.add,
                                      ALU.mult).then_inc(q_in.sem, 1)

                def take_v(r, u):
                    dve.wait_ge(v_ps.sem, v_ps.upto(1, r))
                    for t in range(TG):
                        last = dve.tensor_tensor(v_sb[0:nk, u, t, :, 0:DH],
                                                 k.ps[0:nk, SM, t * P:(t + 1) * P].rearrange("p (h c) -> p h c", c=DH),
                                                 vrow[0:nk, :].rearrange("p (h c) -> p h c", c=DH), ALU.add)
                    last.then_inc(v_in.sem, 1)

                def copy_outputs(r, t):
                    dve.wait_ge(pv.sem, pv.upto(4 * t + 4, r))
                    dve.wait_ge(back.sem, back.upto(t, r))
                    dve.tensor_copy(raw[:, :], k.ps[:, SO + t % 2, :]).then_inc(raw_in.sem, 1)

                def scale_outputs(r, t):
                    dve.wait_ge(back.sem, back.upto(t + 1, r))
                    o = k.ps[:, SO + t % 2, :].rearrange("p (h c) -> p h c", c=DP)
                    dve.reciprocal(rec[:, :], o[:, :, DH]).then_inc(rc.sem, 1)
                    dve.wait_ge(rc.sem, rc.upto(t + 1, r))
                    if t == 0:
                        dve.wait_ge(ot_ps.sem, ot_ps.upto(0, r))
                    dve.tensor_tensor(o_sb[:, t, :].rearrange("p (h c) -> p h c", c=DH), o[:, :, 0:DH],
                                      bc(rec[:, :].unsqueeze(2), [P, H, DH]), ALU.mult).then_inc(nrm.sem, 1)

                def take_oT(r, g):
                    dve.wait_ge(ot_ps.sem, ot_ps.upto(1, r))
                    dve.wait_ge(y_ps.sem, y_ps.upto(0, r))
                    dve.tensor_copy(oT[:, :], k.ps[:, SM, :]).then_inc(ot_in.sem, 1)
                    if gated:
                        dve.wait_ge(added.sem, added.upto(0, r))
                        dve.tensor_copy(gcur[:, :], k.gates[:, ds(e_now[0], 1), ds(g * TG, TG)]
                                        .rearrange("p a t -> p (a t)")).then_inc(gsel.sem, 1)

                def add(r, g):
                    dve.wait_ge(y_ps.sem, y_ps.upto(1, r))
                    if gated:
                        dve.wait_ge(gsel.sem, gsel.upto(1, r))
                    add_gated(k, dve, k.x_all, g, k.ps[:, SM, :], gcur if gated else None, gate_col, added)

                e_now = [0]

                def start(e, r):
                    e_now[0] = e
                    dve.wait_ge(w_in.sem, w_in.upto(1, e))
                    take_k(r)
                    for h in range(ND):
                        mask(r, 0, h, True)
                    take_q(r, 0)
                    take_v(r, 0)
                    top(r, 0)
                    top(r, 1)

                def body(e, g0, first, last):
                    r0 = e * G + g0
                    for r, g, u, s, n, before, after in steps(e, g0, first, last):
                        if s + 2 < NS or after:
                            top(r0, n + 2)
                        if s == 1 and before:
                            copy_outputs(r - 1, TG - 1)
                        if s == 2 and after:
                            take_k(r + 1)
                        if 3 <= s < 3 + ND and after:
                            mask(r + 1, 1 - u, s - 3, not before)
                        if s == 3 and before:
                            scale_outputs(r - 1, TG - 1)
                        if s == 5 and before:
                            take_oT(r - 1, g - 1)
                        if s == 7 and before:
                            add(r - 1, g - 1)
                        if s % 4 == 1 and s > 1:
                            copy_outputs(r, s // 4 - 1)
                        if s % 4 == 3 and s > 3:
                            scale_outputs(r, s // 4 - 1)
                        if s == 10 and after:
                            take_q(r + 1, 1 - u)
                        if s == 13 and after:
                            take_v(r + 1, 1 - u)

                def end(e, r):
                    copy_outputs(r, TG - 1)
                    scale_outputs(r, TG - 1)
                    take_oT(r, G - 1)
                    add(r, G - 1)

                dve.memset(k.ps[:, SO:SO + 2, :], 0.0).then_inc(set_up.sem, 1)
                dve.wait_ge(set_up.sem, set_up.upto(1))
                dve.memset(v_sb[:, :, :, :, DH:DH + 1], 1.0).then_inc(set_up.sem, 1)
                dve.wait_ge(set_up.sem, set_up.upto(2))
                sets(dve, start, body, end)


def add_gated(k, dve, target, g, y, gcur, gate_col, done):
    if gcur is None:
        last = dve.scalar_tensor_tensor(target[:, ds(g * TG, TG), :].rearrange("p t c -> p (t c)"), y, gate_col,
                                        target[:, ds(g * TG, TG), :].rearrange("p t c -> p (t c)"), ALU.mult, ALU.add)
    else:
        for t in range(TG):
            x = target[:, ds(g * TG + t, 1), :].rearrange("p a c -> p (a c)")
            last = dve.scalar_tensor_tensor(x, y[:, t * P:(t + 1) * P], gcur[:, t:t + 1], x, ALU.mult, ALU.add)
    last.then_inc(done.sem, 1)


def add_gated_rows(k, rows_dram):
    nc = k.nc
    NB = P // 8
    with ExitStack() as ctx:
        diag = k.sb("gr_diag", [P, NB, P], ctx=ctx)
        by_sample = k.sb("gr_gates", [P, B, 8], ctx=ctx)
        gT = k.sb("gr_gT", [P, B // NB, P], ctx=ctx)
        loaded = k.sig("dma_landed", 1)
        step = k.sig("dve_step", 2)
        turned = k.sig("turned", 1)
        made = k.sig("y_made", 1, G)
        added = k.sig("y_added", 1, G)
        with nc.Block() as block:
            @block.sync
            def _(sp):
                sp.dma_start(diag[:, :, :], rows_dram).then_inc(loaded.sem, 16)

            @block.tensor
            def _(pe):
                pe.wait_ge(loaded.sem, loaded.upto(1))
                pe.wait_ge(step.sem, step.upto(1))
                for n in range(B // NB):
                    mm = pe.transpose(k.ps[:, 0, n * P:(n + 1) * P],
                                      by_sample[:, NB * n:NB * (n + 1), :].rearrange("p b e -> p (b e)"), k.ident[:, :])
                mm.then_inc(turned.sem, 1)
                pe.wait_ge(step.sem, step.upto(2))
                for g in range(G):
                    if g >= 2:
                        pe.wait_ge(added.sem, added.upto(1, g - 2))
                    b = g * TG % NB
                    pe.matmul(k.ps[:, 1 + g % 2, :], gT[:, g * TG // NB, :],
                              diag[:, b:b + TG, :].rearrange("p b c -> p (b c)"), start=True,
                              stop=True).then_inc(made.sem, 1)

            @block.vector
            def _(dve):
                dve.tensor_copy(by_sample[:, :, :], k.gates[:, 0:8, :].rearrange("p e b -> p b e")).then_inc(step.sem, 1)
                dve.wait_ge(turned.sem, turned.upto(1))
                dve.tensor_copy(gT[:, :, :].rearrange("p n c -> p (n c)"), k.ps[:, 0, :]).then_inc(step.sem, 1)
                for g in range(G):
                    dve.wait_ge(made.sem, made.upto(1, g))
                    x = k.x_all[:, g * TG:(g + 1) * TG, :].rearrange("p t c -> p (t c)")
                    dve.tensor_tensor(x, x, k.ps[:, 1 + g % 2, :], ALU.add).then_inc(added.sem, 1)


def experts(k, E, MC, func, weights, target, up, pair=False, gate_col=None, gated=True):
    nc = k.nc
    R = E * G
    NY = 2 if pair else 1
    with ExitStack() as ctx:
        w1 = k.sb("ex_w1", [P, MC * P], ctx=ctx)
        w3 = k.sb("ex_w3", [P, MC * P], ctx=ctx) if up else None
        w2 = k.sb("ex_w2", [P, MC, P], ctx=ctx)
        bcol = k.sb("ex_bcol", [P, 2 * MC], ctx=ctx)
        orow = k.sb("ex_orow", [1, P], ctx=ctx)
        act_sb = k.sb("ex_act", [P, 2, TG * P], ctx=ctx)
        hid = k.sb("ex_hid", [P, 2, MC, TG * P], ctx=ctx)
        gcur = k.sb("ex_g", [P, 2, NY * TG], ctx=ctx)
        ND = 4 + bool(up)
        loaded = k.sig("dma_landed", ND, E)
        g_ps = k.sig("h1_made", MC, R)
        u_ps = k.sig("h3_made", MC, R) if up else None
        a_in = k.sig("h1_activated", MC, R)
        h_in = k.sig("hidden_in_sbuf", MC, R) if up else None
        y_ps = k.sig("y_made", 1, R)
        added = k.sig("y_added", NY, R)
        gsel = k.sig("gates_copied", 1, R) if gated else None
        hdone = h_in if up else a_in
        with nc.Block() as block:
            @block.sync
            def _(sp):
                with sp.Fori(0, E) as e:
                    sp.wait_ge(added.sem, added.upto(0, e * G))
                    sp.dma_start(w1[:, :], weights["w1"][ds(e, 1)].rearrange("a p m -> p (a m)")).then_inc(loaded.sem, 16)
                    if up:
                        sp.dma_start(w3[:, :], weights["w3"][ds(e, 1)].rearrange("a p m -> p (a m)")
                                     ).then_inc(loaded.sem, 16)
                    sp.dma_start(w2[:, :, :], weights["w2"][ds(e, 1)].rearrange("a p m c -> p (a m) c")
                                 ).then_inc(loaded.sem, 16)
                    sp.dma_start(bcol[:, :], weights["bcol"][ds(e, 1)].rearrange("a p m -> p (a m)")
                                 ).then_inc(loaded.sem, 16)
                    sp.dma_start(orow[:, :], weights["brow"][ds(e, 1), :]).then_inc(loaded.sem, 16)

            @block.tensor
            def _(pe):
                def hidden(r, u, g):
                    x = k.nxT_all[:, ds(g * (TG * P), TG * P)]
                    for m in range(MC):
                        n = u * MC + m
                        back = m - 1 if m >= 1 else 0
                        pe.wait_ge(hdone.sem, hdone.upto(back, r) if m >= 1 or MC > 1 else hdone.upto(0, r))
                        pe.matmul(k.ps[:, n % 2, :], w1[:, m * P:(m + 1) * P], x, start=True,
                                  stop=True).then_inc(g_ps.sem, 1)
                        if up:
                            pe.matmul(k.ps[:, 2 + n % 2, :], w3[:, m * P:(m + 1) * P], x, start=True,
                                      stop=True).then_inc(u_ps.sem, 1)

                def down(r, u):
                    pe.wait_ge(hdone.sem, hdone.upto(MC, r))
                    pe.wait_ge(added.sem, added.upto(0, r))
                    for t in range(TG):
                        tok = slice(t * P, (t + 1) * P)
                        if pair:
                            for a in range(2):
                                f = slice(64 * a, 64 * a + 64)
                                mm = pe.matmul(k.ps[:, 4 + 2 * u + a, tok], hid[f, u, 0, tok], w2[f, 0, :], start=True,
                                               stop=True)
                        else:
                            if not gated:
                                pe.matmul(k.ps[:, 4 + u, tok], k.ones[0:1, :], orow[0:1, :], start=True, stop=False)
                            for m in range(MC):
                                mm = pe.matmul(k.ps[:, 4 + u, tok], hid[:, u, m, tok], w2[:, m, :],
                                               start=gated and m == 0,
                                               stop=m == MC - 1)
                    mm.then_inc(y_ps.sem, 1)

                todo = []
                for e, r, u, g in rounds(pe, E):
                    if u == 0:
                        pe.wait_ge(loaded.sem, loaded.upto(ND, e))
                    hidden(r, u, g)
                    todo.append((r, u))
                    if u == 1:
                        for a in todo:
                            down(*a)
                        todo = []

            @block.scalar
            def _(act):
                for e, r, u, g in rounds(act, E):
                    if u == 0:
                        act.wait_ge(loaded.sem, loaded.upto(ND, e))
                    for m in range(MC):
                        n = u * MC + m
                        act.wait_ge(g_ps.sem, g_ps.upto(m + 1, r))
                        if up:
                            act.wait_ge(h_in.sem, h_in.upto(max(m - 1, 0), r))
                            out = act_sb[:, n % 2]
                        else:
                            if m == 0:
                                act.wait_ge(y_ps.sem, y_ps.upto(0, r) if u == 0 else y_ps.upto(0, r - 1))
                            out = hid[:, u, m, :]
                        act.activation(out, k.ps[:, n % 2, :], func, bias=bcol[:, m:m + 1]).then_inc(a_in.sem, 1)

            @block.vector
            def _(dve):
                held = []
                for e, r, u, g in rounds(dve, E):
                    if u == 0:
                        dve.wait_ge(loaded.sem, loaded.upto(ND, e))
                    if up:
                        for m in range(MC):
                            n = u * MC + m
                            dve.wait_ge(u_ps.sem, u_ps.upto(m + 1, r))
                            dve.wait_ge(a_in.sem, a_in.upto(m + 1, r))
                            dve.scalar_tensor_tensor(hid[:, u, m, :], k.ps[:, 2 + n % 2, :], bcol[:, MC + m:MC + m + 1],
                                                     act_sb[:, n % 2], ALU.add, ALU.mult).then_inc(h_in.sem, 1)
                    if gated:
                        if u == 0:
                            dve.wait_ge(added.sem, added.upto(0, r))
                        for a in range(NY):
                            last = dve.tensor_copy(gcur[:, u, a * TG:(a + 1) * TG],
                                                   k.gates[:, ds(e * NY + a, 1), ds(g * TG, TG)]
                                                   .rearrange("p a t -> p (a t)"))
                        last.then_inc(gsel.sem, 1)
                    held.append((r, u, g))
                    if u == 1:
                        for r, u, g in held:
                            dve.wait_ge(y_ps.sem, y_ps.upto(1, r))
                            if gated:
                                dve.wait_ge(gsel.sem, gsel.upto(1, r))
                            for a in range(NY):
                                if a:
                                    dve.wait_ge(added.sem, added.upto(a, r))
                                bank = 4 + 2 * u + a if pair else 4 + u
                                add_gated(k, dve, target, g, k.ps[:, bank, :],
                                          gcur[:, u, a * TG:(a + 1) * TG] if gated else None, gate_col, added)
                        held = []


def router_logits(k, h_all, H, rw):
    nc = k.nc
    with ExitStack() as ctx:
        w2 = k.sb("ro_w2", [P, 8], ctx=ctx)
        b2 = k.sb("ro_b2", [P, 8], ctx=ctx)
        lg = k.sb("ro_g", [P, H], ctx=ctx)
        lb = k.sb("ro_b", [P, H], ctx=ctx)
        rows = k.sb("ro_rows", [P, 2, TG, H], ctx=ctx)
        hT = k.sb("ro_hT", [P, 2, TG * P // 2], ctx=ctx)
        loaded = k.sig("dma_landed", 5)
        chain = k.sig("dve_step", 3)
        staged = k.sig("staged", 1, G)
        turned = k.sig("turned", 1, G)
        copied = k.sig("copied", 1, G)
        routed = k.sig("routed", 1, G)
        taken = k.sig("routes_taken", 1, G)
        with nc.Block() as block:
            @block.sync
            def _(sp):
                for to, of in ((w2[0:H, :], rw["w2"]), (w2[H:2 * H, :], rw["w2"]), (b2[:, :], rw["b2"].partition_broadcast(P)),
                               (lg[:, :], rw["g"].partition_broadcast(P)), (lb[:, :], rw["b"].partition_broadcast(P))):
                    sp.dma_start(to, of).then_inc(loaded.sem, 16)

            @block.tensor
            def _(pe):
                pe.wait_ge(loaded.sem, loaded.upto(5))
                for _, r, u, g in rounds(pe):
                    pe.wait_ge(staged.sem, staged.upto(1, r))
                    if u == 0:
                        pe.wait_ge(copied.sem, copied.upto(0, r))
                    for t in range(0, TG, 2):
                        mm = pe.transpose(k.ps[:, u, t * H:(t + 2) * H],
                                          rows[:, u, t:t + 2, :].rearrange("p t h -> p (t h)"), k.ident[:, :])
                    mm.then_inc(turned.sem, 1)
                    pe.wait_ge(copied.sem, copied.upto(1, r))
                    if u == 0:
                        pe.wait_ge(taken.sem, taken.upto(0, r))
                    for t in range(TG):
                        a, f = t % 2, slice(H * (t % 2), H * (t % 2) + H)
                        mm = pe.matmul(k.ps[:, 2 + 2 * a + u, (t // 2) * 8:(t // 2 + 1) * 8],
                                       hT[f, u, (t // 2) * P:(t // 2 + 1) * P], w2[f, :], start=True, stop=True)
                    mm.then_inc(routed.sem, 1)

            @block.scalar
            def _(act):
                for _, r, u, g in rounds(act):
                    act.wait_ge(turned.sem, turned.upto(1, r))
                    if u == 0:
                        act.wait_ge(routed.sem, routed.upto(0, r))
                    act.copy(hT[:, u], k.ps[:, u, 0:TG * H]).then_inc(copied.sem, 1)

            @block.vector
            def _(dve):
                link = Chain(dve, chain)
                dve.wait_ge(loaded.sem, loaded.upto(5))
                link(dve.tensor_tensor(h_all[:, :, :], h_all[:, :, :], bc(lg[:, :].unsqueeze(1), [P, B, H]), ALU.mult))
                link(dve.tensor_tensor(h_all[:, :, :], h_all[:, :, :], bc(lb[:, :].unsqueeze(1), [P, B, H]), ALU.add))
                link(dve.tensor_scalar(h_all[:, :, :], h_all[:, :, :], 0.0, None, ALU.max))
                for _, r, u, g in rounds(dve):
                    if u == 0:
                        dve.wait_ge(turned.sem, turned.upto(0, r))
                    dve.tensor_copy(rows[:, u], h_all[:, ds(g * TG, TG), :]).then_inc(staged.sem, 1)
                    dve.wait_ge(routed.sem, routed.upto(1, r))
                    for a in range(2):
                        last = dve.tensor_tensor(k.logits[:, ds(g * TG + a, TG // 2, 2), :],
                                                 k.ps[:, 2 + 2 * a + u, 0:TG * 4].rearrange("p (t w) -> p t w", w=8),
                                                 bc(b2[:, :].unsqueeze(1), [P, TG // 2, 8]), ALU.add)
                    last.then_inc(taken.sem, 1)


def top_two_gates(k, gate_col, plus=None, least=None, shared=0, capacity=None):
    nc = k.nc
    NE = 8
    S3 = [P, B, NE]
    with ExitStack() as ctx:
        t3 = [k.sb(f"tg_{i}", S3, ctx=ctx) for i in range(6)]
        c2 = [k.sb(f"tg_c{i}", [P, B], ctx=ctx) for i in range(3)]
        first, second, prob, a, b, c = t3
        m, s, z = c2
        if capacity:
            before = k.sb("tg_before", [P, P], ctx=ctx)
            tot = k.sb("tg_tot", [P, 2, B, NE], ctx=ctx)
            loc = k.sb("tg_loc", [P, 2, B, NE], ctx=ctx)
            run = k.sb("tg_run", [P, NE, B], ctx=ctx)
            zero = k.sb("tg_zero", [P, B], ctx=ctx)
        chain = k.sig("dve_step", 400)
        chosen = k.sig("chosen", 1)
        shifted = k.sig("shifted", 1)
        expd = k.sig("exp_done", 1)
        if capacity:
            counted = k.sig("counted", 1)
            loaded = k.sig("dma_landed", 1)
        with nc.Block() as block:
            if capacity:
                @block.sync
                def _(sp):
                    sp.dma_start(before[:, :], k.d["before"]).then_inc(loaded.sem, 16)

                @block.tensor
                def _(pe):
                    pe.wait_ge(loaded.sem, loaded.upto(1))
                    pe.wait_ge(chosen.sem, chosen.upto(1))
                    for i, one in enumerate((first, second)):
                        flat = one[:, :, :].rearrange("p t e -> p (t e)")
                        pe.matmul(k.ps[:, 2 * i, :], before[:, :], flat, start=True, stop=True)
                        mm = pe.matmul(k.ps[:, 2 * i + 1, :], k.ones[:, :], flat, start=True, stop=True)
                    mm.then_inc(counted.sem, 1)

            @block.scalar
            def _(act):
                act.wait_ge(shifted.sem, shifted.upto(1))
                act.activation(prob[:, :, :], c[:, :, :], ACT.Exp).then_inc(expd.sem, 1)

            @block.vector
            def _(dve):
                link = Chain(dve, chain)

                def wide(col):
                    return bc(col[:, :].unsqueeze(2), S3)

                def pick(values, onehot):
                    link(dve.tensor_reduce(s[:, :], values[:, :, :], X, ALU.max))
                    link(dve.tensor_tensor(b[:, :, :], values[:, :, :], wide(s), ALU.is_equal))
                    link(dve.tensor_tensor(b[:, :, :], b[:, :, :], bc(k.rank[:, :].unsqueeze(1), S3), ALU.mult))
                    link(dve.tensor_reduce(z[:, :], b[:, :, :], X, ALU.max))
                    link(dve.tensor_tensor(onehot[:, :, :], b[:, :, :], wide(z), ALU.is_equal))

                lg = k.logits
                link(dve.tensor_reduce(m[:, :], lg[:, :, :], X, ALU.max))
                dve.tensor_tensor(c[:, :, :], lg[:, :, :], wide(m), ALU.subtract).then_inc(shifted.sem, 1)
                pick(lg, first)
                link(dve.scalar_tensor_tensor(a[:, :, :], first[:, :, :], -1e30, lg[:, :, :], ALU.mult, ALU.add))
                pick(a, second)
                link(dve.tensor_copy(m[:, 0:1], m[:, 0:1]))
                chosen_now = dve.tensor_tensor(a[:, :, :], first[:, :, :], second[:, :, :], ALU.add)
                chosen_now.then_inc(chosen.sem, 1)
                dve.wait_ge(chosen.sem, chosen.upto(1))
                dve.wait_ge(expd.sem, expd.upto(1))
                link(dve.tensor_reduce(z[:, :], prob[:, :, :], X, ALU.add))
                link(dve.reciprocal(s[:, :], z[:, :]))
                link(dve.tensor_tensor(prob[:, :, :], prob[:, :, :], wide(s), ALU.mult))
                link(dve.tensor_tensor(b[:, :, :], prob[:, :, :], a[:, :, :], ALU.mult))
                link(dve.tensor_reduce(z[:, :], b[:, :, :], X, ALU.add))
                if plus:
                    link(dve.tensor_scalar(z[:, :], z[:, :], plus, None, ALU.add))
                if least:
                    link(dve.tensor_scalar(z[:, :], z[:, :], least, None, ALU.max))
                link(dve.reciprocal(s[:, :], z[:, :]))
                link(dve.tensor_scalar(s[:, :], s[:, :], gate_col, None, ALU.mult))
                if capacity:
                    link(dve.memset(zero[:, :], 0.0))
                    dve.wait_ge(counted.sem, counted.upto(1))
                    for i in range(2):
                        link(dve.tensor_copy(tot[:, i].rearrange("p t e -> p (t e)"), k.ps[:, 2 * i + 1, :]))
                        for e in range(NE):
                            start = 0.0 if i == 0 else z[:, e:e + 1]
                            link(dve.tensor_tensor_scan(run[:, e, :], tot[:, i, :, e], zero[:, :], start, ALU.add,
                                                        ALU.add))
                        link(dve.tensor_copy(z[:, 0:NE], run[:, :, B - 1]))
                        link(dve.tensor_tensor(c[:, :, :], run[:, :, :].rearrange("p e t -> p t e"), tot[:, i],
                                               ALU.subtract))
                        link(dve.tensor_tensor(loc[:, i], c[:, :, :],
                                               k.ps[:, 2 * i, :].rearrange("p (t e) -> p t e", e=NE), ALU.add))
                        one = first if i == 0 else second
                        link(dve.scalar_tensor_tensor(one[:, :, :], loc[:, i], float(capacity), one[:, :, :],
                                                      ALU.is_lt, ALU.mult))
                    link(dve.tensor_tensor(a[:, :, :], first[:, :, :], second[:, :, :], ALU.add))
                    link(dve.tensor_tensor(b[:, :, :], prob[:, :, :], a[:, :, :], ALU.mult))
                link(dve.tensor_tensor(k.gates[:, 0:NE, :].rearrange("p e t -> p t e"), b[:, :, :], wide(s), ALU.mult))
                for e in range(shared):
                    link(dve.tensor_scalar(k.gates[:, NE + e, :], m[:, :], 0.0, gate_col, ALU.mult, ALU.add))
                chain.per = chain.each = link.n


def ssm_kernel(k, ww, conv_dram):
    nc = k.nc
    N, L = 64, P
    re = k.nx_all[:, :, :]
    im = k.nxT_all[:, :].rearrange("p (n l) -> p n l", l=L)
    with ExitStack() as ctx:
        inp = k.sb("sk_in", [P, 4 * N + 2], ctx=ctx)
        t = [k.sb(f"sk_{i}", [P, N], ctx=ctx) for i in range(12)]
        t1 = k.sb("sk_t1", [P, N, L // 2], ctx=ctx)
        t2 = k.sb("sk_t2", [P, N, L // 2], ctx=ctx)
        row = k.sb("sk_row", [P, 2 * P], ctx=ctx)
        loaded = k.sig("dma_landed", 1)
        stored = k.sig("dma_stored", 1)
        chain = k.sig("dve_step", 400)
        to_sin = k.sig("angles_ready", 2)
        sins = k.sig("sines_done", 2)
        finished = k.sig("kernel_ready", 1)
        with nc.Block() as block:
            @block.sync
            def _(sp):
                sp.dma_start(inp[:, :], ww["ssm"]).then_inc(loaded.sem, 16)
                sp.wait_ge(finished.sem, finished.upto(1))
                sp.dma_start(conv_dram, row[:, :]).then_inc(stored.sem, 16)
                sp.wait_ge(stored.sem, stored.upto(1))

            @block.scalar
            def _(act):
                for i in range(2):
                    act.wait_ge(to_sin.sem, to_sin.upto(i + 1))
                    act.activation(t[2 + i][:, :], t[i][:, :], ACT.Sin).then_inc(sins.sem, 1)

            @block.vector
            def _(dve):
                link = Chain(dve, chain)
                A_re, A_im, C_re, C_im = (inp[:, i * N:(i + 1) * N] for i in range(4))
                log_dt, skip = inp[:, 4 * N:4 * N + 1], inp[:, 4 * N + 1:4 * N + 2]

                def exps(x, w, p2, u, r, f, em1=None, ex=None):
                    link(dve.tensor_scalar(r, x, 80.0, -80.0, ALU.min, ALU.max))
                    link(dve.tensor_scalar(p2, r, 1.4426950408889634, None, ALU.mult))
                    link(dve.tensor_scalar(p2, p2, MAGIC + 127.0, None, ALU.add))
                    link(dve.tensor_scalar(f, p2, MAGIC + 127.0, None, ALU.subtract))
                    link(dve.scalar_tensor_tensor(r, f, -0.693359375, r, ALU.mult, ALU.add))
                    link(dve.scalar_tensor_tensor(r, f, 2.12194440e-4, r, ALU.mult, ALU.add))
                    link(dve.tensor_scalar(u, r, 1.0 / 8, 1.0, ALU.mult, ALU.add))
                    for j in range(7, 1, -1):
                        link(dve.scalar_tensor_tensor(u, u, 1.0 / j, r, ALU.mult, ALU.mult))
                        link(dve.tensor_scalar(u, u, 1.0, None, ALU.add))
                    link(dve.tensor_tensor(u, u, r, ALU.mult))
                    link(dve.tensor_scalar(p2.bitcast(I32), p2.bitcast(I32), 23, None, ALU.logical_shift_left))
                    link(dve.tensor_tensor(u, u, p2, ALU.mult))
                    if ex is not None:
                        link(dve.tensor_tensor(ex, u, p2, ALU.add))
                    if em1 is not None:
                        link(dve.tensor_scalar(p2, p2, 1.0, None, ALU.subtract))
                        link(dve.tensor_tensor(em1, u, p2, ALU.add))

                def col(i, w=N):
                    return t[i][:, 0:w]

                dve.wait_ge(loaded.sem, loaded.upto(1))
                exps(log_dt, 1, col(4, 1), col(5, 1), col(6, 1), col(7, 1), ex=col(8, 1))
                dt = t[8][:, 0:1]
                link(dve.tensor_scalar(col(9), A_im, dt, 0.5, ALU.mult, ALU.mult))
                for i in range(2):
                    link(dve.tensor_scalar(col(4), col(9), 0.15915494309189535, 0.25 * i, ALU.mult, ALU.add))
                    link(dve.tensor_scalar(col(4), col(4), MAGIC, None, ALU.add))
                    link(dve.tensor_scalar(col(4), col(4), MAGIC, None, ALU.subtract))
                    link(dve.scalar_tensor_tensor(col(i), col(4), -6.28125, col(9), ALU.mult, ALU.add))
                    link(dve.scalar_tensor_tensor(col(i), col(4), -1.9353071795864769e-3, col(i), ALU.mult, ALU.add))
                    if i:
                        link(dve.tensor_scalar(col(i), col(i), 1.5707963267948966, None, ALU.add))
                    last = dve.tensor_scalar(col(i), col(i), 3.1415925, -3.1415925, ALU.min, ALU.max)
                    last.then_inc(to_sin.sem, 1)
                link(dve.tensor_scalar(col(10), A_re, dt, None, ALU.mult))
                exps(col(10), N, col(4), col(5), col(6), col(7), em1=col(11), ex=col(9))
                dve.wait_ge(sins.sem, sins.upto(2))
                s, c = col(2), col(3)
                link(dve.scalar_tensor_tensor(col(4), s, -2.0, s, ALU.mult, ALU.mult))
                link(dve.scalar_tensor_tensor(col(5), s, 2.0, c, ALU.mult, ALU.mult))
                link(dve.tensor_scalar(col(6), col(4), 1.0, None, ALU.add))
                zi = col(0)
                link(dve.tensor_tensor(zi, col(9), col(5), ALU.mult))
                link(dve.tensor_tensor(col(7), col(11), col(6), ALU.mult))
                link(dve.tensor_tensor(col(7), col(7), col(4), ALU.add))
                zr = col(1)
                link(dve.tensor_tensor(zr, col(9), col(6), ALU.mult))
                link(dve.tensor_tensor(col(2), A_re, A_re, ALU.mult))
                link(dve.tensor_tensor(col(3), A_im, A_im, ALU.mult))
                link(dve.tensor_tensor(col(2), col(2), col(3), ALU.add))
                link(dve.reciprocal(col(2), col(2)))

                def cmul(orr, oi, ar, ai, br, bi, x, y, conj=1.0):
                    link(dve.tensor_tensor(x, ar, br, ALU.mult))
                    link(dve.scalar_tensor_tensor(y, ai, -conj, bi, ALU.mult, ALU.mult))
                    link(dve.tensor_tensor(orr, x, y, ALU.add))
                    link(dve.scalar_tensor_tensor(x, ar, conj, bi, ALU.mult, ALU.mult))
                    link(dve.tensor_tensor(y, ai, br, ALU.mult))
                    link(dve.tensor_tensor(oi, x, y, ALU.add))

                cmul(col(8), col(9), C_re, C_im, col(7), zi, col(3), col(4))
                cmul(col(10), col(11), col(8), col(9), A_re, A_im, col(3), col(4), conj=-1.0)
                link(dve.tensor_tensor(re[:, :, 0], col(10), col(2), ALU.mult))
                link(dve.tensor_tensor(im[:, :, 0], col(11), col(2), ALU.mult))
                m = 1
                while m < L:
                    shape = [P, N, m]
                    a, b = re[:, :, 0:m], im[:, :, 0:m]
                    x, y = t1[:, :, 0:m], t2[:, :, 0:m]
                    zrb, zib = bc(zr.unsqueeze(2), shape), bc(zi.unsqueeze(2), shape)
                    link(dve.tensor_tensor(x, a, zrb, ALU.mult))
                    link(dve.tensor_tensor(y, b, zib, ALU.mult))
                    link(dve.tensor_tensor(re[:, :, m:2 * m], x, y, ALU.subtract))
                    link(dve.tensor_tensor(x, a, zib, ALU.mult))
                    link(dve.tensor_tensor(y, b, zrb, ALU.mult))
                    link(dve.tensor_tensor(im[:, :, m:2 * m], x, y, ALU.add))
                    link(dve.scalar_tensor_tensor(col(5), zr, 2.0, zi, ALU.mult, ALU.mult))
                    link(dve.tensor_tensor(col(3), zr, zr, ALU.mult))
                    link(dve.tensor_tensor(col(4), zi, zi, ALU.mult))
                    link(dve.tensor_tensor(zr, col(3), col(4), ALU.subtract))
                    link(dve.tensor_copy(zi, col(5)))
                    m *= 2
                link(dve.memset(row[:, :], 0.0))
                kk = row[:, P - 1:2 * P - 1]
                link(dve.tensor_reduce(kk, re.rearrange("p n l -> p l n"), X, ALU.add))
                link(dve.tensor_scalar(kk, kk, 2.0, None, ALU.mult))
                link(dve.tensor_scalar(kk[:, 0:1], kk[:, 0:1], skip, None, ALU.add))
                dve.tensor_copy(row[:, 2 * P - 1:2 * P], row[:, 0:1]).then_inc(finished.sem, 1)
                chain.per = chain.each = link.n


def affine(k, target, g_dram, b_dram):
    nc = k.nc
    with ExitStack() as ctx:
        gr = k.sb("af_g", [P, P], ctx=ctx)
        br = k.sb("af_b", [P, P], ctx=ctx)
        loaded = k.sig("dma_landed", 2)
        chain = k.sig("dve_step", 2)
        with nc.Block() as block:
            @block.sync
            def _(sp):
                sp.dma_start(gr[:, :], g_dram.partition_broadcast(P)).then_inc(loaded.sem, 16)
                sp.dma_start(br[:, :], b_dram.partition_broadcast(P)).then_inc(loaded.sem, 16)

            @block.vector
            def _(dve):
                link = Chain(dve, chain)
                dve.wait_ge(loaded.sem, loaded.upto(2))
                for row, op in ((gr, ALU.mult), (br, ALU.add)):
                    link(dve.tensor_tensor(target[:, :, :], target[:, :, :], bc(row[:, :].unsqueeze(1), [P, B, P]), op))


def film_rows(k, block_dve, link, mg, brow, film):
    dve = block_dve
    link(dve.tensor_scalar(film[:, :], brow[:, :], mg, None, ALU.mult))
    link(dve.tensor_scalar(film[:, 0:P], film[:, 0:P], 1.0, None, ALU.add))


def sparse_attention(k, ww, wide):
    nc = k.nc
    H, DH, TOP = 4, 32, 32
    W = H * TG
    with ExitStack() as ctx:
        def sb(name, shape, dt=F32):
            return k.sb("sa_" + name, shape, dt, ctx=ctx)

        w = sb("w", [P, 3, P])
        wf = sb("wf", [P, 2 * P])
        brow = sb("brow", [P, 2 * P])
        film = sb("film", [P, 2 * P])
        mg = sb("mg", [P, 1])
        vm = sb("vm", [P, B * NK], U8)
        tm8 = sb("tm8", [P, B], U8)
        tm = sb("tm", [P, B])
        xT = sb("xT", [P, TG * P])
        kv = sb("kv", [P, TG * NK])
        q_sb = sb("q", [P, TG * P])
        k_sb = sb("k", [P, TG * NK])
        v_sb = sb("v", [P, TG, P])
        mb = sb("mb", [P, TG * NK])
        sm = sb("sm", [P, W, NK])
        wk = sb("wk", [P, W, NK])
        m0 = sb("m0", [P, W, 8])
        m8 = sb("m8", [P, W, 8])
        pad = sb("pad", [P, 1])
        rec = sb("rec", [P, W])
        av = sb("av", [P, TG, NK])
        aT = sb("aT", [P, TG * P])
        cT = sb("cT", [P, TG * P])
        fs = sm[:, :, :].rearrange("p w n -> p (w n)")[:, 0:TG * 2 * P].rearrange("p (t c) -> p t c", t=TG)

        R = G
        NL = 6
        loaded = k.sig("dma_landed", NL)
        setup = k.sig("setup_step", 3)
        ready = k.sig("x_ready", 1, R)
        q_ps, k_ps, v_ps = (k.sig(f"{n}_made", 1, R) for n in "qkv")
        q_in, k_in, v_in = (k.sig(f"{n}_in_sbuf", 1, R) for n in "qkv")
        s_ps = k.sig("scores_made", 1, R)
        s_in = k.sig("scores_masked", 1, R)
        CH = 21
        chain = k.sig("dve_step", CH, R)
        shifted = k.sig("shifted", 1, R)
        ex = k.sig("exp_done", 1, R)
        mean = k.sig("probs_averaged", 1, R)
        t_ps = k.sig("probs_turned", 1, R)
        t_in = k.sig("probsT_in_sbuf", 1, R)
        c_ps = k.sig("c_made", 1, R)
        c_in = k.sig("c_in_sbuf", 1, R)
        f_ps = k.sig("film_made", 1, R)
        f_in = k.sig("film_read", 1, R)
        with nc.Block() as block:
            @block.sync
            def _(sp):
                for to, of in ((w[:, :, :], ww["sa_w"]), (wf[:, :], ww["film_in"]),
                               (brow[:, :], ww["b_film_in"].partition_broadcast(P)),
                               (mg[:, :], ww["mod_gate"].partition_broadcast(P)),
                               (vm[:, :], k.d["vision_mask"].partition_broadcast(P)),
                               (tm8[:, :], k.d["text_mask"]), ):
                    sp.dma_start(to, of).then_inc(loaded.sem, 16)

            def each(eng):
                with eng.Fori(0, G) as g:
                    yield g

            @block.gpsimd
            def _(pool):
                for g in each(pool):
                    pool.wait_ge(v_ps.sem, v_ps.upto(0, g))
                    pool.tensor_copy(xT[:, :], k.nxT_all[:, ds(g * (TG * P), TG * P)])
                    pool.tensor_copy(kv[0:CK, :], k.ctxT[:, ds(g * (TG * NK), TG * NK)]).then_inc(ready.sem, 1)

            @block.tensor
            def _(pe):
                pe.wait_ge(loaded.sem, loaded.upto(NL))
                for g in each(pe):
                    pe.wait_ge(ready.sem, ready.upto(1, g))
                    pe.wait_ge(t_in.sem, t_in.upto(0, g))
                    pe.matmul(k.ps[:, 4, :], w[:, 0, :], xT[:, :], start=True, stop=True).then_inc(q_ps.sem, 1)
                    pe.wait_ge(k_in.sem, k_in.upto(0, g))
                    pe.matmul(k.ps[:, 5, 0:TG * NK], w[0:CK, 1, :], kv[0:CK, :], start=True,
                              stop=True).then_inc(k_ps.sem, 1)
                    pe.wait_ge(v_in.sem, v_in.upto(0, g))
                    for t in range(TG):
                        mm = pe.matmul(k.ps[0:NK, 6, t * P:(t + 1) * P], kv[0:CK, t * NK:(t + 1) * NK], w[0:CK, 2, :],
                                       start=True, stop=True)
                    mm.then_inc(v_ps.sem, 1)
                    pe.wait_ge(q_in.sem, q_in.upto(1, g))
                    pe.wait_ge(k_in.sem, k_in.upto(1, g))
                    pe.wait_ge(f_in.sem, f_in.upto(0, g))
                    for h in range(H):
                        rows = slice(DH * h, DH * (h + 1))
                        for t in range(TG):
                            mm = pe.matmul(k.ps[:, h, t * NK:(t + 1) * NK], q_sb[rows, t * P:(t + 1) * P],
                                           k_sb[rows, t * NK:(t + 1) * NK], start=True, stop=True)
                    mm.then_inc(s_ps.sem, 1)
                    pe.wait_ge(mean.sem, mean.upto(1, g))
                    for t in range(TG):
                        mm = pe.transpose(k.ps[0:NK, 4, t * P:(t + 1) * P], av[:, t, :], k.ident[:, :])
                    mm.then_inc(t_ps.sem, 1)
                    pe.wait_ge(t_in.sem, t_in.upto(1, g))
                    pe.wait_ge(v_in.sem, v_in.upto(1, g))
                    pe.wait_ge(c_in.sem, c_in.upto(0, g))
                    for t in range(TG):
                        mm = pe.matmul(k.ps[:, 7, t * P:(t + 1) * P], v_sb[0:NK, t, :], aT[0:NK, t * P:(t + 1) * P],
                                       start=True, stop=True)
                    mm.then_inc(c_ps.sem, 1)
                    pe.wait_ge(c_in.sem, c_in.upto(1, g))
                    for t in range(TG):
                        mm = pe.matmul(k.ps[:, t // 2, (t % 2) * 2 * P:(t % 2 + 1) * 2 * P], cT[:, t * P:(t + 1) * P],
                                       wf[:, :], start=True, stop=True)
                    mm.then_inc(f_ps.sem, 1)

            @block.scalar
            def _(act):
                for g in each(act):
                    act.wait_ge(q_ps.sem, q_ps.upto(1, g))
                    act.mul(q_sb[:, :], k.ps[:, 4, :], float(DH) ** -0.5).then_inc(q_in.sem, 1)
                    act.wait_ge(k_ps.sem, k_ps.upto(1, g))
                    act.copy(k_sb[:, :], k.ps[:, 5, 0:TG * NK]).then_inc(k_in.sem, 1)
                    act.wait_ge(v_ps.sem, v_ps.upto(1, g))
                    act.copy(v_sb[0:NK, :, :].rearrange("p t c -> p (t c)"), k.ps[0:NK, 6, :]).then_inc(v_in.sem, 1)
                    act.wait_ge(shifted.sem, shifted.upto(1, g))
                    act.activation(sm[:, :, :], sm[:, :, :], ACT.Exp).then_inc(ex.sem, 1)
                    act.wait_ge(t_ps.sem, t_ps.upto(1, g))
                    act.copy(aT[0:NK, :], k.ps[0:NK, 4, :]).then_inc(t_in.sem, 1)
                    act.wait_ge(c_ps.sem, c_ps.upto(1, g))
                    act.copy(cT[:, :], k.ps[:, 7, :])
                    act.copy(k.nxT_all[:, ds(g * (TG * P), TG * P)], k.ps[:, 7, :]).then_inc(c_in.sem, 1)

            @block.vector
            def _(dve):
                dve.wait_ge(loaded.sem, loaded.upto(NL))
                first = Chain(dve, setup)
                first(dve.tensor_copy(tm[:, :], tm8[:, :]))
                film_rows(k, dve, first, mg[:, :], brow, film)
                link = Chain(dve, chain)
                for g in each(dve):
                    link(dve.tensor_scalar(mb[:, :], vm[:, ds(g * (TG * NK), TG * NK)], 1.0, -NEG, ALU.subtract,
                                           ALU.mult), g)
                    dve.wait_ge(s_ps.sem, s_ps.upto(1, g))
                    for h in range(H):
                        last = dve.tensor_tensor(sm[:, TG * h:TG * (h + 1), :].rearrange("p t n -> p (t n)"),
                                                 k.ps[:, h, 0:TG * NK], mb[:, :], ALU.add)
                    last.then_inc(s_in.sem, 1)
                    dve.wait_ge(s_in.sem, s_in.upto(1, g))
                    for n in range(TOP // 8):
                        top = m8 if n else m0
                        dve.memset(pad[:, :], 0.0)
                        src = wk if n else sm
                        for i in range(W):
                            last = dve.max(top[:, i, :], src[:, i, :])
                        link(last, g)
                        dve.memset(pad[:, :], 0.0)
                        for i in range(W):
                            last = dve.match_replace(wk[:, i, :], top[:, i, :], src[:, i, :], TAKEN)
                        link(last, g)
                    dve.tensor_tensor(sm[:, :, :], sm[:, :, :], bc(m0[:, :, 0:1], [P, W, NK]),
                                      ALU.subtract).then_inc(shifted.sem, 1)
                    dve.wait_ge(ex.sem, ex.upto(1, g))
                    link(dve.scalar_tensor_tensor(sm[:, :, :], wk[:, :, :], TAKEN, sm[:, :, :], ALU.is_equal,
                                                  ALU.mult), g)
                    link(dve.tensor_reduce(rec[:, :], sm[:, :, :], X, ALU.add), g)
                    link(dve.reciprocal(rec[:, :], rec[:, :]), g)
                    r2 = rec[:, :].rearrange("p (h t) -> p h t", h=H)
                    link(dve.tensor_tensor(r2, r2, bc(tm[:, ds(g * TG, TG)].unsqueeze(1), [P, H, TG]), ALU.mult), g)
                    link(dve.tensor_scalar(rec[:, :], rec[:, :], 1.0 / H, None, ALU.mult), g)
                    link(dve.tensor_tensor(sm[:, :, :], sm[:, :, :], bc(rec[:, :].unsqueeze(2), [P, W, NK]),
                                           ALU.mult), g)
                    dve.tensor_reduce(av[:, :, :], sm[:, :, :].rearrange("p (h t) n -> p t n h", h=H), X,
                                      ALU.add).then_inc(mean.sem, 1)
                    dve.wait_ge(f_ps.sem, f_ps.upto(1, g))
                    for a in range(2):
                        last = dve.scalar_tensor_tensor(fs[:, 2 * a:2 * a + 2, :],
                                                        k.ps[:, a, :].rearrange("p (t c) -> p t c", t=2), mg[:, :],
                                                        bc(film[:, :].unsqueeze(1), [P, 2, 2 * P]), ALU.mult, ALU.add)
                    last.then_inc(f_in.sem, 1)
                    dve.wait_ge(f_in.sem, f_in.upto(1, g))
                    xw = wide[:, ds(g * TG, TG), :]
                    link(dve.tensor_tensor(xw, xw, fs[:, :, 0:P], ALU.mult), g)
                    link(dve.tensor_tensor(xw, xw, fs[:, :, P:2 * P], ALU.add), g)
                    while link.n < CH:
                        link(dve.tensor_copy(rec[:, 0:1], rec[:, 0:1]), g)
                    link.end_round()


def reverse_tokens(k, wide):
    nc = k.nc
    with ExitStack() as ctx:
        rev = k.sb("rv", [P, P], ctx=ctx)
        loaded = k.sig("dma_landed", 1)
        turned = k.sig("turned", 1, G)
        copied = k.sig("copied", 1, G)
        with nc.Block() as block:
            @block.sync
            def _(sp):
                sp.dma_start(rev[:, :], k.d["reversed"]).then_inc(loaded.sem, 16)

            @block.tensor
            def _(pe):
                pe.wait_ge(loaded.sem, loaded.upto(1))
                for _, r, u, g in rounds(pe):
                    if u == 0:
                        pe.wait_ge(copied.sem, copied.upto(0, r))
                    pe.matmul(k.ps[:, u, :], rev[:, :], wide[:, ds(g * TG, TG), :].rearrange("p t c -> p (t c)"),
                              start=True, stop=True).then_inc(turned.sem, 1)

            @block.scalar
            def _(act):
                for _, r, u, g in rounds(act):
                    act.wait_ge(turned.sem, turned.upto(1, r))
                    act.copy(wide[:, ds(g * TG, TG), :].rearrange("p t c -> p (t c)"), k.ps[:, u, :]
                             ).then_inc(copied.sem, 1)


def convolve(k, wide, conv_tensor):
    nc = k.nc
    CC = 16
    NC = P // CC
    with ExitStack() as ctx:
        hk = k.sb("cv_h", [P, 2, CC, P], ctx=ctx)
        loaded = [k.sig(f"taps_landed_{i}", 1, NC // 2) for i in range(2)]
        made = k.sig("turned", 1, NC)
        taken_a = k.sig("outs_taken_act", 1, NC)
        taken_d = k.sig("outs_taken_dve", 1, NC)
        with nc.Block() as block:
            @block.sync
            def _(sp):
                for c in range(NC):
                    if c >= 2:
                        sp.wait_ge(made.sem, made.upto(1, c - 2))
                    src = bass.AP(conv_tensor, c * CC * 2 * P, [[1, P], [2 * P, CC], [1, P]])
                    sp.dma_start(hk[:, c % 2], src).then_inc(loaded[c % 2].sem, 16)

            @block.tensor
            def _(pe):
                for c in range(NC):
                    pe.wait_ge(loaded[c % 2].sem, loaded[c % 2].upto(c // 2 + 1))
                    if c >= 2:
                        pe.wait_ge(taken_a.sem, taken_a.upto(1, c - 2))
                        pe.wait_ge(taken_d.sem, taken_d.upto(1, c - 2))
                    for i in range(CC):
                        mm = pe.matmul(k.ps[:, 2 * (c % 2) + i // 8, (i % 8) * B:(i % 8 + 1) * B], hk[:, c % 2, i, :],
                                       wide[:, :, c * CC + i], start=True, stop=True)
                    mm.then_inc(made.sem, 1)

            @block.scalar
            def _(act):
                for c in range(NC):
                    act.wait_ge(made.sem, made.upto(1, c))
                    act.copy(wide[:, :, c * CC:c * CC + 8].rearrange("p b d -> p d b"),
                             k.ps[:, 2 * (c % 2), :].rearrange("p (d b) -> p d b", b=B)).then_inc(taken_a.sem, 1)

            @block.vector
            def _(dve):
                for c in range(NC):
                    dve.wait_ge(made.sem, made.upto(1, c))
                    dve.tensor_copy(wide[:, :, c * CC + 8:c * CC + 16].rearrange("p b d -> p d b"),
                                    k.ps[:, 2 * (c % 2) + 1, :].rearrange("p (d b) -> p d b", b=B)
                                    ).then_inc(taken_d.sem, 1)


def modulate_out(k, ww, wide):
    nc = k.nc
    with ExitStack() as ctx:
        wf = k.sb("mo_wf", [P, 2 * P], ctx=ctx)
        brow = k.sb("mo_brow", [P, 2 * P], ctx=ctx)
        film = k.sb("mo_film", [P, 2 * P], ctx=ctx)
        mg = k.sb("mo_mg", [P, 1], ctx=ctx)
        cT = k.sb("mo_cT", [P, 2, TG * P], ctx=ctx)
        fs = k.sb("mo_fs", [P, TG, 2 * P], ctx=ctx)
        loaded = k.sig("dma_landed", 3)
        setup = k.sig("setup_step", 2)
        ready = k.sig("x_ready", 1, G)
        f_ps = k.sig("film_made", 1, G)
        f_in = k.sig("film_read", 1, G)
        chain = k.sig("dve_step", 3, G)
        with nc.Block() as block:
            @block.sync
            def _(sp):
                for to, of in ((wf[:, :], ww["film_out"]), (brow[:, :], ww["b_film_out"].partition_broadcast(P)),
                               (mg[:, :], ww["mod_gate"].partition_broadcast(P))):
                    sp.dma_start(to, of).then_inc(loaded.sem, 16)

            @block.gpsimd
            def _(pool):
                for _, r, u, g in rounds(pool):
                    if u == 0:
                        pool.wait_ge(f_ps.sem, f_ps.upto(0, r))
                    pool.tensor_copy(cT[:, u], k.nxT_all[:, ds(g * (TG * P), TG * P)]).then_inc(ready.sem, 1)

            @block.tensor
            def _(pe):
                pe.wait_ge(loaded.sem, loaded.upto(3))
                for _, r, u, g in rounds(pe):
                    pe.wait_ge(ready.sem, ready.upto(1, r))
                    if u == 0:
                        pe.wait_ge(f_in.sem, f_in.upto(0, r))
                    for t in range(TG):
                        mm = pe.matmul(k.ps[:, 2 * u + t // 2, (t % 2) * 2 * P:(t % 2 + 1) * 2 * P],
                                       cT[:, u, t * P:(t + 1) * P], wf[:, :], start=True, stop=True)
                    mm.then_inc(f_ps.sem, 1)

            @block.vector
            def _(dve):
                dve.wait_ge(loaded.sem, loaded.upto(3))
                first = Chain(dve, setup)
                film_rows(k, dve, first, mg[:, :], brow, film)
                link = Chain(dve, chain)
                for _, r, u, g in rounds(dve):
                    dve.wait_ge(f_ps.sem, f_ps.upto(1, r))
                    for a in range(2):
                        last = dve.scalar_tensor_tensor(fs[:, 2 * a:2 * a + 2, :],
                                                        k.ps[:, 2 * u + a, :].rearrange("p (t c) -> p t c", t=2),
                                                        mg[:, :], bc(film[:, :].unsqueeze(1), [P, 2, 2 * P]),
                                                        ALU.mult, ALU.add)
                    last.then_inc(f_in.sem, 1)
                    dve.wait_ge(f_in.sem, f_in.upto(1, r))
                    xw = wide[:, ds(g * TG, TG), :]
                    link(dve.tensor_tensor(xw, xw, fs[:, :, 0:P], ALU.mult), r)
                    link(dve.tensor_tensor(xw, xw, fs[:, :, P:2 * P], ALU.add), r)
                    link(dve.tensor_tensor(xw, xw, k.nx_all[:, ds(g * TG, TG), :], ALU.add), r)
                    link.end_round()


def add_scaled(k, src, gate_col):
    chain = k.sig("dve_step", 1)
    with k.nc.Block() as block:
        @block.vector
        def _(dve):
            link = Chain(dve, chain)
            flat = k.x_all[:, :, :].rearrange("p b c -> p (b c)")
            link(dve.scalar_tensor_tensor(flat, src[:, :, :].rearrange("p b c -> p (b c)"), gate_col, flat,
                                          ALU.mult, ALU.add))


def load_context(k):
    loaded = k.sig("dma_landed", 1)
    with k.nc.Block() as block:
        @block.sync
        def _(sp):
            sp.dma_start(k.ctxT[:, :], k.d["ctxT"]).then_inc(loaded.sem, 16)
            sp.wait_ge(loaded.sem, loaded.upto(1))


def store_output(k, out):
    stored = k.sig("dma_stored", 4)
    with k.nc.Block() as block:
        @block.sync
        def _(sp):
            for q in range(4):
                s = slice(16 * q, 16 * q + 16)
                sp.dma_start(out[s].rearrange("b s c -> s b c"), k.x_all[:, s, :]).then_inc(stored.sem, 16)
            sp.wait_ge(stored.sem, stored.upto(4))


def build(nc, d, out, stages=range(1, 9)):
    conv = nc.dram_tensor("conv_rows", [P, 2 * P], F32, kind="Internal")
    with ExitStack() as ctx:
        k = Kernel(nc, d, ctx)
        k.rank_i = k.sb("rank_i", [P, 8], I32)
        tgc = [k.tg[:, i:i + 1] for i in range(8)]

        def att(name):
            return {"w": d[name + "_w"], "bcol": d[name + "_bcol"], "rows": d[name + "_rows"]}

        def exp_w(name, up):
            r = {"w1": d[name + "_w1"], "w2": d[name + "_w2"], "bcol": d[name + "_bcol"], "brow": d[name + "_brow"]}
            if up:
                r["w3"] = d[name + "_w3"]
            return r

        prime_signals(k)
        load_inputs(k)
        if 3 in stages:
            ssm_kernel(k, d, conv.ap())
        k.ctxT = k.sb("ctxT", [CK, B * NK])
        load_context(k)

        if 1 in stages:
            layer_norm(k, k.x_all, k.nx_all, P)
            transpose_rows(k)
            narrow_attention(k, 1, NK, 8 ** -0.5, att("a0"), tgc[0], clip=10000.0)
        if 2 in stages:
            with ExitStack() as inner:
                gate_arrays(k, inner)
                layer_norm(k, k.x_all, k.nx_all, P)
                with ExitStack() as inmost:
                    h_all = k.sb("h_all", [P, B, 64], ctx=inmost)
                    transpose_rows(k, (d["m0_rw1"], d["m0_rb1"], 64, h_all))
                    layer_norm(k, h_all, h_all, 64)
                    router_logits(k, h_all, 64, {n: d["m0_r_" + n] for n in ("w2", "b2", "g", "b")})
                top_two_gates(k, tgc[4])
                add_gated_rows(k, d["m0_rows_diag"])
                narrow_attention(k, 8, P, 8 ** -0.5, att("m0"), None, gated=True)
        if 3 in stages:
            layer_norm(k, k.x_all, k.nx_all, P)
            transpose_rows(k)
            with ExitStack() as inner:
                wide = k.sb("wide", [P, B, P], ctx=inner)
                layer_norm(k, k.nx_all, wide, P)
                affine(k, wide, d["g_norm_in"], d["b_norm_in"])
                sparse_attention(k, d, wide)
                reverse_tokens(k, wide)
                convolve(k, wide, conv)
                modulate_out(k, d, wide)
                layer_norm(k, wide, k.nx_all, P)
                affine(k, k.nx_all, d["g_ffn_ln"], d["b_ffn_ln"])
                transpose_rows(k)
                experts(k, 1, 4, ACT.Gelu, exp_w("mlp", False), wide, up=False, gate_col=k.cols[:, 1:2], gated=False)
                layer_norm(k, wide, k.nx_all, P)
                affine(k, k.nx_all, d["g_norm_out"], d["b_norm_out"])
                add_scaled(k, k.nx_all, tgc[1])
        if 4 in stages:
            with ExitStack() as inner:
                gate_arrays(k, inner)
                layer_norm(k, k.x_all, k.nx_all, P)
                transpose_rows(k, (d["m1_rw"], d["m1_rb"], 8, k.logits))
                top_two_gates(k, tgc[5], shared=2)
                experts(k, 5, 1, ACT.Silu, exp_w("m1", True), k.x_all, up=True, pair=True)
        if 5 in stages:
            layer_norm(k, k.x_all, k.nx_all, P)
            transpose_rows(k)
            attention(k, 2, 8, NK, 64 ** -0.5, att("a2"), tgc[2])
        if 6 in stages:
            with ExitStack() as inner:
                gate_arrays(k, inner)
                layer_norm(k, k.x_all, k.nx_all, P)
                transpose_rows(k, (d["m2_rw"], d["zero_row"], 8, k.logits))
                top_two_gates(k, tgc[6], plus=1e-8)
                add_gated_rows(k, d["m2_rows_diag"])
                experts(k, 8, 2, ACT.Silu, exp_w("m2", True), k.x_all, up=True)
        if 7 in stages:
            layer_norm(k, k.x_all, k.nx_all, P)
            transpose_rows(k)
            attention(k, 2, 8, NK, 64 ** -0.5, att("a3"), tgc[3])
        if 8 in stages:
            with ExitStack() as inner:
                gate_arrays(k, inner)
                layer_norm(k, k.x_all, k.nx_all, P)
                transpose_rows(k, (d["m3_rw"], d["zero_row"], 8, k.logits))
                top_two_gates(k, tgc[7], least=1e-9, capacity=2 * B * P // 8)
                experts(k, 8, 4, ACT.Gelu, exp_w("m3", False), k.x_all, up=False)
        store_output(k, out)


def layouts(i):
    import numpy as np
    a = {n: np.asarray(v) for n, v in i.items()}
    f = np.float32
    d = {}
    d["x"] = a["x"]
    d["ctxT"] = np.transpose(a["ctx_768"], (2, 0, 1)).reshape(CK, B * NK)
    d["ident"] = np.eye(P, dtype=f)
    d["reversed"] = np.eye(P, dtype=f)[::-1]
    d["ones"] = np.ones((P, P), f)
    d["before"] = np.triu(np.ones((P, P), f), 1)
    d["zero_row"] = np.zeros((8,), f)
    cols = np.zeros((P, 32), f)
    cols[:, 0] = EPS
    cols[:, 1] = 1.0
    for h in range(16):
        cols[:, 16 + h] = np.arange(P) // 8 == h
    d["cols"] = cols
    d["g_rows"] = np.concatenate([a["g_xattn"], a["g_ffn"]])
    d["text_mask"] = a["mask_BxS_bf1"].view(np.uint8).T
    d["vision_mask"] = a["mask_BxS2_bf1"].view(np.uint8).reshape(-1)

    def attn(name, wq, wk, wv, wo, bq=None, bk=None, bv=None, bo=None):
        E = wq.shape[0]
        w = np.zeros((E, P, 4, P), f)
        for n, m in enumerate((wq, wk, wv, wo)):
            w[:, :m.shape[1], n, :] = m
        d[name + "_w"] = w
        bcol = np.zeros((E, P, 2), f)
        rows = np.zeros((E, 2, P), f)
        for to, b in ((bcol[:, :, 0], bq), (bcol[:, :, 1], bk), (rows[:, 0], bv)):
            if b is not None:
                to[:] = b
        if bo is not None:
            rows[:len(bo), 1] = bo
        d[name + "_bcol"], d[name + "_rows"] = bcol, rows

    L = "L0_xattn_"
    attn("a0", *(a[L + n][None] for n in ("Wq", "Wk", "Wv", "Wo", "bq", "bk", "bv", "bo")))
    L = "L0_ffn_"
    attn("m0", *(np.transpose(a[L + n], (0, 2, 1)) for n in ("qW", "kW", "vW", "oW")),
         *(a[L + n] for n in ("qb", "kb", "vb", "ob")))

    def cut(w):
        return np.transpose(w.reshape(w.shape[0], 8, P), (1, 0, 2))

    attn("a2", cut(a["L2_xattn_Wq"]), cut(a["L2_xattn_Wk"]), cut(a["L2_xattn_Wv"]),
         a["L2_xattn_Wo"].reshape(8, P, P), bo=a["L2_xattn_bo"][None])
    kv = a["L3_xattn_w_kv"]
    attn("a3", cut(a["L3_xattn_w_q"]), cut(kv[:, :1024]), cut(kv[:, 1024:]), a["L3_xattn_w_out"].reshape(8, P, P),
         bo=a["L3_xattn_b_out"][None])

    L = "L0_ffn_"
    d["m0_rw1"], d["m0_rb1"] = a[L + "rW1"].T, a[L + "rb1"]
    d["m0_r_w2"], d["m0_r_b2"], d["m0_r_g"], d["m0_r_b"] = a[L + "rW2"].T, a[L + "rb2"], a[L + "ln_g"], a[L + "ln_b"]

    L = "L1_xattn_"
    w = np.zeros((P, 3, P), f)
    for n, m in enumerate(("Wq", "Wk", "Wv")):
        w[:a[L + m].shape[0], n] = a[L + m]
    d["sa_w"] = w
    d["film_in"], d["b_film_in"] = a[L + "W_film_in"], a[L + "b_film_in"]
    d["film_out"], d["b_film_out"] = a[L + "W_film_out"], a[L + "b_film_out"]
    d["mod_gate"] = a[L + "mod_gate"].reshape(1)
    d["g_norm_in"], d["b_norm_in"] = a[L + "g_norm_in"], a[L + "b_norm_in"]
    d["g_ffn_ln"], d["b_ffn_ln"] = a[L + "g_ffn"], a[L + "b_ffn"]
    d["g_norm_out"], d["b_norm_out"] = a[L + "g_norm_out"], a[L + "b_norm_out"]
    d["ssm"] = np.concatenate([a[L + n] for n in ("A_re", "A_im", "C_re", "C_im")]
                              + [a[L + "log_dt"][:, None], a[L + "D_skip"][:, None]], axis=1)

    def diagonal(rows):
        out = np.zeros((16, 8, 16, P), f)
        for s in range(16):
            out[s, :, s] = rows
        return out.reshape(P, 16, P)

    d["m0_rows_diag"] = diagonal(a["L0_ffn_ob"])
    d["m2_rows_diag"] = diagonal(a["L2_ffn_b_out"])

    def moe(name, w1, w2, w3=None, b1=None, b3=None, b2=None):
        E, _, M = w1.shape
        MC = M // P
        d[name + "_w1"] = w1
        d[name + "_w2"] = np.transpose(w2.reshape(E, MC, P, P), (0, 2, 1, 3))
        if w3 is not None:
            d[name + "_w3"] = w3
        bcol = np.zeros((E, P, 2 * MC), f)
        for n, b in enumerate((b1, b3)):
            if b is not None:
                bcol[:, :, n * MC:(n + 1) * MC] = np.transpose(b.reshape(E, MC, P), (0, 2, 1))
        d[name + "_bcol"] = bcol
        d[name + "_brow"] = b2 if b2 is not None else np.zeros((E, P), f)

    moe("mlp", a[L + "W1"][None], a[L + "W2"][None], b1=a[L + "b1"][None], b2=a[L + "b2"][None])
    L = "L1_ffn_"
    w1, w3, w2 = (np.concatenate([a[L + "routed_" + n], a[L + "shared_" + n]]) for n in ("w1", "w3", "w2"))

    def two(w):
        return np.transpose(w.reshape(5, 2, P, 64), (0, 2, 1, 3)).reshape(5, P, P)

    moe("m1", two(w1), w2.reshape(5, P, P), two(w3))
    d["m1_rw"], d["m1_rb"] = a[L + "router_w"], a[L + "router_b"]
    L = "L2_ffn_"
    moe("m2", a[L + "W_gate"], a[L + "W_out"], a[L + "W_up"], a[L + "b_gate"], a[L + "b_up"], a[L + "b_out"])
    d["m2_rw"] = a[L + "W_router"]
    L = "L3_ffn_"
    moe("m3", a[L + "w_gate"], a[L + "w_down"])
    d["m3_rw"] = a[L + "wg"]
    return {n: np.ascontiguousarray(v) for n, v in d.items()}


STAGES = range(1, 9)


def kernel(**inputs):
    import concourse.bacc as bacc
    from concourse.bass_utils import run_bass_kernel_spmd as run

    nc = bacc.Bacc("TRN2", target_bir_lowering=False, num_devices=1)
    arrays, dram = {}, {}
    for name, v in layouts(inputs).items():
        arrays["in_" + name] = v
        dram[name] = nc.dram_tensor("in_" + name, v.shape, mybir.dt.from_np(v.dtype), kind="ExternalInput").ap()
    out = nc.dram_tensor("out_0", (B, P, P), F32, kind="ExternalOutput").ap()
    build(nc, dram, out, STAGES)
    return run(nc, [arrays], core_ids=[0]).results[0]["out_0"]
```

```python
from contextlib import ExitStack

import concourse.bass as bass
from concourse import mybir

ALU = mybir.AluOpType
ACT = mybir.ActivationFunctionType
F32 = mybir.dt.float32
I32 = mybir.dt.int32
U8 = mybir.dt.uint8
X = mybir.AxisListType.X
ds = bass.ds

P = 128
B = 64
NK = 120
CK = 96
TG = 4
G = B // TG
EPS = 1e-5
NEG = -3e38
TAKEN = -3.3e38
PRIMED = 36
MAGIC = 12582912.0


SIGNALS = """
    dma_landed act_step dve_step centred squared squares_summed
    rooted staged turned copied stored routed
    routes_taken x_ready scores_made max_found exp_done probs_turned
    outputs_made sums_inverted outputs_scaled outputs_turned y_made y_added
    gates_copied scores_clipped ones_column_set h1_made h3_made h1_activated
    hidden_in_sbuf chosen shifted counted dma_stored angles_ready
    sines_done kernel_ready setup_step scores_masked probs_averaged c_made
    c_in_sbuf film_made film_read outs_taken_act outs_taken_dve pool_step
    columns_copied probs_summed probs_scaled weights_copied wo_copied k_masked_dve k_masked_pool outputs_copied outputs_turned_back
    probsT_in_sbuf outputsT_in_sbuf q_made k_made v_made q_in_sbuf k_in_sbuf v_in_sbuf taps_landed_0 taps_landed_1
""".split()
FROM_DMA = ("dma_landed", "dma_stored", "taps_landed_0", "taps_landed_1")


class Signal:

    def __init__(self, sem, step=1):
        self.sem, self.step, self.base, self.per = sem, step, PRIMED, 0

    def stage(self, per, rounds=1, ahead=0):
        self.base += self.per
        self.each, self.per = per, per * rounds + ahead
        return self

    def upto(self, n, r=0):
        return (self.base + n) * self.step + r * (self.each * self.step)


class Chain:

    def __init__(self, eng, steps):
        self.eng, self.steps, self.n = eng, steps, 0

    def __call__(self, instruction, r=0):
        self.n += 1
        instruction.then_inc(self.steps.sem, 1)
        self.eng.wait_ge(self.steps.sem, self.steps.upto(self.n, r))

    def end_round(self):
        assert self.n == self.steps.each, (self.n, self.steps.each)
        self.n = 0


class Kernel:
    def __init__(self, nc, dram, ctx):
        self.nc, self.d, self.ctx = nc, dram, ctx
        self.events = {n: Signal(ctx.enter_context(nc.semaphore(n)), 16 if n in FROM_DMA else 1) for n in SIGNALS}
        self.names = {}
        sb = self.sb
        self.x_all = sb("x_all", [P, B, P])
        self.nx_all = sb("nx_all", [P, B, P])
        self.nxT_all = sb("nxT_all", [P, B * P])
        self.ident = sb("ident", [P, P])
        self.ones = sb("ones", [P, P])
        self.cols = sb("cols", [P, 32])
        self.rank = sb("rank", [P, 8])
        self.tg = sb("tg", [P, 8])
        self.ps = ctx.enter_context(nc.psum_tensor("ps", [P, 8, 512], F32))

    def sb(self, name, shape, dt=F32, ctx=None):
        self.names[name] = self.names.get(name, 0) + 1
        name = f"{name}_{self.names[name]}" if self.names[name] > 1 else name
        return (ctx or self.ctx).enter_context(self.nc.sbuf_tensor(name, shape, dt))

    def sig(self, name, per, rounds=1, ahead=0):
        return self.events[name].stage(per, rounds, ahead)


def bc(ap, shape):
    return ap.to_broadcast(shape)


def rounds(eng, slots=2):
    with eng.Fori(0, G // slots) as i:
        for u in range(slots):
            yield slots * i + u, u, slots * i + u


def gate_arrays(k, ctx):
    k.logits = k.sb("logits", [P, B, 8], ctx=ctx)
    k.gates = k.sb("gates", [P, 10, B], ctx=ctx)


def prime_signals(k):
    with k.nc.Block() as block:
        @block.sync
        def _(sp):
            for s in k.events.values():
                sp.sem_inc(s.sem, PRIMED * s.step)


def load_inputs(k):
    nc, d = k.nc, k.d
    n = 8
    landed = k.sig("dma_landed", n)
    step = k.sig("act_step", 1)
    made = k.sig("pool_step", 1)
    with nc.Block() as block:
        @block.sync
        def _(sp):
            for q in range(4):
                s = slice(16 * q, 16 * q + 16)
                sp.dma_start(k.x_all[:, s, :], d["x"][s].rearrange("b s c -> s b c")).then_inc(landed.sem, 16)
            sp.dma_start(k.ident[:, :], d["ident"]).then_inc(landed.sem, 16)
            sp.dma_start(k.ones[:, :], d["ones"]).then_inc(landed.sem, 16)
            sp.dma_start(k.cols[:, :], d["cols"]).then_inc(landed.sem, 16)
            sp.dma_start(k.tg[:, :], d["g_rows"].partition_broadcast(P)).then_inc(landed.sem, 16)

        @block.gpsimd
        def _(pool):
            pool.iota(k.rank_i[:, :], [[-1, 8]], base=8, channel_multiplier=0).then_inc(made.sem, 1)
            pool.wait_ge(made.sem, made.upto(1))
            pool.tensor_copy(k.rank[:, :], k.rank_i[:, :])

        @block.scalar
        def _(act):
            act.wait_ge(landed.sem, landed.upto(n))
            act.activation(k.tg[:, :], k.tg[:, :], ACT.Tanh).then_inc(step.sem, 1)
            act.wait_ge(step.sem, step.upto(1))


def layer_norm(k, src, dst, n):
    nc = k.nc
    Q = 4
    BQ = B // Q
    with ExitStack() as ctx:
        st = [k.sb(f"ln_{i}", [P, B], ctx=ctx) for i in range(3)]
        sq = k.sb("ln_sq", [P, 2, BQ, n], ctx=ctx)
        total, mean, rstd = st
        chain = k.sig("dve_step", 4 + Q)
        centred = k.sig("centred", Q)
        squared = k.sig("squared", Q)
        summed = k.sig("squares_summed", Q)
        rooted = k.sig("rooted", 1)
        with nc.Block() as block:
            @block.vector
            def _(dve):
                link = Chain(dve, chain)
                link(dve.tensor_reduce(total[:, :], src[:, :, :n], X, ALU.add))
                link(dve.tensor_scalar(mean[:, :], total[:, :], 1.0 / n, None, ALU.mult))
                for q in range(Q):
                    s = slice(BQ * q, BQ * (q + 1))
                    dve.tensor_tensor(dst[:, s, :n], src[:, s, :n], bc(mean[:, s].unsqueeze(2), [P, BQ, n]),
                                      ALU.subtract).then_inc(centred.sem, 1)
                for q in range(Q):
                    dve.wait_ge(squared.sem, squared.upto(q + 1))
                    dve.tensor_reduce(total[:, BQ * q:BQ * (q + 1)], sq[:, q % 2], X, ALU.add).then_inc(summed.sem, 1)
                dve.wait_ge(rooted.sem, rooted.upto(1))
                link(dve.reciprocal(rstd[:, :], mean[:, :]))
                for q in range(Q):
                    s = slice(BQ * q, BQ * (q + 1))
                    link(dve.tensor_tensor(dst[:, s, :n], dst[:, s, :n], bc(rstd[:, s].unsqueeze(2), [P, BQ, n]),
                                           ALU.mult))
                link(dve.tensor_copy(total[:, 0:1], rstd[:, 0:1]))

            @block.scalar
            def _(act):
                for q in range(Q):
                    act.wait_ge(centred.sem, centred.upto(q + 1))
                    if q >= 2:
                        act.wait_ge(summed.sem, summed.upto(q - 1))
                    act.activation(sq[:, q % 2], dst[:, BQ * q:BQ * (q + 1), :n], ACT.Square).then_inc(squared.sem, 1)
                act.wait_ge(summed.sem, summed.upto(Q))
                act.activation(mean[:, :], total[:, :], ACT.Sqrt, bias=k.cols[:, 0:1],
                               scale=1.0 / n).then_inc(rooted.sem, 1)


def normalise_and_turn(k, keep=False, router=None):
    nc = k.nc
    with ExitStack() as ctx:
        stats = k.sb("nt_stats", [P, B, 6], ctx=ctx)
        mean, var, rstd = (k.sb(f"nt_{n}", [P, B], ctx=ctx) for n in ("mean", "var", "rstd"))
        mid = k.sb("nt_centred", [P, 4, TG, P], ctx=ctx)
        rows = k.sb("nt_rows", [P, 4, TG, P], ctx=ctx)
        cols = k.sb("nt_cols", [P, 4, TG * P], ctx=ctx)
        counted = k.sig("counted", 1)
        chain = k.sig("dve_step", 7)
        rooted = k.sig("rooted", 1)
        centred = k.sig("centred", 1, G)
        staged = k.sig("staged", 1, G)
        kept = k.sig("stored", 1, G) if keep else None
        turned = k.sig("turned", 1, G)
        copied = k.sig("copied", 1, G)
        if router:
            in_cols = k.sig("columns_copied", 1, G)
            routed = k.sig("routed", 1, G)
            taken = k.sig("routes_taken", 1, G)
            loaded = k.sig("dma_landed", 2)
            w_dram, b_dram, W, target = router
            w = k.sb("nt_w", [P, W], ctx=ctx)
            b = k.sb("nt_b", [P, W], ctx=ctx)
        with nc.Block() as block:
            if router:
                @block.sync
                def _(sp):
                    sp.dma_start(w[:, :], w_dram).then_inc(loaded.sem, 16)
                    sp.dma_start(b[:, :], b_dram.partition_broadcast(P)).then_inc(loaded.sem, 16)

            @block.vector
            def _(dve):
                link = Chain(dve, chain)
                for sample in range(B):
                    last = dve.bn_stats(stats[:, sample, :], k.x_all[:, sample, :])
                last.then_inc(counted.sem, 1)
                dve.wait_ge(counted.sem, counted.upto(1))
                link(dve.tensor_tensor(var[:, :], stats[:, :, 1], stats[:, :, 4], ALU.subtract))
                link(dve.scalar_tensor_tensor(var[:, :], var[:, :], P / 4.0, var[:, :], ALU.mult, ALU.mult))
                link(dve.tensor_tensor(var[:, :], var[:, :], stats[:, :, 2], ALU.add))
                link(dve.tensor_tensor(mean[:, :], stats[:, :, 1], stats[:, :, 4], ALU.add))
                link(dve.tensor_scalar(mean[:, :], mean[:, :], 0.5, None, ALU.mult))
                link(dve.tensor_tensor(var[:, :], var[:, :], stats[:, :, 5], ALU.add))
                dve.wait_ge(rooted.sem, rooted.upto(1))
                link(dve.reciprocal(rstd[:, :], rstd[:, :]))
                if router:
                    dve.wait_ge(loaded.sem, loaded.upto(2))
                for r, u, g in rounds(dve, slots=4):
                    dve.wait_ge(centred.sem, centred.upto(1, r))
                    if u == 0:
                        dve.wait_ge(turned.sem, turned.upto(0, r))
                    by = bc(rstd[:, ds(g * TG, TG)].unsqueeze(2), [P, TG, P])
                    dve.tensor_tensor(rows[:, u], mid[:, u], by, ALU.mult).then_inc(staged.sem, 1)
                    if keep:
                        dve.wait_ge(staged.sem, staged.upto(1, r))
                        dve.tensor_copy(k.nx_all[:, ds(g * TG, TG), :], rows[:, u]).then_inc(kept.sem, 1)
                    for r, u, g in [(r + v, 3 + v, g + v) for v in range(-3, 1)] if router and u == 3 else ():
                        dve.wait_ge(routed.sem, routed.upto(1, r))
                        dve.tensor_tensor(target[:, ds(g * TG, TG), :],
                                          k.ps[:, 4 + u, 0:TG * W].rearrange("p (t w) -> p t w", w=W),
                                          bc(b[:, :].unsqueeze(1), [P, TG, W]), ALU.add).then_inc(taken.sem, 1)

            @block.gpsimd
            def _(pool):
                pool.wait_ge(chain.sem, chain.upto(6))
                for r, u, g in rounds(pool, slots=4):
                    if u == 0:
                        pool.wait_ge(staged.sem, staged.upto(0, r))
                    pool.tensor_tensor(mid[:, u], k.x_all[:, ds(g * TG, TG), :],
                                       bc(mean[:, ds(g * TG, TG)].unsqueeze(2), [P, TG, P]),
                                       ALU.subtract).then_inc(centred.sem, 1)

            @block.tensor
            def _(pe):
                if router:
                    pe.wait_ge(loaded.sem, loaded.upto(2))
                for r, u, g in rounds(pe, slots=4):
                    pe.wait_ge(staged.sem, staged.upto(1, r))
                    if u == 0:
                        pe.wait_ge(copied.sem, copied.upto(0, r))
                    for t in range(TG):
                        mm = pe.transpose(k.ps[:, u, t * P:(t + 1) * P], rows[:, u, t, :], k.ident[:, :])
                    mm.then_inc(turned.sem, 1)
                    for r, u in [(r + v, 3 + v) for v in range(-3, 1)] if router and u == 3 else ():
                        pe.wait_ge(in_cols.sem, in_cols.upto(1, r))
                        if u == 0:
                            pe.wait_ge(taken.sem, taken.upto(0, r))
                        for t in range(TG):
                            mm = pe.matmul(k.ps[:, 4 + u, t * W:(t + 1) * W], cols[:, u, t * P:(t + 1) * P], w[:, :],
                                           start=True, stop=True)
                        mm.then_inc(routed.sem, 1)

            @block.scalar
            def _(act):
                act.wait_ge(chain.sem, chain.upto(6))
                act.activation(rstd[:, :], var[:, :], ACT.Sqrt, bias=k.cols[:, 0:1],
                               scale=1.0 / P).then_inc(rooted.sem, 1)
                for r, u, g in rounds(act, slots=4):
                    act.wait_ge(turned.sem, turned.upto(1, r))
                    if router:
                        if u == 0:
                            act.wait_ge(routed.sem, routed.upto(0, r))
                        act.copy(cols[:, u], k.ps[:, u, :]).then_inc(in_cols.sem, 1)
                    act.copy(k.nxT_all[:, ds(g * (TG * P), TG * P)], k.ps[:, u, :]).then_inc(copied.sem, 1)


def transpose_rows(k, router=None):
    nc = k.nc
    with ExitStack() as ctx:
        rows = k.sb("tr_rows", [P, 2, TG, P], ctx=ctx)
        cols = k.sb("tr_cols", [P, 2, TG * P], ctx=ctx)
        staged = k.sig("staged", 1, G)
        turned = k.sig("turned", 1, G)
        copied = k.sig("copied", 1, G)
        stored = k.sig("stored", 1, G)
        if router:
            routed = k.sig("routed", 1, G)
            taken = k.sig("routes_taken", 1, G)
            loaded = k.sig("dma_landed", 2)
            w_dram, b_dram, W, target = router
            w = k.sb("tr_w", [P, W], ctx=ctx)
            b = k.sb("tr_b", [P, W], ctx=ctx)
        with nc.Block() as block:
            if router:
                @block.sync
                def _(sp):
                    sp.dma_start(w[:, :], w_dram).then_inc(loaded.sem, 16)
                    sp.dma_start(b[:, :], b_dram.partition_broadcast(P)).then_inc(loaded.sem, 16)

            @block.gpsimd
            def _(pool):
                for r, u, g in rounds(pool):
                    if u == 0:
                        pool.wait_ge(turned.sem, turned.upto(0, r))
                    pool.tensor_copy(rows[:, u], k.nx_all[:, ds(g * TG, TG), :]).then_inc(staged.sem, 1)

            @block.tensor
            def _(pe):
                if router:
                    pe.wait_ge(loaded.sem, loaded.upto(2))
                for r, u, g in rounds(pe):
                    pe.wait_ge(staged.sem, staged.upto(1, r))
                    if u == 0:
                        pe.wait_ge(copied.sem, copied.upto(0, r))
                    for t in range(TG):
                        mm = pe.transpose(k.ps[:, u, t * P:(t + 1) * P], rows[:, u, t, :], k.ident[:, :])
                    mm.then_inc(turned.sem, 1)
                    if router:
                        pe.wait_ge(copied.sem, copied.upto(1, r))
                        if u == 0:
                            pe.wait_ge(taken.sem, taken.upto(0, r))
                        for t in range(TG):
                            mm = pe.matmul(k.ps[:, 2 + u, t * W:(t + 1) * W], cols[:, u, t * P:(t + 1) * P], w[:, :],
                                           start=True, stop=True)
                        mm.then_inc(routed.sem, 1)

            @block.scalar
            def _(act):
                for r, u, g in rounds(act):
                    act.wait_ge(turned.sem, turned.upto(1, r))
                    if u == 0:
                        act.wait_ge(stored.sem, stored.upto(0, r))
                        if router:
                            act.wait_ge(routed.sem, routed.upto(0, r))
                    act.copy(cols[:, u], k.ps[:, u, :]).then_inc(copied.sem, 1)

            @block.vector
            def _(dve):
                if router:
                    dve.wait_ge(loaded.sem, loaded.upto(2))
                for r, u, g in rounds(dve):
                    dve.wait_ge(copied.sem, copied.upto(1, r))
                    dve.tensor_copy(k.nxT_all[:, ds(g * (TG * P), TG * P)], cols[:, u]).then_inc(stored.sem, 1)
                    if router:
                        dve.wait_ge(routed.sem, routed.upto(1, r))
                        dve.tensor_tensor(target[:, ds(g * TG, TG), :],
                                          k.ps[:, 2 + u, 0:TG * W].rearrange("p (t w) -> p t w", w=W),
                                          bc(b[:, :].unsqueeze(1), [P, TG, W]), ALU.add).then_inc(taken.sem, 1)


def narrow_attention(k, E, nk, scale, weights, gate_col, clip=None, gated=False):
    nc = k.nc
    H, DH, DP = 16, 8, 32
    NS = TG * H // 4
    ND, ND_START = 10, 14
    self_attn = nk == P
    ck = P if self_attn else CK
    R = E * G
    SA, ST, SO, SM = 0, 3, 5, 7
    with ExitStack() as ctx:
        xT = k.sb("na_xT", [P, 2, TG * P], ctx=ctx)
        kv = xT if self_attn else k.sb("na_kv", [P, 2, TG * nk], ctx=ctx)
        w_next = k.sb("na_w_next", [P, 5 * P + 2], ctx=ctx)
        w_now = k.sb("na_w", [P, 5 * P + 2], ctx=ctx)
        NQ = 3 * P
        orow_next = k.sb("na_orow_next", [1, P], ctx=ctx)
        orow = k.sb("na_orow", [1, P], ctx=ctx)
        wq, wk, wv = (w_now[:, n * P:(n + 1) * P] for n in range(3))
        vrow, bcol, wo = w_now[:, NQ:4 * P], w_now[:, 4 * P:4 * P + 2], w_now[:, 4 * P + 2:5 * P + 2]
        q_sb = k.sb("na_q", [P, 2, TG * P], ctx=ctx)
        k_all = k.sb("na_k", [P, TG * nk], ctx=ctx)
        k_heads = [k.nx_all[:, :, :].rearrange("p b c -> p (b c)")[:, 0:H * TG * nk],
                   k.sb("na_km", [P, H * TG * nk], ctx=ctx)[:, :]]
        k_heads = [a.rearrange("p (h t n) -> p h t n", h=H, t=TG) for a in k_heads]
        v_sb = k.sb("na_v", [P, 2, TG, H, DH + 1], ctx=ctx)
        clipped = k.sb("na_clip", [P, 3, 4 * nk], ctx=ctx) if clip else None
        negmax = k.sb("na_max", [P, 3, 4], ctx=ctx)
        probs = k.sb("na_p", [P, 2, 4, nk], ctx=ctx)
        pT = k.sb("na_pT", [P, 2, 4 * P], ctx=ctx)
        raw = k.sb("na_raw", [P, 4 * P], ctx=ctx)
        rec = k.sb("na_rec", [P, H], ctx=ctx)
        o_sb = k.sb("na_o", [P, TG, P], ctx=ctx)
        oT = k.sb("na_oT", [P, TG * P], ctx=ctx)
        gcur = k.sb("na_g", [P, TG], ctx=ctx)
        pad = k.sb("na_pad", [P, 3], ctx=ctx)

        loaded = k.sig("dma_landed", 5, E, ahead=5)
        w_in = k.sig("weights_copied", 1, E, ahead=1)
        wo_in = k.sig("wo_copied", 1, E, ahead=1)
        ready = k.sig("x_ready", 1, R, ahead=2)
        q_ps, k_ps, v_ps = (k.sig(f"{n}_made", 1, R, ahead=1) for n in "qkv")
        q_in, k_in, v_in = (k.sig(f"{n}_in_sbuf", 1, R, ahead=1) for n in "qkv")
        masked_d, masked_p = k.sig("k_masked_dve", 1, R, ahead=1), k.sig("k_masked_pool", 1, R, ahead=1)
        s_ps, mx = k.sig("scores_made", NS, R, ahead=2), k.sig("max_found", NS, R, ahead=2)
        ex = k.sig("exp_done", NS, R, ahead=1)
        clp = k.sig("scores_clipped", NS, R, ahead=2) if clip else None
        t_ps, t_in = k.sig("probs_turned", NS, R), k.sig("probsT_in_sbuf", NS, R)
        pv = k.sig("outputs_made", NS, R)
        raw_in = k.sig("outputs_copied", TG, R)
        back = k.sig("outputs_turned_back", TG, R)
        rc, nrm = k.sig("sums_inverted", TG, R), k.sig("outputs_scaled", TG, R)
        ot_ps, ot_in = k.sig("outputs_turned", 1, R), k.sig("outputsT_in_sbuf", 1, R)
        y_ps, added = k.sig("y_made", 1, R), k.sig("y_added", 1, R)
        gsel = k.sig("gates_copied", 1, R) if gated else None
        set_up = k.sig("setup_step", 2)

        def slot(n):
            return (n % 32) % 3, (n - 3 if n % 32 >= 3 else n - 2 if n % 32 < 2 else n - 5)

        def sets(eng, start, body, end):
            def one(e):
                body(e, 0, True, False)
                with eng.Fori(1, G // 2 - 1) as i:
                    body(e, 2 * i, False, False)
                body(e, G - 2, False, True)
                end(e, e * G + (G - 1))
            start()
            if E == 1:
                one(0)
            else:
                with eng.Fori(0, E) as e:
                    one(e)

        def steps(e, g0, first, last):
            for u in range(2):
                for s in range(NS):
                    yield e * G + (g0 + u), g0 + u, u, s, NS * u + s, not (first and u == 0), last and u == 1

        with nc.Block() as block:
            @block.sync
            def _(sp):
                with sp.Fori(0, E + 1) as e:
                    sp.wait_ge(w_in.sem, w_in.upto(0, e))
                    sp.wait_ge(wo_in.sem, wo_in.upto(0, e))
                    src = weights["w"][ds(e, 1)]
                    sp.dma_start(w_next[:, 0:NQ], src[:, :, 0:3, :].rearrange("a p n c -> p (a n c)")
                                 ).then_inc(loaded.sem, 16)
                    sp.dma_start(w_next[:, 4 * P + 2:5 * P + 2], src[:, :, 3:4, :].rearrange("a p n c -> p (a n c)")
                                 ).then_inc(loaded.sem, 16)
                    sp.dma_start(w_next[:, 4 * P:4 * P + 2], weights["bcol"][ds(e, 1)].rearrange("a p n -> p (a n)")
                                 ).then_inc(loaded.sem, 16)
                    sp.dma_start(w_next[:, NQ:4 * P], weights["rows"][ds(e, 1), 0, :].rearrange("a c -> (a c)")
                                 .partition_broadcast(P)).then_inc(loaded.sem, 16)
                    sp.dma_start(orow_next[:, :], weights["rows"][ds(e, 1), 1, :]).then_inc(loaded.sem, 16)

            @block.gpsimd
            def _(pool):
                def carry(n):
                    pool.tensor_tensor(pad[:, n:n + 1], k.cols[:, 0:1], k.cols[:, 0:1], ALU.mult)

                def copy(r, g, u):
                    pool.wait_ge(v_ps.sem, v_ps.upto(1, r - 2))
                    carry(0)
                    last = pool.tensor_copy(xT[:, u], k.nxT_all[:, ds(g * (TG * P), TG * P)])
                    if not self_attn:
                        last = pool.tensor_copy(kv[0:CK, u], k.ctxT[:, ds(g * (TG * nk), TG * nk)])
                    last.then_inc(ready.sem, 1)

                def mask(r, u, first=ND):
                    pool.wait_ge(k_in.sem, k_in.upto(1, r))
                    pool.wait_ge(s_ps.sem, s_ps.upto(0, r - 1))
                    carry(1)
                    for h in range(first, H):
                        last = pool.tensor_scalar(k_heads[u][:, h].rearrange("p t n -> p (t n)"), k_all[:, :],
                                                  k.cols[:, 16 + h:17 + h], None, ALU.mult)
                    last.then_inc(masked_p.sem, 1)

                def start():
                    copy(0, 0, 0)
                    mask(0, 0, ND_START)
                    copy(1, 1, 1)

                def body(e, g0, first, last):
                    for r, g, u, s, n, before, switch in steps(e, g0, first, last):
                        if s == 0:
                            mask(r + 1, 1 - u)
                            copy(r + 2, u if last else g + 2, u)

                sets(pool, start, body, lambda e, r: None)

            @block.tensor
            def _(pe):
                def project_k(r, u, before):
                    pe.wait_ge(ready.sem, ready.upto(1, r))
                    if before:
                        pe.wait_ge(v_in.sem, v_in.upto(0, r))
                    else:
                        pe.wait_ge(added.sem, added.upto(1, r - 2))
                    pe.matmul(k.ps[:, SM, 0:TG * nk], wk[0:ck, :], kv[0:ck, u], start=True,
                              stop=True).then_inc(k_ps.sem, 1)

                def project_q(r, u, before):
                    if before:
                        pe.wait_ge(added.sem, added.upto(1, r - 2))
                    else:
                        pe.wait_ge(k_in.sem, k_in.upto(1, r))
                    pe.matmul(k.ps[:, SM, :], wq, xT[:, u], start=True, stop=True).then_inc(q_ps.sem, 1)

                def project_v(r, u):
                    pe.wait_ge(q_in.sem, q_in.upto(1, r))
                    for t in range(TG):
                        mm = pe.matmul(k.ps[0:nk, SM, t * P:(t + 1) * P], kv[0:ck, u, t * nk:(t + 1) * nk],
                                       wv[0:ck, :], start=True, stop=True)
                    mm.then_inc(v_ps.sem, 1)

                def scores(r0, n, u):
                    b, before = slot(n)
                    s = n % NS
                    r = r0 + n // NS
                    if s == 0:
                        pe.wait_ge(q_in.sem, q_in.upto(1, r))
                        pe.wait_ge(masked_d.sem, masked_d.upto(1, r))
                        pe.wait_ge(masked_p.sem, masked_p.upto(1, r))
                    pe.wait_ge(ex.sem, ex.upto(before + 1, r0))
                    t, rg = divmod(s, 4)
                    pe.matmul(k.ps[:, SA + b, 0:4 * nk].rearrange("p (h n) -> p h n", n=nk),
                              q_sb[:, u, t * P:(t + 1) * P], k_heads[u][:, 4 * rg:4 * rg + 4, t, :], start=True,
                              stop=True).then_inc(s_ps.sem, 1)

                def turn(r, s):
                    pe.wait_ge(ex.sem, ex.upto(s + 1, r))
                    pe.wait_ge(t_in.sem, t_in.upto(s - 1, r))
                    for j in range(4):
                        mm = pe.transpose(k.ps[0:nk, ST + s % 2, j * P:(j + 1) * P], probs[:, s % 2, j, :],
                                          k.ident[:, :])
                    mm.then_inc(t_ps.sem, 1)

                def outputs(r, u, s):
                    t, rg = divmod(s, 4)
                    pe.wait_ge(t_in.sem, t_in.upto(s + 1, r))
                    if s == 0:
                        pe.wait_ge(v_in.sem, v_in.upto(1, r))
                    if rg == 0:
                        pe.wait_ge(nrm.sem, nrm.upto(t - 1, r))
                    for j in range(4):
                        mm = pe.matmul(k.ps[DP * j:DP * j + DH + 1, SO + t % 2, rg * P:(rg + 1) * P],
                                       v_sb[0:nk, u, t, 4 * rg + j, :], pT[0:nk, s % 2, j * P:(j + 1) * P],
                                       start=True, stop=True)
                    mm.then_inc(pv.sem, 1)

                def turn_back(r, t):
                    pe.wait_ge(raw_in.sem, raw_in.upto(t + 1, r))
                    for c in range(4):
                        mm = pe.transpose(k.ps[:, SO + t % 2, c * P:(c + 1) * P], raw[:, c * P:(c + 1) * P], k.ident[:, :])
                    mm.then_inc(back.sem, 1)

                def turn_outputs(r, at_end=False):
                    pe.wait_ge(nrm.sem, nrm.upto(TG, r))
                    if at_end:
                        pe.wait_ge(v_in.sem, v_in.upto(1, r + 1))
                    else:
                        pe.wait_ge(k_in.sem, k_in.upto(1, r + 2))
                    for t in range(TG):
                        mm = pe.transpose(k.ps[:, SM, t * P:(t + 1) * P], o_sb[:, t, :], k.ident[:, :])
                    mm.then_inc(ot_ps.sem, 1)

                def project_out(r):
                    pe.wait_ge(ot_in.sem, ot_in.upto(1, r))
                    for t in range(TG):
                        y = k.ps[:, SM, t * P:(t + 1) * P]
                        if not gated:
                            pe.matmul(y, k.ones[0:1, :], orow[0:1, :], start=True, stop=False)
                        mm = pe.matmul(y, oT[:, t * P:(t + 1) * P], wo, start=gated, stop=True)
                    mm.then_inc(y_ps.sem, 1)

                def start():
                    pe.wait_ge(w_in.sem, w_in.upto(1))
                    project_k(0, 0, True)
                    project_q(0, 0, False)
                    project_v(0, 0)
                    scores(0, 0, 0)
                    scores(0, 1, 0)

                def body(e, g0, first, last):
                    r0 = e * G + g0
                    for r, g, u, s, n, before, switch in steps(e, g0, first, last):
                        scores(r0, n + 2, ((n + 2) // NS) % 2)
                        turn(r, s)
                        if s >= 1:
                            outputs(r, u, s - 1)
                        elif before:
                            outputs(r - 1, 1 - u, NS - 1)
                        if s == 1:
                            if switch:
                                pe.wait_ge(w_in.sem, w_in.upto(2, e))
                            project_k(r + 1, 1 - u, before)
                        if s == 2 and before:
                            turn_back(r - 1, TG - 1)
                        if s == 4 and before:
                            turn_outputs(r - 1)
                        if s == 6 and before:
                            if first:
                                pe.wait_ge(wo_in.sem, wo_in.upto(1, e))
                            project_out(r - 1)
                        if s % 4 == 2 and s > 2:
                            turn_back(r, s // 4 - 1)
                        if s == 9:
                            project_q(r + 1, 1 - u, before)
                        if s == 12:
                            project_v(r + 1, 1 - u)

                def end(e, r):
                    outputs(r, 1, NS - 1)
                    turn_back(r, TG - 1)
                    turn_outputs(r, True)
                    project_out(r)

                sets(pe, start, body, end)

            @block.scalar
            def _(act):
                def exps(r0, n):
                    b, _ = slot(n)
                    act.wait_ge(mx.sem, mx.upto(n + 1, r0))
                    act.wait_ge(t_ps.sem, t_ps.upto(n - 1, r0))
                    for j in range(4):
                        src = clipped[:, b, j * nk:(j + 1) * nk] if clip else \
                            k.ps[:, SA + b, j * nk:(j + 1) * nk]
                        last = act.activation(probs[:, n % 2, j, :], src, ACT.Exp, bias=negmax[:, b, j:j + 1])
                    last.then_inc(ex.sem, 1)

                def fetch(r, s):
                    act.wait_ge(t_ps.sem, t_ps.upto(s + 1, r))
                    act.wait_ge(pv.sem, pv.upto(s - 1, r))
                    act.copy(pT[0:nk, s % 2, :], k.ps[0:nk, ST + s % 2, :]).then_inc(t_in.sem, 1)

                def copy_qkv():
                    act.copy(w_now[:, 0:4 * P + 2], w_next[:, 0:4 * P + 2]).then_inc(w_in.sem, 1)

                def copy_o():
                    act.copy(wo, w_next[:, 4 * P + 2:5 * P + 2])
                    act.copy(orow[:, :], orow_next[:, :]).then_inc(wo_in.sem, 1)

                def start():
                    act.wait_ge(loaded.sem, loaded.upto(5))
                    copy_qkv()
                    copy_o()
                    exps(0, 0)

                def body(e, g0, first, last):
                    r0 = e * G + g0
                    for r, g, u, s, n, before, switch in steps(e, g0, first, last):
                        if s == 0 and switch:
                            act.wait_ge(loaded.sem, loaded.upto(10, e))
                            act.wait_ge(v_in.sem, v_in.upto(1, r))
                            copy_qkv()
                        exps(r0, n + 1)
                        fetch(r, s)

                def end(e, r):
                    act.wait_ge(y_ps.sem, y_ps.upto(1, r))
                    copy_o()

                sets(act, start, body, end)

            @block.vector
            def _(dve):
                def top(r0, n):
                    b, _ = slot(n)
                    dve.wait_ge(s_ps.sem, s_ps.upto(n + 1, r0))
                    src = k.ps[:, SA + b, 0:4 * nk]
                    if clip:
                        dve.tensor_scalar(clipped[:, b], src, clip, -clip, ALU.min, ALU.max).then_inc(clp.sem, 1)
                        dve.wait_ge(clp.sem, clp.upto(n + 1, r0))
                        src = clipped[:, b]
                    dve.tensor_reduce(negmax[:, b], src.rearrange("p (h n) -> p h n", n=nk), X, ALU.max,
                                      negate=True).then_inc(mx.sem, 1)

                def take_k(r):
                    dve.wait_ge(k_ps.sem, k_ps.upto(1, r))
                    dve.wait_ge(masked_d.sem, masked_d.upto(0, r))
                    dve.wait_ge(masked_p.sem, masked_p.upto(0, r))
                    dve.tensor_scalar(k_all[:, :], k.ps[:, SM, 0:TG * nk], bcol[:, 1:2], None,
                                      ALU.add).then_inc(k_in.sem, 1)

                def mask(r, u, h, n=ND):
                    if h == 0:
                        dve.wait_ge(k_in.sem, k_in.upto(1, r))
                        dve.wait_ge(s_ps.sem, s_ps.upto(0, r - 1))
                    last = dve.tensor_scalar(k_heads[u][:, h].rearrange("p t n -> p (t n)"), k_all[:, :],
                                             k.cols[:, 16 + h:17 + h], None, ALU.mult)
                    if h == n - 1:
                        last.then_inc(masked_d.sem, 1)

                def take_q(r, u):
                    dve.wait_ge(q_ps.sem, q_ps.upto(1, r))
                    dve.tensor_scalar(q_sb[:, u], k.ps[:, SM, :], bcol[:, 0:1], scale, ALU.add,
                                      ALU.mult).then_inc(q_in.sem, 1)

                def take_v(r, u):
                    dve.wait_ge(v_ps.sem, v_ps.upto(1, r))
                    for t in range(TG):
                        last = dve.tensor_tensor(v_sb[0:nk, u, t, :, 0:DH],
                                                 k.ps[0:nk, SM, t * P:(t + 1) * P].rearrange("p (h c) -> p h c", c=DH),
                                                 vrow[0:nk, :].rearrange("p (h c) -> p h c", c=DH), ALU.add)
                    last.then_inc(v_in.sem, 1)

                def copy_outputs(r, t):
                    dve.wait_ge(pv.sem, pv.upto(4 * t + 4, r))
                    dve.wait_ge(back.sem, back.upto(t, r))
                    dve.tensor_copy(raw[:, :], k.ps[:, SO + t % 2, :]).then_inc(raw_in.sem, 1)

                def scale_outputs(r, t):
                    dve.wait_ge(back.sem, back.upto(t + 1, r))
                    o = k.ps[:, SO + t % 2, :].rearrange("p (h c) -> p h c", c=DP)
                    dve.reciprocal(rec[:, :], o[:, :, DH]).then_inc(rc.sem, 1)
                    dve.wait_ge(rc.sem, rc.upto(t + 1, r))
                    if t == 0:
                        dve.wait_ge(ot_ps.sem, ot_ps.upto(0, r))
                    dve.tensor_tensor(o_sb[:, t, :].rearrange("p (h c) -> p h c", c=DH), o[:, :, 0:DH],
                                      bc(rec[:, :].unsqueeze(2), [P, H, DH]), ALU.mult).then_inc(nrm.sem, 1)

                def take_oT(r, g):
                    dve.wait_ge(ot_ps.sem, ot_ps.upto(1, r))
                    dve.wait_ge(y_ps.sem, y_ps.upto(0, r))
                    dve.tensor_copy(oT[:, :], k.ps[:, SM, :]).then_inc(ot_in.sem, 1)
                    if gated:
                        dve.wait_ge(added.sem, added.upto(0, r))
                        dve.tensor_copy(gcur[:, :], k.gates[:, ds(e_now[0], 1), ds(g * TG, TG)]
                                        .rearrange("p a t -> p (a t)")).then_inc(gsel.sem, 1)

                def add(r, g):
                    dve.wait_ge(y_ps.sem, y_ps.upto(1, r))
                    if gated:
                        dve.wait_ge(gsel.sem, gsel.upto(1, r))
                    add_gated(k, dve, k.x_all, g, k.ps[:, SM, :], gcur if gated else None, gate_col, added)

                e_now = [0]

                def start():
                    take_k(0)
                    for h in range(ND_START):
                        mask(0, 0, h, ND_START)
                    take_q(0, 0)
                    take_v(0, 0)
                    top(0, 0)
                    top(0, 1)

                def body(e, g0, first, last):
                    e_now[0] = e
                    r0 = e * G + g0
                    for r, g, u, s, n, before, switch in steps(e, g0, first, last):
                        top(r0, n + 2)
                        if s == 1 and before:
                            copy_outputs(r - 1, TG - 1)
                        if s == 2:
                            take_k(r + 1)
                        if 3 <= s < 3 + ND:
                            mask(r + 1, 1 - u, s - 3)
                        if s == 3 and before:
                            scale_outputs(r - 1, TG - 1)
                        if s == 5 and before:
                            take_oT(r - 1, g - 1)
                        if s == 7 and before:
                            add(r - 1, g - 1)
                        if s % 4 == 1 and s > 1:
                            copy_outputs(r, s // 4 - 1)
                        if s % 4 == 3 and s > 3:
                            scale_outputs(r, s // 4 - 1)
                        if s == 10:
                            take_q(r + 1, 1 - u)
                        if s == 13:
                            take_v(r + 1, 1 - u)

                def end(e, r):
                    copy_outputs(r, TG - 1)
                    scale_outputs(r, TG - 1)
                    take_oT(r, G - 1)
                    add(r, G - 1)

                dve.memset(k.ps[:, SO:SO + 2, :], 0.0).then_inc(set_up.sem, 1)
                dve.wait_ge(set_up.sem, set_up.upto(1))
                dve.memset(v_sb[:, :, :, :, DH:DH + 1], 1.0).then_inc(set_up.sem, 1)
                dve.wait_ge(set_up.sem, set_up.upto(2))
                sets(dve, start, body, end)


def wide_attention(k, scale, weights, gate_col):
    nc = k.nc
    E, nk, DH = 8, NK, 64
    NS = 2 * E
    R = G
    SA, ST, SO, SY, SM = 0, 3, 5, 6, 7
    with ExitStack() as ctx:
        w = k.sb("wa_w", [P, E, 4, P], ctx=ctx)
        orow = k.sb("wa_orow", [1, P], ctx=ctx)
        xT = k.sb("wa_xT", [P, 2, TG * P], ctx=ctx)
        kv = k.sb("wa_kv", [P, 2, TG * nk], ctx=ctx)
        q_sb = k.sb("wa_q", [P, 2, TG * P], ctx=ctx)
        k_sb = k.sb("wa_k", [P, 2, TG * nk], ctx=ctx)
        v_sb = k.sb("wa_v", [P, 4, TG * P], ctx=ctx)
        negmax = k.sb("wa_max", [P, 3, TG], ctx=ctx)
        probs = k.sb("wa_p", [P, 2, TG, nk], ctx=ctx)
        sums = k.sb("wa_sums", [P, 2, TG], ctx=ctx)
        pT = k.sb("wa_pT", [P, 2, TG * P], ctx=ctx)
        oT = k.sb("wa_oT", [P, 2, TG * P], ctx=ctx)

        loaded = k.sig("dma_landed", 2)
        ready = k.sig("x_ready", 1, R)
        q_ps, k_ps, v_ps = (k.sig(f"{n}_made", E, R) for n in "qkv")
        q_in, k_in, v_in = (k.sig(f"{n}_in_sbuf", E, R) for n in "qkv")
        s_ps, mx, ex = k.sig("scores_made", NS, R), k.sig("max_found", NS, R), k.sig("exp_done", NS, R)
        summed, rc, scaled = k.sig("probs_summed", NS, R), k.sig("sums_inverted", NS, R), k.sig("probs_scaled", NS, R)
        t_ps, t_in = k.sig("probs_turned", NS, R), k.sig("probsT_in_sbuf", NS, R)
        pv = k.sig("outputs_made", NS, R)
        ot_in = k.sig("outputsT_in_sbuf", E, R)
        y_ps = k.sig("y_made", E, R)
        added = k.sig("y_added", 1, R)

        def slot(n):
            return (n % 32) % 3, (n - 3 if n % 32 >= 3 else n - 2 if n % 32 < 2 else n - 5)

        def run(start, body, end):
            def go(eng):
                start()
                body(0, True, False)
                with eng.Fori(1, G // 2 - 1) as i:
                    body(2 * i, False, False)
                body(G - 2, False, True)
                end()
            return go

        def steps(r0, first, last):
            for u in range(2):
                for s in range(NS):
                    yield r0 + u, u, s, NS * u + s, not (first and u == 0), not (last and u == 1)

        with nc.Block() as block:
            @block.sync
            def _(sp):
                sp.dma_start(w[:, :, :, :], weights["w"][0:E].rearrange("e p n c -> p e n c")).then_inc(loaded.sem, 16)
                sp.dma_start(orow[:, :], weights["rows"][0:1, 1, :]).then_inc(loaded.sem, 16)

            @block.gpsimd
            def _(pool):
                def copy(g, u):
                    pool.tensor_copy(xT[:, u], k.nxT_all[:, ds(g * (TG * P), TG * P)])
                    pool.tensor_copy(kv[0:CK, u], k.ctxT[:, ds(g * (TG * nk), TG * nk)]).then_inc(ready.sem, 1)

                copy(0, 0)
                copy(1, 1)
                with pool.Fori(1, G // 2) as i:
                    for u in range(2):
                        pool.wait_ge(v_ps.sem, v_ps.upto(0, 2 * i + (u - 1)))
                        copy(2 * i + u, u)

            @block.tensor
            def _(pe):
                def project_q(r, u, e):
                    if e == 0:
                        pe.wait_ge(ready.sem, ready.upto(1, r))
                    pe.wait_ge(v_in.sem, v_in.upto(e, r))
                    pe.matmul(k.ps[:, SM, :], w[:, e, 0, :], xT[:, u], start=True, stop=True).then_inc(q_ps.sem, 1)

                def project_k(r, u, e):
                    pe.wait_ge(q_in.sem, q_in.upto(e + 1, r))
                    pe.matmul(k.ps[:, SM, 0:TG * nk], w[0:CK, e, 1, :], kv[0:CK, u], start=True,
                              stop=True).then_inc(k_ps.sem, 1)

                def project_v(r, u, e):
                    pe.wait_ge(k_in.sem, k_in.upto(e + 1, r))
                    for t in range(TG):
                        mm = pe.matmul(k.ps[0:nk, SM, t * P:(t + 1) * P], kv[0:CK, u, t * nk:(t + 1) * nk],
                                       w[0:CK, e, 2, :], start=True, stop=True)
                    mm.then_inc(v_ps.sem, 1)

                def scores(r0, n, fresh):
                    b, before = slot(n)
                    e, h = divmod(n % NS, 2)
                    if h == 0:
                        pe.wait_ge(q_in.sem, q_in.upto(e + 1, r0 + n // NS))
                        pe.wait_ge(k_in.sem, k_in.upto(e + 1, r0 + n // NS))
                    if not fresh:
                        pe.wait_ge(ex.sem, ex.upto(before + 1, r0))
                    rows = slice(DH * h, DH * (h + 1))
                    for t in range(TG):
                        mm = pe.matmul(k.ps[:, SA + b, t * nk:(t + 1) * nk], q_sb[rows, e % 2, t * P:(t + 1) * P],
                                       k_sb[rows, e % 2, t * nk:(t + 1) * nk], start=True, stop=True)
                    mm.then_inc(s_ps.sem, 1)

                def turn(r, s, fresh):
                    pe.wait_ge(scaled.sem, scaled.upto(s + 1, r))
                    if not fresh:
                        pe.wait_ge(t_in.sem, t_in.upto(s - 1, r))
                    for j in range(TG):
                        mm = pe.transpose(k.ps[0:nk, ST + s % 2, j * P:(j + 1) * P], probs[:, s % 2, j, :],
                                          k.ident[:, :])
                    mm.then_inc(t_ps.sem, 1)

                def outputs(r, s):
                    e, h = divmod(s, 2)
                    pe.wait_ge(t_in.sem, t_in.upto(s + 1, r))
                    if h == 0:
                        pe.wait_ge(v_in.sem, v_in.upto(e + 1, r))
                        pe.wait_ge(ot_in.sem, ot_in.upto(e, r))
                    for t in range(TG):
                        mm = pe.matmul(k.ps[DH * h:DH * (h + 1), SO, t * P:(t + 1) * P],
                                       v_sb[0:nk, e % 4, t * P + DH * h:t * P + DH * (h + 1)],
                                       pT[0:nk, s % 2, t * P:(t + 1) * P], start=True, stop=True)
                    mm.then_inc(pv.sem, 1)

                def project_out(r, e):
                    pe.wait_ge(ot_in.sem, ot_in.upto(e + 1, r))
                    if e == 0:
                        pe.wait_ge(added.sem, added.upto(0, r))
                        pe.matmul(k.ps[:, SY, :].rearrange("p (t c) -> p t c", c=P), k.ones[0:1, :],
                                  bc(orow[0:1, :].unsqueeze(1), [1, TG, P]), start=True, stop=False)
                    for t in range(TG):
                        mm = pe.matmul(k.ps[:, SY, t * P:(t + 1) * P], oT[:, e % 2, t * P:(t + 1) * P], w[:, e, 3, :],
                                       start=False, stop=e == E - 1 and t == TG - 1)
                    mm.then_inc(y_ps.sem, 1)

                def start():
                    pe.wait_ge(loaded.sem, loaded.upto(2))
                    project_q(0, 0, 0)
                    project_k(0, 0, 0)
                    project_v(0, 0, 0)
                    project_q(0, 0, 1)
                    project_k(0, 0, 1)
                    project_v(0, 0, 1)
                    scores(0, 0, True)
                    scores(0, 1, True)

                def body(r0, first, last):
                    for r, u, s, n, before, after in steps(r0, first, last):
                        e = s // 2
                        r2, u2, e2 = (r, u, e + 2) if e + 2 < E else (r + 1, 1 - u, e + 2 - E)
                        due = e + 2 < E or after
                        if s + 2 < NS or after:
                            scores(r0, n + 2, first and n + 2 < 3)
                        if s % 2 == 1 and due:
                            project_k(r2, u2, e2)
                        turn(r, s, s == 0 and not before)
                        if s % 2 == 0 and due:
                            project_q(r2, u2, e2)
                        if s > 0 or before:
                            outputs(r if s else r - 1, (s - 1) % NS)
                        if s % 2 == 1:
                            if e > 0:
                                project_out(r, e - 1)
                            elif before:
                                project_out(r - 1, E - 1)
                            if due:
                                project_v(r2, u2, e2)

                def end():
                    outputs(G - 1, NS - 1)
                    project_out(G - 1, E - 1)

                run(start, body, end)(pe)

            @block.scalar
            def _(act):
                def exps(r0, n, fresh):
                    b, _ = slot(n)
                    act.wait_ge(mx.sem, mx.upto(n + 1, r0))
                    if not fresh:
                        act.wait_ge(t_ps.sem, t_ps.upto(n - 1, r0))
                    for j in range(TG):
                        last = act.activation(probs[:, n % 2, j, :], k.ps[:, SA + b, j * nk:(j + 1) * nk], ACT.Exp,
                                              bias=negmax[:, b, j:j + 1])
                    last.then_inc(ex.sem, 1)

                def fetch(r, s, fresh):
                    act.wait_ge(t_ps.sem, t_ps.upto(s + 1, r))
                    if not fresh:
                        act.wait_ge(pv.sem, pv.upto(s - 1, r))
                    act.copy(pT[0:nk, s % 2, :], k.ps[0:nk, ST + s % 2, :]).then_inc(t_in.sem, 1)

                def take_q(r, e, fresh):
                    act.wait_ge(q_ps.sem, q_ps.upto(e + 1, r))
                    if not fresh:
                        act.wait_ge(s_ps.sem, s_ps.upto(2 * e - 2, r))
                    act.mul(q_sb[:, e % 2, :], k.ps[:, SM, :], scale).then_inc(q_in.sem, 1)

                def take_k(r, e, fresh):
                    act.wait_ge(k_ps.sem, k_ps.upto(e + 1, r))
                    if not fresh:
                        act.wait_ge(s_ps.sem, s_ps.upto(2 * e - 2, r))
                    act.copy(k_sb[:, e % 2, :], k.ps[:, SM, 0:TG * nk]).then_inc(k_in.sem, 1)

                def start():
                    take_q(0, 0, True)
                    take_k(0, 0, True)
                    take_q(0, 1, True)
                    take_k(0, 1, True)
                    exps(0, 0, True)

                def body(r0, first, last):
                    for r, u, s, n, before, after in steps(r0, first, last):
                        e = s // 2
                        r2, e2 = (r, e + 2) if e + 2 < E else (r + 1, e + 2 - E)
                        due = e + 2 < E or after
                        if s + 1 < NS or after:
                            exps(r0, n + 1, False)
                        if s % 2 == 1 and due:
                            take_k(r2, e2, False)
                        fetch(r, s, s == 0 and not before)
                        if s % 2 == 0 and due:
                            take_q(r2, e2, False)

                run(start, body, lambda: None)(act)

            @block.vector
            def _(dve):
                def top(r0, n):
                    b, _ = slot(n)
                    dve.wait_ge(s_ps.sem, s_ps.upto(n + 1, r0))
                    dve.tensor_reduce(negmax[:, b], k.ps[:, SA + b, 0:TG * nk].rearrange("p (h n) -> p h n", n=nk),
                                      X, ALU.max, negate=True).then_inc(mx.sem, 1)

                def normalise(r0, n):
                    p, a = probs[:, n % 2], sums[:, n % 2]
                    dve.wait_ge(ex.sem, ex.upto(n + 1, r0))
                    dve.tensor_reduce(a, p, X, ALU.add).then_inc(summed.sem, 1)
                    dve.wait_ge(summed.sem, summed.upto(n + 1, r0))
                    dve.reciprocal(a, a).then_inc(rc.sem, 1)
                    dve.wait_ge(rc.sem, rc.upto(n + 1, r0))
                    dve.tensor_tensor(p, p, bc(a.unsqueeze(2), [P, TG, nk]), ALU.mult).then_inc(scaled.sem, 1)

                def take_v(r, e, fresh):
                    dve.wait_ge(v_ps.sem, v_ps.upto(e + 1, r))
                    if not fresh:
                        dve.wait_ge(pv.sem, pv.upto(2 * e - 6, r))
                    dve.tensor_copy(v_sb[0:nk, e % 4, :], k.ps[0:nk, SM, :]).then_inc(v_in.sem, 1)

                def take_oT(r, e):
                    dve.wait_ge(pv.sem, pv.upto(2 * e + 2, r))
                    dve.wait_ge(y_ps.sem, y_ps.upto(e - 1, r) if e else y_ps.upto(0, r))
                    dve.tensor_copy(oT[:, e % 2, :], k.ps[:, SO, :]).then_inc(ot_in.sem, 1)

                def add(r):
                    dve.wait_ge(y_ps.sem, y_ps.upto(E, r))
                    add_gated(k, dve, k.x_all, r, k.ps[:, SY, :], None, gate_col, added)

                def start():
                    take_v(0, 0, True)
                    take_v(0, 1, True)
                    top(0, 0)
                    top(0, 1)
                    normalise(0, 0)

                def body(r0, first, last):
                    for r, u, s, n, before, after in steps(r0, first, last):
                        e = s // 2
                        if s % 2 == 0 and e + 1 < E and (e > 0 or before):
                            take_v(r, e + 1, not before and e + 1 < 4)
                        elif s % 2 == 0 and e + 1 == E and after:
                            take_v(r + 1, 0, False)
                        if s % 2 == 1:
                            if e > 0:
                                take_oT(r, e - 1)
                            elif before:
                                take_oT(r - 1, E - 1)
                        if s + 2 < NS or after:
                            top(r0, n + 2)
                        if s + 1 < NS or after:
                            normalise(r0, n + 1)
                        if s == 2 and before:
                            add(r - 1)

                def end():
                    take_oT(G - 1, E - 1)
                    add(G - 1)

                run(start, body, end)(dve)


def add_gated(k, dve, target, g, y, gcur, gate_col, done):
    if gcur is None:
        last = dve.scalar_tensor_tensor(target[:, ds(g * TG, TG), :].rearrange("p t c -> p (t c)"), y, gate_col,
                                        target[:, ds(g * TG, TG), :].rearrange("p t c -> p (t c)"), ALU.mult, ALU.add)
    else:
        for t in range(TG):
            x = target[:, ds(g * TG + t, 1), :].rearrange("p a c -> p (a c)")
            last = dve.scalar_tensor_tensor(x, y[:, t * P:(t + 1) * P], gcur[:, t:t + 1], x, ALU.mult, ALU.add)
    last.then_inc(done.sem, 1)


def add_gated_rows(k, rows_dram):
    nc = k.nc
    NB = P // 8
    with ExitStack() as ctx:
        diag = k.sb("gr_diag", [P, NB, P], ctx=ctx)
        by_sample = k.sb("gr_gates", [P, B, 8], ctx=ctx)
        gT = k.sb("gr_gT", [P, B // NB, P], ctx=ctx)
        loaded = k.sig("dma_landed", 1)
        step = k.sig("dve_step", 2)
        turned = k.sig("turned", 1)
        made = k.sig("y_made", 1, G)
        added = k.sig("y_added", 1, G)
        with nc.Block() as block:
            @block.sync
            def _(sp):
                sp.dma_start(diag[:, :, :], rows_dram).then_inc(loaded.sem, 16)

            @block.tensor
            def _(pe):
                pe.wait_ge(loaded.sem, loaded.upto(1))
                pe.wait_ge(step.sem, step.upto(1))
                for n in range(B // NB):
                    mm = pe.transpose(k.ps[:, 0, n * P:(n + 1) * P],
                                      by_sample[:, NB * n:NB * (n + 1), :].rearrange("p b e -> p (b e)"), k.ident[:, :])
                mm.then_inc(turned.sem, 1)
                pe.wait_ge(step.sem, step.upto(2))
                for g in range(G):
                    if g >= 2:
                        pe.wait_ge(added.sem, added.upto(1, g - 2))
                    b = g * TG % NB
                    pe.matmul(k.ps[:, 1 + g % 2, :], gT[:, g * TG // NB, :],
                              diag[:, b:b + TG, :].rearrange("p b c -> p (b c)"), start=True,
                              stop=True).then_inc(made.sem, 1)

            @block.vector
            def _(dve):
                dve.tensor_copy(by_sample[:, :, :], k.gates[:, 0:8, :].rearrange("p e b -> p b e")).then_inc(step.sem, 1)
                dve.wait_ge(turned.sem, turned.upto(1))
                dve.tensor_copy(gT[:, :, :].rearrange("p n c -> p (n c)"), k.ps[:, 0, :]).then_inc(step.sem, 1)
                for g in range(G):
                    dve.wait_ge(made.sem, made.upto(1, g))
                    x = k.x_all[:, g * TG:(g + 1) * TG, :].rearrange("p t c -> p (t c)")
                    dve.tensor_tensor(x, x, k.ps[:, 1 + g % 2, :], ALU.add).then_inc(added.sem, 1)


def experts(k, E, MC, func, weights, target, up, pair=False, gate_col=None, gated=True):
    nc = k.nc
    R = E * G
    NY = 2 if pair else 1
    NW = (2 + bool(up)) * MC * P
    with ExitStack() as ctx:
        w_next = k.sb("ex_w_next", [P, NW + 2 * MC], ctx=ctx)
        w_now = k.sb("ex_w", [P, NW + 2 * MC], ctx=ctx)
        w1 = w_now[:, 0:MC * P]
        w2 = w_now[:, MC * P:2 * MC * P].rearrange("p (m c) -> p m c", c=P)
        w3 = w_now[:, 2 * MC * P:3 * MC * P] if up else None
        bcol = w_now[:, NW:NW + 2 * MC]
        orow = None if gated else k.sb("ex_orow", [1, P], ctx=ctx)
        act_sb = k.sb("ex_act", [P, 2, TG * P], ctx=ctx)
        hid = k.sb("ex_hid", [P, 2, MC, TG * P], ctx=ctx)
        gcur = k.sb("ex_g", [P, 2, NY * TG], ctx=ctx)
        ND = 3 + bool(up) + (not gated)
        loaded = k.sig("dma_landed", ND, E)
        w_in = k.sig("weights_copied", 1, E)
        g_ps = k.sig("h1_made", MC, R)
        u_ps = k.sig("h3_made", MC, R) if up else None
        a_in = k.sig("h1_activated", MC, R)
        h_in = k.sig("hidden_in_sbuf", MC, R) if up else None
        y_ps = k.sig("y_made", 1, R)
        added = k.sig("y_added", NY, R)
        gsel = k.sig("gates_copied", 1, R) if gated else None
        table = k.sig("act_step", 1)
        hdone = h_in if up else a_in

        def sets(eng, start, body, end):
            def one(e):
                start(e, e * G)
                body(e, 0, True)
                with eng.Fori(1, G // 2) as i:
                    body(e, 2 * i, False)
                end(e, e * G + (G - 1))
            if E == 1:
                one(0)
            else:
                with eng.Fori(0, E) as e:
                    one(e)

        with nc.Block() as block:
            @block.sync
            def _(sp):
                if not gated:
                    sp.dma_start(orow[:, :], weights["brow"][0:1, :]).then_inc(loaded.sem, 16)
                with sp.Fori(0, E) as e:
                    sp.wait_ge(w_in.sem, w_in.upto(0, e))
                    sp.dma_start(w_next[:, 0:MC * P], weights["w1"][ds(e, 1)].rearrange("a p m -> p (a m)")
                                 ).then_inc(loaded.sem, 16)
                    sp.dma_start(w_next[:, MC * P:2 * MC * P], weights["w2"][ds(e, 1)].rearrange("a p m c -> p (a m c)")
                                 ).then_inc(loaded.sem, 16)
                    if up:
                        sp.dma_start(w_next[:, 2 * MC * P:3 * MC * P], weights["w3"][ds(e, 1)]
                                     .rearrange("a p m -> p (a m)")).then_inc(loaded.sem, 16)
                    sp.dma_start(w_next[:, NW:NW + 2 * MC], weights["bcol"][ds(e, 1)].rearrange("a p m -> p (a m)")
                                 ).then_inc(loaded.sem, 16)

            @block.tensor
            def _(pe):
                def hidden(r, u, g, m, fresh):
                    n = u * MC + m
                    x = k.nxT_all[:, ds(g * (TG * P), TG * P)]
                    if not fresh:
                        pe.wait_ge(hdone.sem, hdone.upto(m - 1, r))
                    pe.matmul(k.ps[:, n % 2, :], w1[:, m * P:(m + 1) * P], x, start=True,
                              stop=True).then_inc(g_ps.sem, 1)
                    if up:
                        pe.matmul(k.ps[:, 2 + n % 2, :], w3[:, m * P:(m + 1) * P], x, start=True,
                                  stop=True).then_inc(u_ps.sem, 1)

                def down(r, u, part, fresh):
                    if part == 0:
                        pe.wait_ge(hdone.sem, hdone.upto(MC, r))
                        if not fresh:
                            pe.wait_ge(added.sem, added.upto(0, r - 1))
                    for t in range(TG * part // MC, TG * (part + 1) // MC):
                        tok = slice(t * P, (t + 1) * P)
                        if pair:
                            for a in range(2):
                                f = slice(64 * a, 64 * a + 64)
                                mm = pe.matmul(k.ps[:, 4 + 2 * u + a, tok], hid[f, u, 0, tok], w2[f, 0, :], start=True,
                                               stop=True)
                        else:
                            if not gated:
                                pe.matmul(k.ps[:, 4 + u, tok], k.ones[0:1, :], orow[0:1, :], start=True, stop=False)
                            for m in range(MC):
                                mm = pe.matmul(k.ps[:, 4 + u, tok], hid[:, u, m, tok], w2[:, m, :],
                                               start=gated and m == 0, stop=m == MC - 1)
                    if part == MC - 1:
                        mm.then_inc(y_ps.sem, 1)

                def start(e, r):
                    pe.wait_ge(w_in.sem, w_in.upto(1, e))

                def body(e, g0, first):
                    for u in range(2):
                        for m in range(MC):
                            hidden(e * G + (g0 + u), u, g0 + u, m, first and u * MC + m < 2)
                            if u or not first:
                                down(e * G + (g0 + (u - 1)), 1 - u, m, first)

                def end(e, r):
                    for m in range(MC):
                        down(r, 1, m, False)

                sets(pe, start, body, end)

            @block.scalar
            def _(act):
                def start(e, r):
                    act.wait_ge(w_in.sem, w_in.upto(1, e))

                def body(e, g0, first):
                    for u in range(2):
                        r = e * G + (g0 + u)
                        for m in range(MC):
                            n = u * MC + m
                            act.wait_ge(g_ps.sem, g_ps.upto(m + 1, r))
                            if up:
                                if not (first and n < 2):
                                    act.wait_ge(h_in.sem, h_in.upto(m - 1, r))
                                out = act_sb[:, n % 2]
                            else:
                                if m == 0 and not first:
                                    act.wait_ge(y_ps.sem, y_ps.upto(0, r - 1))
                                out = hid[:, u, m, :]
                            act.activation(out, k.ps[:, n % 2, :], func, bias=bcol[:, m:m + 1]).then_inc(a_in.sem, 1)

                act.activation(act_sb[:, 0, 0:1], k.cols[:, 1:2], func).then_inc(table.sem, 1)
                act.wait_ge(table.sem, table.upto(1))
                sets(act, start, body, lambda e, r: None)

            @block.vector
            def _(dve):
                def start(e, r):
                    dve.wait_ge(loaded.sem, loaded.upto(ND, e))
                    dve.wait_ge(added.sem, added.upto(0, r))
                    dve.tensor_copy(w_now[:, :], w_next[:, :]).then_inc(w_in.sem, 1)
                    dve.wait_ge(w_in.sem, w_in.upto(1, e))

                def add(r, u, g):
                    dve.wait_ge(y_ps.sem, y_ps.upto(1, r))
                    if gated:
                        dve.wait_ge(gsel.sem, gsel.upto(1, r))
                    for a in range(NY):
                        if a:
                            dve.wait_ge(added.sem, added.upto(a, r))
                        bank = 4 + 2 * u + a if pair else 4 + u
                        add_gated(k, dve, target, g, k.ps[:, bank, :],
                                  gcur[:, u, a * TG:(a + 1) * TG] if gated else None, gate_col, added)

                def body(e, g0, first):
                    for u in range(2):
                        g = g0 + u
                        r = e * G + g
                        for m in range(MC) if up else ():
                            n = u * MC + m
                            dve.wait_ge(u_ps.sem, u_ps.upto(m + 1, r))
                            dve.wait_ge(a_in.sem, a_in.upto(m + 1, r))
                            if m == 0 and not first:
                                dve.wait_ge(y_ps.sem, y_ps.upto(0, r - 1))
                            dve.scalar_tensor_tensor(hid[:, u, m, :], k.ps[:, 2 + n % 2, :], bcol[:, MC + m:MC + m + 1],
                                                     act_sb[:, n % 2], ALU.add, ALU.mult).then_inc(h_in.sem, 1)
                        if gated:
                            if not first:
                                dve.wait_ge(added.sem, added.upto(0, r - 1))
                            for a in range(NY):
                                last = dve.tensor_copy(gcur[:, u, a * TG:(a + 1) * TG],
                                                       k.gates[:, ds(e * NY + a, 1), ds(g * TG, TG)]
                                                       .rearrange("p a t -> p (a t)"))
                            last.then_inc(gsel.sem, 1)
                        if u or not first:
                            add(e * G + (g0 + (u - 1)), 1 - u, g0 + (u - 1))

                def end(e, r):
                    add(r, 1, G - 1)

                sets(dve, start, body, end)


def router_logits(k, h_all, H, rw):
    nc = k.nc
    with ExitStack() as ctx:
        w2 = k.sb("ro_w2", [P, 8], ctx=ctx)
        b2 = k.sb("ro_b2", [P, 8], ctx=ctx)
        lg = k.sb("ro_g", [P, H], ctx=ctx)
        lb = k.sb("ro_b", [P, H], ctx=ctx)
        rows = k.sb("ro_rows", [P, 2, TG, H], ctx=ctx)
        hT = k.sb("ro_hT", [P, 2, TG * P // 2], ctx=ctx)
        loaded = k.sig("dma_landed", 5)
        chain = k.sig("dve_step", 3)
        staged = k.sig("staged", 1, G)
        turned = k.sig("turned", 1, G)
        copied = k.sig("copied", 1, G)
        routed = k.sig("routed", 1, G)
        taken = k.sig("routes_taken", 1, G)
        with nc.Block() as block:
            @block.sync
            def _(sp):
                for to, of in ((w2[0:H, :], rw["w2"]), (w2[H:2 * H, :], rw["w2"]), (b2[:, :], rw["b2"].partition_broadcast(P)),
                               (lg[:, :], rw["g"].partition_broadcast(P)), (lb[:, :], rw["b"].partition_broadcast(P))):
                    sp.dma_start(to, of).then_inc(loaded.sem, 16)

            @block.tensor
            def _(pe):
                pe.wait_ge(loaded.sem, loaded.upto(5))
                for r, u, g in rounds(pe):
                    pe.wait_ge(staged.sem, staged.upto(1, r))
                    if u == 0:
                        pe.wait_ge(copied.sem, copied.upto(0, r))
                    for t in range(0, TG, 2):
                        mm = pe.transpose(k.ps[:, u, t * H:(t + 2) * H],
                                          rows[:, u, t:t + 2, :].rearrange("p t h -> p (t h)"), k.ident[:, :])
                    mm.then_inc(turned.sem, 1)
                    pe.wait_ge(copied.sem, copied.upto(1, r))
                    if u == 0:
                        pe.wait_ge(taken.sem, taken.upto(0, r))
                    for t in range(TG):
                        a, f = t % 2, slice(H * (t % 2), H * (t % 2) + H)
                        mm = pe.matmul(k.ps[:, 2 + 2 * a + u, (t // 2) * 8:(t // 2 + 1) * 8],
                                       hT[f, u, (t // 2) * P:(t // 2 + 1) * P], w2[f, :], start=True, stop=True)
                    mm.then_inc(routed.sem, 1)

            @block.scalar
            def _(act):
                for r, u, g in rounds(act):
                    act.wait_ge(turned.sem, turned.upto(1, r))
                    if u == 0:
                        act.wait_ge(routed.sem, routed.upto(0, r))
                    act.copy(hT[:, u], k.ps[:, u, 0:TG * H]).then_inc(copied.sem, 1)

            @block.vector
            def _(dve):
                link = Chain(dve, chain)
                dve.wait_ge(loaded.sem, loaded.upto(5))
                link(dve.tensor_tensor(h_all[:, :, :], h_all[:, :, :], bc(lg[:, :].unsqueeze(1), [P, B, H]), ALU.mult))
                link(dve.tensor_tensor(h_all[:, :, :], h_all[:, :, :], bc(lb[:, :].unsqueeze(1), [P, B, H]), ALU.add))
                link(dve.tensor_scalar(h_all[:, :, :], h_all[:, :, :], 0.0, None, ALU.max))
                for r, u, g in rounds(dve):
                    if u == 0:
                        dve.wait_ge(turned.sem, turned.upto(0, r))
                    dve.tensor_copy(rows[:, u], h_all[:, ds(g * TG, TG), :]).then_inc(staged.sem, 1)
                    dve.wait_ge(routed.sem, routed.upto(1, r))
                    for a in range(2):
                        last = dve.tensor_tensor(k.logits[:, ds(g * TG + a, TG // 2, 2), :],
                                                 k.ps[:, 2 + 2 * a + u, 0:TG * 4].rearrange("p (t w) -> p t w", w=8),
                                                 bc(b2[:, :].unsqueeze(1), [P, TG // 2, 8]), ALU.add)
                    last.then_inc(taken.sem, 1)


def top_two_gates(k, gate_col, plus=None, least=None, shared=0, capacity=None):
    nc = k.nc
    NE = 8
    S3 = [P, B, NE]
    with ExitStack() as ctx:
        t3 = [k.sb(f"tg_{i}", S3, ctx=ctx) for i in range(6)]
        c2 = [k.sb(f"tg_c{i}", [P, B], ctx=ctx) for i in range(3)]
        first, second, prob, a, b, c = t3
        m, s, z = c2
        if capacity:
            before = k.sb("tg_before", [P, P], ctx=ctx)
            tot = k.sb("tg_tot", [P, 2, B, NE], ctx=ctx)
            loc = k.sb("tg_loc", [P, 2, B, NE], ctx=ctx)
            run = k.sb("tg_run", [P, NE, B], ctx=ctx)
            zero = k.sb("tg_zero", [P, B], ctx=ctx)
        chain = k.sig("dve_step", 400)
        chosen = k.sig("chosen", 1)
        shifted = k.sig("shifted", 1)
        expd = k.sig("exp_done", 1)
        if capacity:
            counted = k.sig("counted", 1)
            loaded = k.sig("dma_landed", 1)
        with nc.Block() as block:
            if capacity:
                @block.sync
                def _(sp):
                    sp.dma_start(before[:, :], k.d["before"]).then_inc(loaded.sem, 16)

                @block.tensor
                def _(pe):
                    pe.wait_ge(loaded.sem, loaded.upto(1))
                    pe.wait_ge(chosen.sem, chosen.upto(1))
                    for i, one in enumerate((first, second)):
                        flat = one[:, :, :].rearrange("p t e -> p (t e)")
                        pe.matmul(k.ps[:, 2 * i, :], before[:, :], flat, start=True, stop=True)
                        mm = pe.matmul(k.ps[:, 2 * i + 1, :], k.ones[:, :], flat, start=True, stop=True)
                    mm.then_inc(counted.sem, 1)

            @block.scalar
            def _(act):
                act.wait_ge(shifted.sem, shifted.upto(1))
                act.activation(prob[:, :, :], c[:, :, :], ACT.Exp).then_inc(expd.sem, 1)

            @block.vector
            def _(dve):
                link = Chain(dve, chain)

                def wide(col):
                    return bc(col[:, :].unsqueeze(2), S3)

                def pick(values, onehot):
                    link(dve.tensor_reduce(s[:, :], values[:, :, :], X, ALU.max))
                    link(dve.tensor_tensor(b[:, :, :], values[:, :, :], wide(s), ALU.is_equal))
                    link(dve.tensor_tensor(b[:, :, :], b[:, :, :], bc(k.rank[:, :].unsqueeze(1), S3), ALU.mult))
                    link(dve.tensor_reduce(z[:, :], b[:, :, :], X, ALU.max))
                    link(dve.tensor_tensor(onehot[:, :, :], b[:, :, :], wide(z), ALU.is_equal))

                lg = k.logits
                link(dve.tensor_reduce(m[:, :], lg[:, :, :], X, ALU.max))
                dve.tensor_tensor(c[:, :, :], lg[:, :, :], wide(m), ALU.subtract).then_inc(shifted.sem, 1)
                pick(lg, first)
                link(dve.scalar_tensor_tensor(a[:, :, :], first[:, :, :], -1e30, lg[:, :, :], ALU.mult, ALU.add))
                pick(a, second)
                link(dve.tensor_copy(m[:, 0:1], m[:, 0:1]))
                chosen_now = dve.tensor_tensor(a[:, :, :], first[:, :, :], second[:, :, :], ALU.add)
                chosen_now.then_inc(chosen.sem, 1)
                dve.wait_ge(chosen.sem, chosen.upto(1))
                dve.wait_ge(expd.sem, expd.upto(1))
                link(dve.tensor_reduce(z[:, :], prob[:, :, :], X, ALU.add))
                link(dve.reciprocal(s[:, :], z[:, :]))
                link(dve.tensor_tensor(prob[:, :, :], prob[:, :, :], wide(s), ALU.mult))
                link(dve.tensor_tensor(b[:, :, :], prob[:, :, :], a[:, :, :], ALU.mult))
                link(dve.tensor_reduce(z[:, :], b[:, :, :], X, ALU.add))
                if plus:
                    link(dve.tensor_scalar(z[:, :], z[:, :], plus, None, ALU.add))
                if least:
                    link(dve.tensor_scalar(z[:, :], z[:, :], least, None, ALU.max))
                link(dve.reciprocal(s[:, :], z[:, :]))
                link(dve.tensor_scalar(s[:, :], s[:, :], gate_col, None, ALU.mult))
                if capacity:
                    link(dve.memset(zero[:, :], 0.0))
                    dve.wait_ge(counted.sem, counted.upto(1))
                    for i in range(2):
                        link(dve.tensor_copy(tot[:, i].rearrange("p t e -> p (t e)"), k.ps[:, 2 * i + 1, :]))
                        for e in range(NE):
                            start = 0.0 if i == 0 else z[:, e:e + 1]
                            link(dve.tensor_tensor_scan(run[:, e, :], tot[:, i, :, e], zero[:, :], start, ALU.add,
                                                        ALU.add))
                        link(dve.tensor_copy(z[:, 0:NE], run[:, :, B - 1]))
                        link(dve.tensor_tensor(c[:, :, :], run[:, :, :].rearrange("p e t -> p t e"), tot[:, i],
                                               ALU.subtract))
                        link(dve.tensor_tensor(loc[:, i], c[:, :, :],
                                               k.ps[:, 2 * i, :].rearrange("p (t e) -> p t e", e=NE), ALU.add))
                        one = first if i == 0 else second
                        link(dve.scalar_tensor_tensor(one[:, :, :], loc[:, i], float(capacity), one[:, :, :],
                                                      ALU.is_lt, ALU.mult))
                    link(dve.tensor_tensor(a[:, :, :], first[:, :, :], second[:, :, :], ALU.add))
                    link(dve.tensor_tensor(b[:, :, :], prob[:, :, :], a[:, :, :], ALU.mult))
                link(dve.tensor_tensor(k.gates[:, 0:NE, :].rearrange("p e t -> p t e"), b[:, :, :], wide(s), ALU.mult))
                for e in range(shared):
                    link(dve.tensor_scalar(k.gates[:, NE + e, :], m[:, :], 0.0, gate_col, ALU.mult, ALU.add))
                chain.per = chain.each = link.n


def ssm_kernel(k, ww, conv_dram):
    nc = k.nc
    N, L = 64, P
    re = k.nx_all[:, :, :]
    im = k.nxT_all[:, :].rearrange("p (n l) -> p n l", l=L)
    with ExitStack() as ctx:
        inp = k.sb("sk_in", [P, 4 * N + 2], ctx=ctx)
        t = [k.sb(f"sk_{i}", [P, N], ctx=ctx) for i in range(12)]
        t1 = k.sb("sk_t1", [P, N, L // 2], ctx=ctx)
        t2 = k.sb("sk_t2", [P, N, L // 2], ctx=ctx)
        row = k.sb("sk_row", [P, 2 * P], ctx=ctx)
        loaded = k.sig("dma_landed", 1)
        stored = k.sig("dma_stored", 1)
        chain = k.sig("dve_step", 400)
        to_sin = k.sig("angles_ready", 2)
        sins = k.sig("sines_done", 2)
        finished = k.sig("kernel_ready", 1)
        with nc.Block() as block:
            @block.sync
            def _(sp):
                sp.dma_start(inp[:, :], ww["ssm"]).then_inc(loaded.sem, 16)
                sp.wait_ge(finished.sem, finished.upto(1))
                sp.dma_start(conv_dram, row[:, :]).then_inc(stored.sem, 16)
                sp.wait_ge(stored.sem, stored.upto(1))

            @block.scalar
            def _(act):
                for i in range(2):
                    act.wait_ge(to_sin.sem, to_sin.upto(i + 1))
                    act.activation(t[2 + i][:, :], t[i][:, :], ACT.Sin).then_inc(sins.sem, 1)

            @block.vector
            def _(dve):
                link = Chain(dve, chain)
                A_re, A_im, C_re, C_im = (inp[:, i * N:(i + 1) * N] for i in range(4))
                log_dt, skip = inp[:, 4 * N:4 * N + 1], inp[:, 4 * N + 1:4 * N + 2]

                def exps(x, w, p2, u, r, f, em1=None, ex=None):
                    link(dve.tensor_scalar(r, x, 80.0, -80.0, ALU.min, ALU.max))
                    link(dve.tensor_scalar(p2, r, 1.4426950408889634, None, ALU.mult))
                    link(dve.tensor_scalar(p2, p2, MAGIC + 127.0, None, ALU.add))
                    link(dve.tensor_scalar(f, p2, MAGIC + 127.0, None, ALU.subtract))
                    link(dve.scalar_tensor_tensor(r, f, -0.693359375, r, ALU.mult, ALU.add))
                    link(dve.scalar_tensor_tensor(r, f, 2.12194440e-4, r, ALU.mult, ALU.add))
                    link(dve.tensor_scalar(u, r, 1.0 / 8, 1.0, ALU.mult, ALU.add))
                    for j in range(7, 1, -1):
                        link(dve.scalar_tensor_tensor(u, u, 1.0 / j, r, ALU.mult, ALU.mult))
                        link(dve.tensor_scalar(u, u, 1.0, None, ALU.add))
                    link(dve.tensor_tensor(u, u, r, ALU.mult))
                    link(dve.tensor_scalar(p2.bitcast(I32), p2.bitcast(I32), 23, None, ALU.logical_shift_left))
                    link(dve.tensor_tensor(u, u, p2, ALU.mult))
                    if ex is not None:
                        link(dve.tensor_tensor(ex, u, p2, ALU.add))
                    if em1 is not None:
                        link(dve.tensor_scalar(p2, p2, 1.0, None, ALU.subtract))
                        link(dve.tensor_tensor(em1, u, p2, ALU.add))

                def col(i, w=N):
                    return t[i][:, 0:w]

                dve.wait_ge(loaded.sem, loaded.upto(1))
                exps(log_dt, 1, col(4, 1), col(5, 1), col(6, 1), col(7, 1), ex=col(8, 1))
                dt = t[8][:, 0:1]
                link(dve.tensor_scalar(col(9), A_im, dt, 0.5, ALU.mult, ALU.mult))
                for i in range(2):
                    link(dve.tensor_scalar(col(4), col(9), 0.15915494309189535, 0.25 * i, ALU.mult, ALU.add))
                    link(dve.tensor_scalar(col(4), col(4), MAGIC, None, ALU.add))
                    link(dve.tensor_scalar(col(4), col(4), MAGIC, None, ALU.subtract))
                    link(dve.scalar_tensor_tensor(col(i), col(4), -6.28125, col(9), ALU.mult, ALU.add))
                    link(dve.scalar_tensor_tensor(col(i), col(4), -1.9353071795864769e-3, col(i), ALU.mult, ALU.add))
                    if i:
                        link(dve.tensor_scalar(col(i), col(i), 1.5707963267948966, None, ALU.add))
                    last = dve.tensor_scalar(col(i), col(i), 3.1415925, -3.1415925, ALU.min, ALU.max)
                    last.then_inc(to_sin.sem, 1)
                link(dve.tensor_scalar(col(10), A_re, dt, None, ALU.mult))
                exps(col(10), N, col(4), col(5), col(6), col(7), em1=col(11), ex=col(9))
                dve.wait_ge(sins.sem, sins.upto(2))
                s, c = col(2), col(3)
                link(dve.scalar_tensor_tensor(col(4), s, -2.0, s, ALU.mult, ALU.mult))
                link(dve.scalar_tensor_tensor(col(5), s, 2.0, c, ALU.mult, ALU.mult))
                link(dve.tensor_scalar(col(6), col(4), 1.0, None, ALU.add))
                zi = col(0)
                link(dve.tensor_tensor(zi, col(9), col(5), ALU.mult))
                link(dve.tensor_tensor(col(7), col(11), col(6), ALU.mult))
                link(dve.tensor_tensor(col(7), col(7), col(4), ALU.add))
                zr = col(1)
                link(dve.tensor_tensor(zr, col(9), col(6), ALU.mult))
                link(dve.tensor_tensor(col(2), A_re, A_re, ALU.mult))
                link(dve.tensor_tensor(col(3), A_im, A_im, ALU.mult))
                link(dve.tensor_tensor(col(2), col(2), col(3), ALU.add))
                link(dve.reciprocal(col(2), col(2)))

                def cmul(orr, oi, ar, ai, br, bi, x, y, conj=1.0):
                    link(dve.tensor_tensor(x, ar, br, ALU.mult))
                    link(dve.scalar_tensor_tensor(y, ai, -conj, bi, ALU.mult, ALU.mult))
                    link(dve.tensor_tensor(orr, x, y, ALU.add))
                    link(dve.scalar_tensor_tensor(x, ar, conj, bi, ALU.mult, ALU.mult))
                    link(dve.tensor_tensor(y, ai, br, ALU.mult))
                    link(dve.tensor_tensor(oi, x, y, ALU.add))

                cmul(col(8), col(9), C_re, C_im, col(7), zi, col(3), col(4))
                cmul(col(10), col(11), col(8), col(9), A_re, A_im, col(3), col(4), conj=-1.0)
                link(dve.tensor_tensor(re[:, :, 0], col(10), col(2), ALU.mult))
                link(dve.tensor_tensor(im[:, :, 0], col(11), col(2), ALU.mult))
                m = 1
                while m < L:
                    shape = [P, N, m]
                    a, b = re[:, :, 0:m], im[:, :, 0:m]
                    x, y = t1[:, :, 0:m], t2[:, :, 0:m]
                    zrb, zib = bc(zr.unsqueeze(2), shape), bc(zi.unsqueeze(2), shape)
                    link(dve.tensor_tensor(x, a, zrb, ALU.mult))
                    link(dve.tensor_tensor(y, b, zib, ALU.mult))
                    link(dve.tensor_tensor(re[:, :, m:2 * m], x, y, ALU.subtract))
                    m *= 2
                    if m == L:
                        break
                    link(dve.tensor_tensor(x, a, zib, ALU.mult))
                    link(dve.tensor_tensor(y, b, zrb, ALU.mult))
                    link(dve.tensor_tensor(im[:, :, m // 2:m], x, y, ALU.add))
                    link(dve.scalar_tensor_tensor(col(5), zr, 2.0, zi, ALU.mult, ALU.mult))
                    link(dve.tensor_tensor(col(3), zr, zr, ALU.mult))
                    link(dve.tensor_tensor(col(4), zi, zi, ALU.mult))
                    link(dve.tensor_tensor(zr, col(3), col(4), ALU.subtract))
                    link(dve.tensor_copy(zi, col(5)))
                link(dve.memset(row[:, :], 0.0))
                kk = row[:, P - 1:2 * P - 1]
                link(dve.tensor_reduce(kk, re.rearrange("p n l -> p l n"), X, ALU.add))
                link(dve.tensor_scalar(kk, kk, 2.0, None, ALU.mult))
                link(dve.tensor_scalar(kk[:, 0:1], kk[:, 0:1], skip, None, ALU.add))
                dve.tensor_copy(row[:, 2 * P - 1:2 * P], row[:, 0:1]).then_inc(finished.sem, 1)
                chain.per = chain.each = link.n


def film_rows(k, block_dve, link, mg, brow, film):
    dve = block_dve
    link(dve.tensor_scalar(film[:, :], brow[:, :], mg, None, ALU.mult))
    link(dve.tensor_scalar(film[:, 0:P], film[:, 0:P], 1.0, None, ALU.add))


def sparse_attention(k, ww, wide):
    nc = k.nc
    H, DH, TOP = 4, 32, 32
    W = H * TG
    with ExitStack() as ctx:
        def sb(name, shape, dt=F32):
            return k.sb("sa_" + name, shape, dt, ctx=ctx)

        w = sb("w", [P, 3, P])
        wf = sb("wf", [P, 2 * P])
        brow = sb("brow", [P, 2 * P])
        film = sb("film", [P, 2 * P])
        mg = sb("mg", [P, 1])
        vm = sb("vm", [P, B * NK], U8)
        tm8 = sb("tm8", [P, B], U8)
        tm = sb("tm", [P, B])
        xT = sb("xT", [P, TG * P])
        kv = sb("kv", [P, TG * NK])
        q_sb = sb("q", [P, TG * P])
        k_sb = sb("k", [P, TG * NK])
        v_sb = sb("v", [P, TG, P])
        mb = sb("mb", [P, TG * NK])
        sm = sb("sm", [P, W, NK])
        wk = sb("wk", [P, W, NK])
        m0 = sb("m0", [P, W, 8])
        m8 = sb("m8", [P, W, 8])
        negmax = sb("negmax", [P, W])
        pad = sb("pad", [P, 1])
        carry = sb("carry", [P, 2])
        rec = sb("rec", [P, W])
        aT = sb("aT", [P, TG * P])
        cT = sb("cT", [P, TG * P])
        fs = sb("fs", [P, TG, 2 * P])

        R = G
        NL = 6
        loaded = k.sig("dma_landed", NL)
        setup = k.sig("setup_step", 3)
        ready = k.sig("x_ready", 1, R)
        q_ps, k_ps, v_ps = (k.sig(f"{n}_made", 1, R) for n in "qkv")
        q_in, k_in, v_in = (k.sig(f"{n}_in_sbuf", 1, R) for n in "qkv")
        s_ps = k.sig("scores_made", 1, R)
        s_in = k.sig("scores_masked", 1, R)
        CH = 13
        chain = k.sig("dve_step", CH, R)
        marked = k.sig("max_found", 1, R)
        ex = k.sig("exp_done", 1, R)
        inverted = k.sig("sums_inverted", 1, R)
        scaled = k.sig("probs_scaled", TG, R)
        t_ps = k.sig("probs_turned", 1, R)
        t_in = k.sig("probsT_in_sbuf", 1, R)
        c_ps = k.sig("c_made", 1, R)
        c_in = k.sig("c_in_sbuf", 1, R)
        f_ps = k.sig("film_made", 1, R)
        f_in = k.sig("film_read", 1, R)
        mod = k.sig("pool_step", 3, R)
        with nc.Block() as block:
            @block.sync
            def _(sp):
                for to, of in ((w[:, :, :], ww["sa_w"]), (wf[:, :], ww["film_in"]),
                               (brow[:, :], ww["b_film_in"].partition_broadcast(P)),
                               (mg[:, :], ww["mod_gate"].partition_broadcast(P)),
                               (vm[:, :], k.d["vision_mask"].partition_broadcast(P)),
                               (tm8[:, :], k.d["text_mask"]), ):
                    sp.dma_start(to, of).then_inc(loaded.sem, 16)

            def each(eng):
                with eng.Fori(0, G - 1) as g:
                    yield g, True
                yield G - 1, False

            @block.gpsimd
            def _(pool):
                def copy(g):
                    pool.tensor_copy(xT[:, :], k.nxT_all[:, ds(g * (TG * P), TG * P)])
                    pool.tensor_copy(kv[0:CK, :], k.ctxT[:, ds(g * (TG * NK), TG * NK)]).then_inc(ready.sem, 1)

                link = Chain(pool, mod)

                def modulate(g):
                    pool.wait_ge(f_in.sem, f_in.upto(1, g))
                    link(pool.tensor_tensor(fs[:, :, :], fs[:, :, :], bc(film[:, :].unsqueeze(1), [P, TG, 2 * P]),
                                            ALU.add), g)
                    xw = wide[:, ds(g * TG, TG), :]
                    for n, (part, op) in enumerate(((fs[:, :, 0:P], ALU.mult), (fs[:, :, P:2 * P], ALU.add))):
                        pool.tensor_tensor(carry[:, n:n + 1], k.cols[:, 0:1], k.cols[:, 0:1], ALU.mult)
                        link(pool.tensor_tensor(xw, xw, part, op), g)
                    link.end_round()

                pool.wait_ge(setup.sem, setup.upto(3))
                copy(0)
                pool.wait_ge(v_ps.sem, v_ps.upto(1))
                copy(1)
                with pool.Fori(0, G - 2) as g:
                    modulate(g)
                    pool.wait_ge(v_ps.sem, v_ps.upto(2, g))
                    copy(g + 2)
                modulate(G - 2)
                modulate(G - 1)

            @block.tensor
            def _(pe):
                def scores(g, first=False):
                    pe.wait_ge(ready.sem, ready.upto(1, g))
                    if not first:
                        pe.wait_ge(f_in.sem, f_in.upto(0, g - 1))
                    pe.matmul(k.ps[:, 4, :], w[:, 0, :], xT[:, :], start=True, stop=True).then_inc(q_ps.sem, 1)
                    pe.matmul(k.ps[:, 5, 0:TG * NK], w[0:CK, 1, :], kv[0:CK, :], start=True,
                              stop=True).then_inc(k_ps.sem, 1)
                    pe.wait_ge(q_in.sem, q_in.upto(1, g))
                    pe.wait_ge(k_in.sem, k_in.upto(1, g))
                    pe.wait_ge(s_in.sem, s_in.upto(0, g))
                    for t in range(TG):
                        for h in range(H):
                            rows = slice(DH * h, DH * (h + 1))
                            mm = pe.matmul(k.ps[:, h, t * NK:(t + 1) * NK], q_sb[rows, t * P:(t + 1) * P],
                                           k_sb[rows, t * NK:(t + 1) * NK], start=True, stop=True)
                    mm.then_inc(s_ps.sem, 1)

                def project_v(g):
                    for t in range(TG):
                        mm = pe.matmul(k.ps[0:NK, 6, t * P:(t + 1) * P], kv[0:CK, t * NK:(t + 1) * NK], w[0:CK, 2, :],
                                       start=True, stop=True)
                    mm.then_inc(v_ps.sem, 1)

                pe.wait_ge(loaded.sem, loaded.upto(NL))
                scores(0, True)
                project_v(0)
                for g, after in each(pe):
                    if after:
                        scores(g + 1)
                    pe.wait_ge(v_in.sem, v_in.upto(1, g))
                    for t in range(TG):
                        pe.wait_ge(scaled.sem, scaled.upto(t + 1, g))
                        for h in range(H):
                            mm = pe.matmul(k.ps[0:NK, 6, t * P:(t + 1) * P], wk[:, h * TG + t, :], k.ident[:, :],
                                           start=h == 0, stop=h == H - 1)
                    mm.then_inc(t_ps.sem, 1)
                    pe.wait_ge(t_in.sem, t_in.upto(1, g))
                    pe.wait_ge(c_in.sem, c_in.upto(0, g))
                    for t in range(TG):
                        mm = pe.matmul(k.ps[:, 7, t * P:(t + 1) * P], v_sb[0:NK, t, :], aT[0:NK, t * P:(t + 1) * P],
                                       start=True, stop=True)
                    mm.then_inc(c_ps.sem, 1)
                    if after:
                        project_v(g + 1)
                    pe.wait_ge(c_in.sem, c_in.upto(1, g))
                    for t in range(TG):
                        mm = pe.matmul(k.ps[:, 4 + t // 2, (t % 2) * 2 * P:(t % 2 + 1) * 2 * P],
                                       cT[:, t * P:(t + 1) * P], wf[:, :], start=True, stop=True)
                    mm.then_inc(f_ps.sem, 1)

            @block.scalar
            def _(act):
                def take_qk(g, first=False):
                    act.wait_ge(q_ps.sem, q_ps.upto(1, g))
                    if not first:
                        act.wait_ge(s_ps.sem, s_ps.upto(0, g))
                    act.mul(q_sb[:, :], k.ps[:, 4, :], float(DH) ** -0.5).then_inc(q_in.sem, 1)
                    act.wait_ge(k_ps.sem, k_ps.upto(1, g))
                    act.copy(k_sb[:, :], k.ps[:, 5, 0:TG * NK]).then_inc(k_in.sem, 1)

                def take_v(g):
                    act.wait_ge(v_ps.sem, v_ps.upto(1, g))
                    act.copy(v_sb[0:NK, :, :].rearrange("p t c -> p (t c)"), k.ps[0:NK, 6, :]).then_inc(v_in.sem, 1)

                act.wait_ge(loaded.sem, loaded.upto(NL))
                take_qk(0, True)
                take_v(0)
                for g, after in each(act):
                    if after:
                        take_qk(g + 1)
                    act.wait_ge(marked.sem, marked.upto(1, g))
                    for i in range(W):
                        last = act.activation(sm[:, i, :], sm[:, i, :], ACT.Exp, bias=negmax[:, i:i + 1])
                    last.then_inc(ex.sem, 1)
                    act.wait_ge(inverted.sem, inverted.upto(1, g))
                    for t in range(TG):
                        for h in range(H):
                            i = h * TG + t
                            last = act.mul(wk[:, i, :], wk[:, i, :], rec[:, i:i + 1])
                        last.then_inc(scaled.sem, 1)
                    act.wait_ge(t_ps.sem, t_ps.upto(1, g))
                    act.copy(aT[0:NK, :], k.ps[0:NK, 6, :]).then_inc(t_in.sem, 1)
                    act.wait_ge(c_ps.sem, c_ps.upto(1, g))
                    act.copy(cT[:, :], k.ps[:, 7, :])
                    act.copy(k.nxT_all[:, ds(g * (TG * P), TG * P)], k.ps[:, 7, :]).then_inc(c_in.sem, 1)
                    if after:
                        take_v(g + 1)
                    act.wait_ge(f_ps.sem, f_ps.upto(1, g))
                    act.wait_ge(mod.sem, mod.upto(0, g))
                    for a in range(2):
                        last = act.mul(fs[:, 2 * a:2 * a + 2, :].rearrange("p t c -> p (t c)"), k.ps[:, 4 + a, :], mg[:, :])
                    last.then_inc(f_in.sem, 1)

            @block.vector
            def _(dve):
                dve.wait_ge(loaded.sem, loaded.upto(NL))
                first = Chain(dve, setup)
                first(dve.tensor_copy(tm[:, :], tm8[:, :]))
                film_rows(k, dve, first, mg[:, :], brow, film)
                link = Chain(dve, chain)
                for g, after in each(dve):
                    link(dve.tensor_scalar(mb[:, :], vm[:, ds(g * (TG * NK), TG * NK)], 1.0, -NEG, ALU.subtract,
                                           ALU.mult), g)
                    dve.wait_ge(s_ps.sem, s_ps.upto(1, g))
                    for h in range(H):
                        last = dve.tensor_tensor(sm[:, TG * h:TG * (h + 1), :].rearrange("p t n -> p (t n)"),
                                                 k.ps[:, h, 0:TG * NK], mb[:, :], ALU.add)
                    last.then_inc(s_in.sem, 1)
                    dve.wait_ge(s_in.sem, s_in.upto(1, g))
                    for n in range(TOP // 8):
                        top = m8 if n else m0
                        dve.memset(pad[:, :], 0.0)
                        src = wk if n else sm
                        for i in range(W):
                            last = dve.max(top[:, i, :], src[:, i, :])
                        link(last, g)
                        if n == 0:
                            link(dve.tensor_scalar(negmax[:, :], m0[:, :, 0], -1.0, None, ALU.mult), g)
                            dve.wait_ge(t_ps.sem, t_ps.upto(0, g))
                        dve.memset(pad[:, :], 0.0)
                        for i in range(W):
                            last = dve.match_replace(wk[:, i, :], top[:, i, :], src[:, i, :], TAKEN)
                        if n == 0:
                            last.then_inc(marked.sem, 1)
                            dve.wait_ge(marked.sem, marked.upto(1, g))
                        else:
                            link(last, g)
                    dve.wait_ge(ex.sem, ex.upto(1, g))
                    link(dve.scalar_tensor_tensor(wk[:, :, :], wk[:, :, :], TAKEN, sm[:, :, :], ALU.is_equal,
                                                  ALU.mult), g)
                    dve.wait_ge(scaled.sem, scaled.upto(0, g))
                    link(dve.tensor_reduce(rec[:, :], wk[:, :, :], X, ALU.add), g)
                    link(dve.reciprocal(rec[:, :], rec[:, :]), g)
                    r2 = rec[:, :].rearrange("p (h t) -> p h t", h=H)
                    link(dve.tensor_tensor(r2, r2, bc(tm[:, ds(g * TG, TG)].unsqueeze(1), [P, H, TG]), ALU.mult), g)
                    dve.tensor_scalar(rec[:, :], rec[:, :], 1.0 / H, None, ALU.mult).then_inc(inverted.sem, 1)
                    link.end_round()


def reverse_tokens(k, wide):
    nc = k.nc
    with ExitStack() as ctx:
        rev = k.sb("rv", [P, P], ctx=ctx)
        loaded = k.sig("dma_landed", 1)
        turned = k.sig("turned", 1, G)
        copied = k.sig("copied", 1, G)
        with nc.Block() as block:
            @block.sync
            def _(sp):
                sp.dma_start(rev[:, :], k.d["reversed"]).then_inc(loaded.sem, 16)

            @block.tensor
            def _(pe):
                pe.wait_ge(loaded.sem, loaded.upto(1))
                for r, u, g in rounds(pe):
                    if u == 0:
                        pe.wait_ge(copied.sem, copied.upto(0, r))
                    pe.matmul(k.ps[:, u, :], rev[:, :], wide[:, ds(g * TG, TG), :].rearrange("p t c -> p (t c)"),
                              start=True, stop=True).then_inc(turned.sem, 1)

            @block.scalar
            def _(act):
                for r, u, g in rounds(act):
                    act.wait_ge(turned.sem, turned.upto(1, r))
                    act.copy(wide[:, ds(g * TG, TG), :].rearrange("p t c -> p (t c)"), k.ps[:, u, :]
                             ).then_inc(copied.sem, 1)


def convolve(k, wide, conv_tensor):
    nc = k.nc
    CC = 16
    NC = P // CC
    with ExitStack() as ctx:
        hk = k.sb("cv_h", [P, 2, CC, P], ctx=ctx)
        loaded = [k.sig(f"taps_landed_{i}", 1, NC // 2) for i in range(2)]
        made = k.sig("turned", 1, NC)
        taken_a = k.sig("outs_taken_act", 1, NC)
        taken_d = k.sig("outs_taken_dve", 1, NC)
        with nc.Block() as block:
            @block.sync
            def _(sp):
                for c in range(NC):
                    if c >= 2:
                        sp.wait_ge(made.sem, made.upto(1, c - 2))
                    src = bass.AP(conv_tensor, c * CC * 2 * P, [[1, P], [2 * P, CC], [1, P]])
                    sp.dma_start(hk[:, c % 2], src).then_inc(loaded[c % 2].sem, 16)

            @block.tensor
            def _(pe):
                for c in range(NC):
                    pe.wait_ge(loaded[c % 2].sem, loaded[c % 2].upto(c // 2 + 1))
                    if c >= 2:
                        pe.wait_ge(taken_a.sem, taken_a.upto(1, c - 2))
                        pe.wait_ge(taken_d.sem, taken_d.upto(1, c - 2))
                    for i in range(CC):
                        mm = pe.matmul(k.ps[:, 2 * (c % 2) + i // 8, (i % 8) * B:(i % 8 + 1) * B], hk[:, c % 2, i, :],
                                       wide[:, :, c * CC + i], start=True, stop=True)
                    mm.then_inc(made.sem, 1)

            @block.scalar
            def _(act):
                for c in range(NC):
                    act.wait_ge(made.sem, made.upto(1, c))
                    act.copy(wide[:, :, c * CC:c * CC + 8].rearrange("p b d -> p d b"),
                             k.ps[:, 2 * (c % 2), :].rearrange("p (d b) -> p d b", b=B)).then_inc(taken_a.sem, 1)

            @block.vector
            def _(dve):
                for c in range(NC):
                    dve.wait_ge(made.sem, made.upto(1, c))
                    dve.tensor_copy(wide[:, :, c * CC + 8:c * CC + 16].rearrange("p b d -> p d b"),
                                    k.ps[:, 2 * (c % 2) + 1, :].rearrange("p (d b) -> p d b", b=B)
                                    ).then_inc(taken_d.sem, 1)


def modulate_out(k, ww, wide):
    nc = k.nc
    S = 4
    with ExitStack() as ctx:
        wf = k.sb("mo_wf", [P, 2 * P], ctx=ctx)
        brow = k.sb("mo_brow", [P, 2 * P], ctx=ctx)
        film = k.sb("mo_film", [P, 2 * P], ctx=ctx)
        mg = k.sb("mo_mg", [P, 1], ctx=ctx)
        cT = k.sb("mo_cT", [P, S, TG * P], ctx=ctx)
        fs = k.sb("mo_fs", [P, S, TG, 2 * P], ctx=ctx)
        carry = k.sb("mo_carry", [P, S], ctx=ctx)
        loaded = k.sig("dma_landed", 3)
        setup = k.sig("setup_step", 2)
        ready = k.sig("x_ready", 1, G)
        f_ps = k.sig("film_made", 1, G)
        f_in = k.sig("film_read", 1, G)
        scaled = k.sig("outputs_scaled", 1, G)
        shifted = k.sig("shifted", 1, G)
        summed = k.sig("staged", 1, G)
        with nc.Block() as block:
            @block.sync
            def _(sp):
                for to, of in ((wf[:, :], ww["film_out"]), (brow[:, :], ww["b_film_out"].partition_broadcast(P)),
                               (mg[:, :], ww["mod_gate"].partition_broadcast(P))):
                    sp.dma_start(to, of).then_inc(loaded.sem, 16)

            @block.scalar
            def _(act):
                for r, u, g in rounds(act, slots=S):
                    if u == 0:
                        act.wait_ge(f_ps.sem, f_ps.upto(0, r))
                    act.copy(cT[:, u], k.nxT_all[:, ds(g * (TG * P), TG * P)]).then_inc(ready.sem, 1)

            @block.tensor
            def _(pe):
                pe.wait_ge(loaded.sem, loaded.upto(3))
                for r, u, g in rounds(pe, slots=S):
                    pe.wait_ge(ready.sem, ready.upto(1, r))
                    if u == 0:
                        pe.wait_ge(f_in.sem, f_in.upto(0, r))
                    for t in range(TG):
                        mm = pe.matmul(k.ps[:, 2 * u + t // 2, (t % 2) * 2 * P:(t % 2 + 1) * 2 * P],
                                       cT[:, u, t * P:(t + 1) * P], wf[:, :], start=True, stop=True)
                    mm.then_inc(f_ps.sem, 1)

            @block.vector
            def _(dve):
                dve.wait_ge(loaded.sem, loaded.upto(3))
                first = Chain(dve, setup)
                film_rows(k, dve, first, mg[:, :], brow, film)
                for r, u, g in rounds(dve, slots=S):
                    if u == 0:
                        dve.wait_ge(summed.sem, summed.upto(0, r))
                    dve.wait_ge(f_ps.sem, f_ps.upto(1, r))
                    for a in range(2):
                        last = dve.scalar_tensor_tensor(fs[:, u, 2 * a:2 * a + 2, :],
                                                        k.ps[:, 2 * u + a, :].rearrange("p (t c) -> p t c", t=2),
                                                        mg[:, :], bc(film[:, :].unsqueeze(1), [P, 2, 2 * P]),
                                                        ALU.mult, ALU.add)
                    last.then_inc(f_in.sem, 1)
                    dve.wait_ge(f_in.sem, f_in.upto(1, r))
                    xw = wide[:, ds(g * TG, TG), :]
                    dve.tensor_tensor(xw, xw, fs[:, u, :, 0:P], ALU.mult).then_inc(scaled.sem, 1)

            @block.gpsimd
            def _(pool):
                for r, u, g in rounds(pool, slots=S):
                    xw = wide[:, ds(g * TG, TG), :]
                    pool.wait_ge(scaled.sem, scaled.upto(1, r))
                    pool.tensor_tensor(xw, xw, fs[:, u, :, P:2 * P], ALU.add).then_inc(shifted.sem, 1)
                    pool.wait_ge(shifted.sem, shifted.upto(1, r))
                    pool.tensor_tensor(carry[:, u:u + 1], k.cols[:, 0:1], k.cols[:, 0:1], ALU.mult)
                    pool.tensor_tensor(xw, xw, k.nx_all[:, ds(g * TG, TG), :], ALU.add).then_inc(summed.sem, 1)


def norm_rows(k, src, dst, scale_dram, shift_dram, gate_col=None):
    nc = k.nc
    S = 4
    with ExitStack() as ctx:
        stats = k.sb("nr_stats", [P, B, 6], ctx=ctx)
        mean, var, rstd = (k.sb(f"nr_{n}", [P, B], ctx=ctx) for n in ("mean", "var", "rstd"))
        mid = k.sb("nr_mid", [P, S, TG, P], ctx=ctx)
        gr = k.sb("nr_g", [P, P], ctx=ctx)
        br = k.sb("nr_b", [P, P], ctx=ctx)
        carry = k.sb("nr_carry", [P, S], ctx=ctx)
        loaded = k.sig("dma_landed", 2)
        counted = k.sig("counted", 1)
        chain = k.sig("dve_step", 7)
        rooted = k.sig("rooted", 1)
        centred = k.sig("centred", 1, G)
        scaled = k.sig("outputs_scaled", 2, G)
        shifted = k.sig("shifted", 1, G)
        summed = k.sig("staged", 1, G) if gate_col is not None else None
        with nc.Block() as block:
            @block.sync
            def _(sp):
                sp.dma_start(gr[:, :], scale_dram.partition_broadcast(P)).then_inc(loaded.sem, 16)
                sp.dma_start(br[:, :], shift_dram.partition_broadcast(P)).then_inc(loaded.sem, 16)

            @block.vector
            def _(dve):
                link = Chain(dve, chain)
                for sample in range(B):
                    last = dve.bn_stats(stats[:, sample, :], src[:, sample, :])
                last.then_inc(counted.sem, 1)
                dve.wait_ge(counted.sem, counted.upto(1))
                link(dve.tensor_tensor(var[:, :], stats[:, :, 1], stats[:, :, 4], ALU.subtract))
                link(dve.scalar_tensor_tensor(var[:, :], var[:, :], P / 4.0, var[:, :], ALU.mult, ALU.mult))
                link(dve.tensor_tensor(var[:, :], var[:, :], stats[:, :, 2], ALU.add))
                link(dve.tensor_tensor(mean[:, :], stats[:, :, 1], stats[:, :, 4], ALU.add))
                link(dve.tensor_scalar(mean[:, :], mean[:, :], -0.5, None, ALU.mult))
                link(dve.tensor_tensor(var[:, :], var[:, :], stats[:, :, 5], ALU.add))
                dve.wait_ge(rooted.sem, rooted.upto(1))
                link(dve.reciprocal(rstd[:, :], rstd[:, :]))
                dve.wait_ge(loaded.sem, loaded.upto(2))
                for r, u, g in rounds(dve, slots=S):
                    dve.wait_ge(centred.sem, centred.upto(1, r))
                    by = bc(rstd[:, ds(g * TG, TG)].unsqueeze(2), [P, TG, P])
                    dve.tensor_tensor(mid[:, u], mid[:, u], by, ALU.mult).then_inc(scaled.sem, 1)
                    dve.wait_ge(scaled.sem, scaled.upto(1, r))
                    dve.tensor_tensor(mid[:, u], mid[:, u], bc(gr[:, :].unsqueeze(1), [P, TG, P]),
                                      ALU.mult).then_inc(scaled.sem, 1)
                    for r, u, g in [(r + v, 3 + v, g + v) for v in range(-3, 1)] if gate_col is not None and u == 3 else ():
                        dve.wait_ge(shifted.sem, shifted.upto(1, r))
                        x = dst[:, ds(g * TG, TG), :]
                        dve.scalar_tensor_tensor(x, mid[:, u], gate_col, x, ALU.mult, ALU.add).then_inc(summed.sem, 1)

            @block.scalar
            def _(act):
                act.wait_ge(chain.sem, chain.upto(6))
                act.activation(rstd[:, :], var[:, :], ACT.Sqrt, bias=k.cols[:, 0:1],
                               scale=1.0 / P).then_inc(rooted.sem, 1)
                for r, u, g in rounds(act, slots=S):
                    if u == 0:
                        free = summed if summed else shifted
                        act.wait_ge(free.sem, free.upto(0, r))
                    for t in range(TG):
                        last = act.activation(mid[:, u, t, :],
                                              src[:, ds(g * TG + t, 1), :].rearrange("p a c -> p (a c)"), ACT.Identity,
                                              bias=mean[:, ds(g * TG + t, 1)])
                    last.then_inc(centred.sem, 1)

            @block.gpsimd
            def _(pool):
                pool.wait_ge(loaded.sem, loaded.upto(2))
                for r, u, g in rounds(pool, slots=S):
                    pool.wait_ge(scaled.sem, scaled.upto(2, r))
                    out = mid[:, u] if gate_col is not None else dst[:, ds(g * TG, TG), :]
                    pool.tensor_tensor(carry[:, u:u + 1], k.cols[:, 0:1], k.cols[:, 0:1], ALU.mult)
                    pool.tensor_tensor(out, mid[:, u], bc(br[:, :].unsqueeze(1), [P, TG, P]),
                                       ALU.add).then_inc(shifted.sem, 1)


def load_context(k):
    loaded = k.sig("dma_landed", 1)
    with k.nc.Block() as block:
        @block.sync
        def _(sp):
            sp.dma_start(k.ctxT[:, :], k.d["ctxT"]).then_inc(loaded.sem, 16)
            sp.wait_ge(loaded.sem, loaded.upto(1))


def store_output(k, out):
    stored = k.sig("dma_stored", 4)
    with k.nc.Block() as block:
        @block.sync
        def _(sp):
            for q in range(4):
                s = slice(16 * q, 16 * q + 16)
                sp.dma_start(out[s].rearrange("b s c -> s b c"), k.x_all[:, s, :]).then_inc(stored.sem, 16)
            sp.wait_ge(stored.sem, stored.upto(4))


def build(nc, d, out, stages=range(1, 9)):
    conv = nc.dram_tensor("conv_rows", [P, 2 * P], F32, kind="Internal")
    with ExitStack() as ctx:
        k = Kernel(nc, d, ctx)
        k.rank_i = k.sb("rank_i", [P, 8], I32)
        tgc = [k.tg[:, i:i + 1] for i in range(8)]

        def att(name):
            return {"w": d[name + "_w"], "bcol": d[name + "_bcol"], "rows": d[name + "_rows"]}

        def exp_w(name, up):
            r = {"w1": d[name + "_w1"], "w2": d[name + "_w2"], "bcol": d[name + "_bcol"], "brow": d[name + "_brow"]}
            if up:
                r["w3"] = d[name + "_w3"]
            return r

        prime_signals(k)
        load_inputs(k)
        if 3 in stages:
            ssm_kernel(k, d, conv.ap())
        k.ctxT = k.sb("ctxT", [CK, B * NK])
        load_context(k)

        if 1 in stages:
            normalise_and_turn(k)
            narrow_attention(k, 1, NK, 8 ** -0.5, att("a0"), tgc[0], clip=10000.0)
        if 2 in stages:
            with ExitStack() as inner:
                gate_arrays(k, inner)
                with ExitStack() as inmost:
                    h_all = k.sb("h_all", [P, B, 64], ctx=inmost)
                    normalise_and_turn(k, router=(d["m0_rw1"], d["m0_rb1"], 64, h_all))
                    layer_norm(k, h_all, h_all, 64)
                    router_logits(k, h_all, 64, {n: d["m0_r_" + n] for n in ("w2", "b2", "g", "b")})
                top_two_gates(k, tgc[4])
                add_gated_rows(k, d["m0_rows_diag"])
                narrow_attention(k, 8, P, 8 ** -0.5, att("m0"), None, gated=True)
        if 3 in stages:
            normalise_and_turn(k, keep=True)
            with ExitStack() as inner:
                wide = k.sb("wide", [P, B, P], ctx=inner)
                norm_rows(k, k.nx_all, wide, d["g_norm_in"], d["b_norm_in"])
                sparse_attention(k, d, wide)
                reverse_tokens(k, wide)
                convolve(k, wide, conv)
                modulate_out(k, d, wide)
                norm_rows(k, wide, k.nx_all, d["g_ffn_ln"], d["b_ffn_ln"])
                transpose_rows(k)
                experts(k, 1, 4, ACT.Gelu, exp_w("mlp", False), wide, up=False, gate_col=k.cols[:, 1:2], gated=False)
                norm_rows(k, wide, k.x_all, d["g_norm_out"], d["b_norm_out"], gate_col=tgc[1])
        if 4 in stages:
            with ExitStack() as inner:
                gate_arrays(k, inner)
                normalise_and_turn(k, router=(d["m1_rw"], d["m1_rb"], 8, k.logits))
                top_two_gates(k, tgc[5], shared=2)
                experts(k, 5, 1, ACT.Silu, exp_w("m1", True), k.x_all, up=True, pair=True)
        if 5 in stages:
            normalise_and_turn(k)
            wide_attention(k, 64 ** -0.5, att("a2"), tgc[2])
        if 6 in stages:
            with ExitStack() as inner:
                gate_arrays(k, inner)
                normalise_and_turn(k, router=(d["m2_rw"], d["zero_row"], 8, k.logits))
                top_two_gates(k, tgc[6], plus=1e-8)
                add_gated_rows(k, d["m2_rows_diag"])
                experts(k, 8, 2, ACT.Silu, exp_w("m2", True), k.x_all, up=True)
        if 7 in stages:
            normalise_and_turn(k)
            wide_attention(k, 64 ** -0.5, att("a3"), tgc[3])
        if 8 in stages:
            with ExitStack() as inner:
                gate_arrays(k, inner)
                normalise_and_turn(k, router=(d["m3_rw"], d["zero_row"], 8, k.logits))
                top_two_gates(k, tgc[7], least=1e-9, capacity=2 * B * P // 8)
                experts(k, 8, 4, ACT.Gelu, exp_w("m3", False), k.x_all, up=False)
        store_output(k, out)


def layouts(i):
    import numpy as np
    a = {n: np.asarray(v) for n, v in i.items()}
    f = np.float32
    d = {}
    d["x"] = a["x"]
    d["ctxT"] = np.transpose(a["ctx_768"], (2, 0, 1)).reshape(CK, B * NK)
    d["ident"] = np.eye(P, dtype=f)
    d["reversed"] = np.eye(P, dtype=f)[::-1]
    d["ones"] = np.ones((P, P), f)
    d["before"] = np.triu(np.ones((P, P), f), 1)
    d["zero_row"] = np.zeros((8,), f)
    cols = np.zeros((P, 32), f)
    cols[:, 0] = EPS
    cols[:, 1] = 1.0
    for h in range(16):
        cols[:, 16 + h] = np.arange(P) // 8 == h
    d["cols"] = cols
    d["g_rows"] = np.concatenate([a["g_xattn"], a["g_ffn"]])
    d["text_mask"] = a["mask_BxS_bf1"].view(np.uint8).T
    d["vision_mask"] = a["mask_BxS2_bf1"].view(np.uint8).reshape(-1)

    def attn(name, wq, wk, wv, wo, bq=None, bk=None, bv=None, bo=None):
        E = wq.shape[0]
        w = np.zeros((E + 1, P, 4, P), f)
        for n, m in enumerate((wq, wk, wv, wo)):
            w[:E, :m.shape[1], n, :] = m
        d[name + "_w"] = w
        bcol = np.zeros((E + 1, P, 2), f)
        rows = np.zeros((E + 1, 2, P), f)
        for to, b in ((bcol[:E, :, 0], bq), (bcol[:E, :, 1], bk), (rows[:E, 0], bv)):
            if b is not None:
                to[:] = b
        if bo is not None:
            rows[:len(bo), 1] = bo
        d[name + "_bcol"], d[name + "_rows"] = bcol, rows

    L = "L0_xattn_"
    attn("a0", *(a[L + n][None] for n in ("Wq", "Wk", "Wv", "Wo", "bq", "bk", "bv", "bo")))
    L = "L0_ffn_"
    attn("m0", *(np.transpose(a[L + n], (0, 2, 1)) for n in ("qW", "kW", "vW", "oW")),
         *(a[L + n] for n in ("qb", "kb", "vb", "ob")))

    def cut(w):
        return np.transpose(w.reshape(w.shape[0], 8, P), (1, 0, 2))

    attn("a2", cut(a["L2_xattn_Wq"]), cut(a["L2_xattn_Wk"]), cut(a["L2_xattn_Wv"]),
         a["L2_xattn_Wo"].reshape(8, P, P), bo=a["L2_xattn_bo"][None])
    kv = a["L3_xattn_w_kv"]
    attn("a3", cut(a["L3_xattn_w_q"]), cut(kv[:, :1024]), cut(kv[:, 1024:]), a["L3_xattn_w_out"].reshape(8, P, P),
         bo=a["L3_xattn_b_out"][None])

    L = "L0_ffn_"
    d["m0_rw1"], d["m0_rb1"] = a[L + "rW1"].T, a[L + "rb1"]
    d["m0_r_w2"], d["m0_r_b2"], d["m0_r_g"], d["m0_r_b"] = a[L + "rW2"].T, a[L + "rb2"], a[L + "ln_g"], a[L + "ln_b"]

    L = "L1_xattn_"
    w = np.zeros((P, 3, P), f)
    for n, m in enumerate(("Wq", "Wk", "Wv")):
        w[:a[L + m].shape[0], n] = a[L + m]
    d["sa_w"] = w
    d["film_in"], d["b_film_in"] = a[L + "W_film_in"], a[L + "b_film_in"]
    d["film_out"], d["b_film_out"] = a[L + "W_film_out"], a[L + "b_film_out"]
    d["mod_gate"] = a[L + "mod_gate"].reshape(1)
    d["g_norm_in"], d["b_norm_in"] = a[L + "g_norm_in"], a[L + "b_norm_in"]
    d["g_ffn_ln"], d["b_ffn_ln"] = a[L + "g_ffn"], a[L + "b_ffn"]
    d["g_norm_out"], d["b_norm_out"] = a[L + "g_norm_out"], a[L + "b_norm_out"]
    d["ssm"] = np.concatenate([a[L + n] for n in ("A_re", "A_im", "C_re", "C_im")]
                              + [a[L + "log_dt"][:, None], a[L + "D_skip"][:, None]], axis=1)

    def diagonal(rows):
        out = np.zeros((16, 8, 16, P), f)
        for s in range(16):
            out[s, :, s] = rows
        return out.reshape(P, 16, P)

    d["m0_rows_diag"] = diagonal(a["L0_ffn_ob"])
    d["m2_rows_diag"] = diagonal(a["L2_ffn_b_out"])

    def moe(name, w1, w2, w3=None, b1=None, b3=None, b2=None):
        E, _, M = w1.shape
        MC = M // P
        d[name + "_w1"] = w1
        d[name + "_w2"] = np.transpose(w2.reshape(E, MC, P, P), (0, 2, 1, 3))
        if w3 is not None:
            d[name + "_w3"] = w3
        bcol = np.zeros((E, P, 2 * MC), f)
        for n, b in enumerate((b1, b3)):
            if b is not None:
                bcol[:, :, n * MC:(n + 1) * MC] = np.transpose(b.reshape(E, MC, P), (0, 2, 1))
        d[name + "_bcol"] = bcol
        d[name + "_brow"] = b2 if b2 is not None else np.zeros((E, P), f)

    moe("mlp", a[L + "W1"][None], a[L + "W2"][None], b1=a[L + "b1"][None], b2=a[L + "b2"][None])
    L = "L1_ffn_"
    w1, w3, w2 = (np.concatenate([a[L + "routed_" + n], a[L + "shared_" + n]]) for n in ("w1", "w3", "w2"))

    def two(w):
        return np.transpose(w.reshape(5, 2, P, 64), (0, 2, 1, 3)).reshape(5, P, P)

    moe("m1", two(w1), w2.reshape(5, P, P), two(w3))
    d["m1_rw"], d["m1_rb"] = a[L + "router_w"], a[L + "router_b"]
    L = "L2_ffn_"
    moe("m2", a[L + "W_gate"], a[L + "W_out"], a[L + "W_up"], a[L + "b_gate"], a[L + "b_up"], a[L + "b_out"])
    d["m2_rw"] = a[L + "W_router"]
    L = "L3_ffn_"
    moe("m3", a[L + "w_gate"], a[L + "w_down"])
    d["m3_rw"] = a[L + "wg"]
    return {n: np.ascontiguousarray(v) for n, v in d.items()}


STAGES = range(1, 9)


def kernel(**inputs):
    import concourse.bacc as bacc
    from concourse.bass_utils import run_bass_kernel_spmd as run

    nc = bacc.Bacc("TRN2", target_bir_lowering=False, num_devices=1)
    arrays, dram = {}, {}
    for name, v in layouts(inputs).items():
        arrays["in_" + name] = v
        dram[name] = nc.dram_tensor("in_" + name, v.shape, mybir.dt.from_np(v.dtype), kind="ExternalInput").ap()
    out = nc.dram_tensor("out_0", (B, P, P), F32, kind="ExternalOutput").ap()
    build(nc, dram, out, STAGES)
    return run(nc, [arrays], core_ids=[0]).results[0]["out_0"]
```
